# Optimizing a Trainium2 kernel written in Bass

```python
import numpy as np
import jax
import jax.numpy as jnp

def _softmax(x, axis=-1):
    return jax.nn.softmax(x, axis=axis)

def _gelu(x):
    return jax.nn.gelu(x, approximate=True)

def _silu(x):
    return jax.nn.silu(x)

def _sigmoid(x):
    return jax.nn.sigmoid(x)

def _layernorm(x, axis=-1, eps=1e-05):
    m = jnp.mean(x, axis=axis, keepdims=True)
    v = jnp.var(x, axis=axis, keepdims=True)
    return (x - m) / jnp.sqrt(v + eps)

def _scatter_add(tgt, idx, src, axis=0):
    return tgt.at[idx].add(src)

def _segment_sum(src, seg, n):
    return jax.ops.segment_sum(src, seg, n)
kernel_name = 'mk_audio_tower_d2_tok_audfeat512_r4_8c4143'

def setup_inputs(seed: int=0):
    np.random.seed(seed)
    _w = jnp.asarray

    def _rec_inputs():
        import jax
        import jax.numpy as jnp
        _rk = jax.random.key(seed)
        x = -0.000125008 + 0.999885 * jax.random.normal(jax.random.fold_in(_rk, 1), (16, 250, 128), jnp.float32)
        return x
    x = _rec_inputs()

    def _L0_tok_setup():
        import jax, jax.numpy as jnp
        import numpy as np
        from jax import lax
        B, L, F, K = (32, 512, 128, 128)
        LOUT = L - K + 1
        key = jax.random.key(seed)
        k1, k2 = jax.random.split(key)
        x = jax.random.normal(k1, (B, L, F), dtype=jnp.float32)
        W = jax.random.normal(k2, (F, F), dtype=jnp.float32) / np.float32(np.sqrt(F))
        b = jnp.zeros((F,), dtype=jnp.float32)
        return {'x': x, 'W': W, 'b': b}
    _L0_tok_all = _L0_tok_setup()
    _L0_tok_in = {k: v for k, v in _L0_tok_all.items() if k in ('W', 'b')}
    del _L0_tok_all

    def _L0_attn_setup():
        import jax, jax.numpy as jnp
        import numpy as np
        B, S, D, H = (8, 1024, 128, 8)
        DK = D // H
        DFF = 2 * D
        KS = 3
        EPS = 1e-06
        LN_EPS = 1e-05

        def _sdwc(x, w, b):
            s = x.shape[1]
            xp = jnp.pad(x, ((0, 0), (KS - 1, 0), (0, 0), (0, 0)))
            y = sum((xp[:, j:j + s] * w[:, j] for j in range(KS)))
            return y + b

        def _ln(x, g, b):
            m = jnp.mean(x, axis=-1, keepdims=True)
            v = jnp.mean((x - m) ** 2, axis=-1, keepdims=True)
            return (x - m) * jax.lax.rsqrt(v + LN_EPS) * g + b
        key = jax.random.key(seed)
        ks = jax.random.split(key, 24)
        w = lambda k, shape, s=0.02: (jax.random.normal(k, shape) * s).astype(jnp.float32)
        return {'x': jax.random.normal(ks[0], (B, S, D), dtype=jnp.float32), 'wq': w(ks[1], (D, D)), 'bq': w(ks[2], (D,)), 'wk': w(ks[3], (D, D)), 'bk': w(ks[4], (D,)), 'wv': w(ks[5], (D, D)), 'bv': w(ks[6], (D,)), 'wo': w(ks[7], (D, D)), 'bo': w(ks[8], (D,)), 'qcw': w(ks[9], (DK, KS)), 'qcb': w(ks[10], (DK,)), 'kcw': w(ks[11], (DK, KS)), 'kcb': w(ks[12], (DK,)), 'vcw': w(ks[13], (DK, KS)), 'vcb': w(ks[14], (DK,)), 'w1': w(ks[15], (DFF, D)), 'b1': w(ks[16], (DFF,)), 'w2': w(ks[17], (D, DFF)), 'b2': w(ks[18], (D,)), 'ln1_g': jnp.ones((D,), jnp.float32), 'ln1_b': jnp.zeros((D,), jnp.float32), 'ln2_g': jnp.ones((D,), jnp.float32), 'ln2_b': jnp.zeros((D,), jnp.float32)}
    _L0_attn_all = _L0_attn_setup()
    _L0_attn_in = {k: v for k, v in _L0_attn_all.items() if k in ('wq', 'bq', 'wk', 'bk', 'wv', 'bv', 'qcw', 'qcb', 'kcw', 'kcb', 'vcw', 'vcb', 'wo', 'bo', 'w1', 'b1', 'w2', 'b2', 'ln1_g', 'ln1_b', 'ln2_g', 'ln2_b')}
    del _L0_attn_all

    def _L0_ffn_setup():
        import jax, jax.numpy as jnp
        import numpy as np
        B, L, H, E, F, C = (8, 2048, 128, 8, 256, 2)
        key = jax.random.key(seed)
        ks = jax.random.split(key, 4)
        x = jax.random.normal(ks[0], (B, L, H), jnp.float32)
        Wg = jax.random.normal(ks[1], (H, E), jnp.float32) * H ** (-0.5)
        W1 = jax.random.normal(ks[2], (E, H, F), jnp.float32) * H ** (-0.5)
        b1 = jnp.zeros((E, F), jnp.float32)
        W2 = jax.random.normal(ks[3], (E, F, H), jnp.float32) * F ** (-0.5)
        b2 = jnp.zeros((E, H), jnp.float32)
        return {'x': x, 'Wg': Wg, 'W1': W1, 'b1': b1, 'W2': W2, 'b2': b2}
    _L0_ffn_all = _L0_ffn_setup()
    _L0_ffn_in = {k: v for k, v in _L0_ffn_all.items() if k in ('Wg', 'W1', 'b1', 'W2', 'b2')}
    del _L0_ffn_all

    def _L1_attn_setup():
        import jax, jax.numpy as jnp
        import numpy as np
        B, N, DIM = (2, 1024, 128)
        HEADS, HEAD_DIM = (8, 64)
        INNER = HEADS * HEAD_DIM
        key = jax.random.key(seed)
        k1, k2, k3 = jax.random.split(key, 3)
        x = jax.random.normal(k1, (B, N, DIM), dtype=jnp.float32)
        w_qkv = jax.random.normal(k2, (DIM, 3 * INNER), dtype=jnp.float32) * DIM ** (-0.5)
        temperature = jnp.asarray(np.log(HEAD_DIM ** (-0.5)), dtype=jnp.float32)
        w_out = jax.random.normal(k3, (INNER, DIM), dtype=jnp.float32) * INNER ** (-0.5)
        b_out = jnp.zeros((DIM,), dtype=jnp.float32)
        return {'x': x, 'w_qkv': w_qkv, 'temperature': temperature, 'w_out': w_out, 'b_out': b_out}
    _L1_attn_all = _L1_attn_setup()
    _L1_attn_in = {k: v for k, v in _L1_attn_all.items() if k in ('w_qkv', 'temperature', 'w_out', 'b_out')}
    del _L1_attn_all

    def _L1_ffn_setup():
        import jax, jax.numpy as jnp
        import numpy as np
        B, S, D = (8, 1024, 128)
        H = 512
        O = 128
        E = 8
        TOP_K = 1
        key = jax.random.key(seed)
        ks = jax.random.split(key, 8)
        sc = 0.02
        return {'x': jax.random.normal(ks[0], (B, S, D), dtype=jnp.float32), 'Wr': jax.random.normal(ks[1], (D, E), dtype=jnp.float32) * sc, 'br': jnp.zeros((E,), dtype=jnp.float32), 'W1': jax.random.normal(ks[2], (E, D, H), dtype=jnp.float32) * sc, 'b1': jnp.zeros((E, H), dtype=jnp.float32), 'W2': jax.random.normal(ks[3], (E, H, O), dtype=jnp.float32) * sc, 'b2': jnp.zeros((E, O), dtype=jnp.float32)}
    _L1_ffn_all = _L1_ffn_setup()
    _L1_ffn_in = {k: v for k, v in _L1_ffn_all.items() if k in ('Wr', 'br', 'W1', 'b1', 'W2', 'b2')}
    del _L1_ffn_all
    return {'x': x, 'L0_tok_W': _L0_tok_in['W'], 'L0_tok_b': _L0_tok_in['b'], 'L0_attn_wq': _L0_attn_in['wq'], 'L0_attn_bq': _L0_attn_in['bq'], 'L0_attn_wk': _L0_attn_in['wk'], 'L0_attn_bk': _L0_attn_in['bk'], 'L0_attn_wv': _L0_attn_in['wv'], 'L0_attn_bv': _L0_attn_in['bv'], 'L0_attn_qcw': _L0_attn_in['qcw'], 'L0_attn_qcb': _L0_attn_in['qcb'], 'L0_attn_kcw': _L0_attn_in['kcw'], 'L0_attn_kcb': _L0_attn_in['kcb'], 'L0_attn_vcw': _L0_attn_in['vcw'], 'L0_attn_vcb': _L0_attn_in['vcb'], 'L0_attn_wo': _L0_attn_in['wo'], 'L0_attn_bo': _L0_attn_in['bo'], 'L0_attn_w1': _L0_attn_in['w1'], 'L0_attn_b1': _L0_attn_in['b1'], 'L0_attn_w2': _L0_attn_in['w2'], 'L0_attn_b2': _L0_attn_in['b2'], 'L0_attn_ln1_g': _L0_attn_in['ln1_g'], 'L0_attn_ln1_b': _L0_attn_in['ln1_b'], 'L0_attn_ln2_g': _L0_attn_in['ln2_g'], 'L0_attn_ln2_b': _L0_attn_in['ln2_b'], 'L0_ffn_Wg': _L0_ffn_in['Wg'], 'L0_ffn_W1': _L0_ffn_in['W1'], 'L0_ffn_b1': _L0_ffn_in['b1'], 'L0_ffn_W2': _L0_ffn_in['W2'], 'L0_ffn_b2': _L0_ffn_in['b2'], 'L1_attn_w_qkv': _L1_attn_in['w_qkv'], 'L1_attn_temperature': _L1_attn_in['temperature'], 'L1_attn_w_out': _L1_attn_in['w_out'], 'L1_attn_b_out': _L1_attn_in['b_out'], 'L1_ffn_Wr': _L1_ffn_in['Wr'], 'L1_ffn_br': _L1_ffn_in['br'], 'L1_ffn_W1': _L1_ffn_in['W1'], 'L1_ffn_b1': _L1_ffn_in['b1'], 'L1_ffn_W2': _L1_ffn_in['W2'], 'L1_ffn_b2': _L1_ffn_in['b2']}

def reference(x, L0_tok_W, L0_tok_b, L0_attn_wq, L0_attn_bq, L0_attn_wk, L0_attn_bk, L0_attn_wv, L0_attn_bv, L0_attn_qcw, L0_attn_qcb, L0_attn_kcw, L0_attn_kcb, L0_attn_vcw, L0_attn_vcb, L0_attn_wo, L0_attn_bo, L0_attn_w1, L0_attn_b1, L0_attn_w2, L0_attn_b2, L0_attn_ln1_g, L0_attn_ln1_b, L0_attn_ln2_g, L0_attn_ln2_b, L0_ffn_Wg, L0_ffn_W1, L0_ffn_b1, L0_ffn_W2, L0_ffn_b2, L1_attn_w_qkv, L1_attn_temperature, L1_attn_w_out, L1_attn_b_out, L1_ffn_Wr, L1_ffn_br, L1_ffn_W1, L1_ffn_b1, L1_ffn_W2, L1_ffn_b2):
    import jax
    import jax.numpy as jnp

    def _L0_tok_ref(x, W, b):
        import jax, jax.numpy as jnp
        import numpy as np
        from jax import lax
        B, L, F, K = (32, 512, 128, 128)
        LOUT = L - K + 1
        feat = lax.stop_gradient(x)[:, -1, :]
        tau = jax.nn.sigmoid((feat @ W.T + b) / 10.0 + -3.0)
        exps = jnp.arange(K, dtype=x.dtype)
        powers = tau[:, None, :] ** exps[None, :, None]
        den = powers.sum(axis=1)
        norm = lax.stop_gradient(1.0 / den)
        w = norm[:, None, :] * powers[:, ::-1, :]

        def conv_one(xb, wb):
            return lax.conv_general_dilated(xb[None], wb[:, None, :], (1,), 'VALID', dimension_numbers=('NWC', 'WIO', 'NWC'), feature_group_count=F)[0]
        return jax.vmap(conv_one)(x, w)

    def _L0_attn_ref(x, wq, bq, wk, bk, wv, bv, qcw, qcb, kcw, kcb, vcw, vcb, wo, bo, w1, b1, w2, b2, ln1_g, ln1_b, ln2_g, ln2_b):
        import jax, jax.numpy as jnp
        import numpy as np
        B, S, D, H = (8, 1024, 128, 8)
        DK = D // H
        DFF = 2 * D
        KS = 3
        EPS = 1e-06
        LN_EPS = 1e-05

        def _sdwc(x, w, b):
            s = x.shape[1]
            xp = jnp.pad(x, ((0, 0), (KS - 1, 0), (0, 0), (0, 0)))
            y = sum((xp[:, j:j + s] * w[:, j] for j in range(KS)))
            return y + b

        def _ln(x, g, b):
            m = jnp.mean(x, axis=-1, keepdims=True)
            v = jnp.mean((x - m) ** 2, axis=-1, keepdims=True)
            return (x - m) * jax.lax.rsqrt(v + LN_EPS) * g + b
        b_, s_, _ = x.shape
        q = (jnp.einsum('bsd,od->bso', x, wq) + bq).reshape(b_, s_, H, DK)
        k = (jnp.einsum('bsd,od->bso', x, wk) + bk).reshape(b_, s_, H, DK)
        v = (jnp.einsum('bsd,od->bso', x, wv) + bv).reshape(b_, s_, H, DK)
        q = jax.nn.elu(_sdwc(q, qcw, qcb)) + 1.0
        k = jax.nn.elu(_sdwc(k, kcw, kcb)) + 1.0
        v = _sdwc(v, vcw, vcb)
        Q = q.transpose(0, 2, 1, 3)
        K = k.transpose(0, 2, 1, 3)
        V = v.transpose(0, 2, 1, 3)
        KV = jnp.einsum('bhsd,bhse->bhde', K, V)
        Z = 1.0 / jnp.einsum('bhsd,bhd->bhs', Q, K.sum(axis=2) + EPS)
        Vn = jnp.einsum('bhde,bhsd,bhs->bhse', KV, Q, Z)
        attn = Vn.transpose(0, 2, 1, 3).reshape(b_, s_, D)
        attn = jnp.einsum('bsd,od->bso', attn, wo) + bo
        x = _ln(x + attn, ln1_g, ln1_b)
        h = jnp.einsum('bsd,cd->bsc', x, w1) + b1
        g = jax.nn.gelu(h, approximate=False)
        h = g * g
        h = jnp.einsum('bsc,dc->bsd', h, w2) + b2
        return _ln(x + h, ln2_g, ln2_b)

    def _L0_ffn_ref(x, Wg, W1, b1, W2, b2):
        import jax, jax.numpy as jnp
        import numpy as np
        B, L, H, E, F, C = (8, 2048, 128, 8, 256, 2)
        b, l, h = x.shape
        e = Wg.shape[1]
        k = min(max(int(l * C / e), 1), l)
        S = jax.nn.softmax(x @ Wg, axis=-1)
        St = jnp.swapaxes(S, 1, 2)
        G, I = jax.lax.top_k(St, k)
        ex = jnp.take_along_axis(x[:, None], I[..., None], axis=2)
        hmid = jax.nn.gelu(jnp.einsum('bekh,ehf->bekf', ex, W1) + b1[None, :, None, :], approximate=False)
        out = jnp.einsum('bekf,efh->bekh', hmid, W2) + b2[None, :, None, :]
        vals = G[..., None] * out
        new_x = jnp.zeros_like(x).at[jnp.arange(b)[:, None, None], I].add(vals)
        return new_x

    def _L1_attn_ref(x, w_qkv, temperature, w_out, b_out):
        import jax, jax.numpy as jnp
        import numpy as np
        B, N, DIM = (2, 1024, 128)
        HEADS, HEAD_DIM = (8, 64)
        INNER = HEADS * HEAD_DIM
        b, n, _ = x.shape
        qkv = x @ w_qkv
        q, k, v = jnp.split(qkv, 3, axis=-1)
        q = q.reshape(b, HEADS, n, HEAD_DIM)
        k = k.reshape(b, HEADS, n, HEAD_DIM)
        v = v.reshape(b, HEADS, n, HEAD_DIM)
        scores = jnp.einsum('bhnd,bhmd->bhnm', q, k) * jnp.exp(temperature)
        mask = jnp.eye(n, dtype=bool)
        mask_value = jnp.finfo(scores.dtype).min
        scores = jnp.where(mask, mask_value, scores)
        attn = jax.nn.softmax(scores, axis=-1)
        out = jnp.einsum('bhnm,bhmd->bhnd', attn, v)
        out = out.reshape(b, n, HEADS * HEAD_DIM)
        return out @ w_out + b_out

    def _L1_ffn_ref(x, Wr, br, W1, b1, W2, b2):
        import jax, jax.numpy as jnp
        import numpy as np
        B, S, D = (8, 1024, 128)
        H = 512
        O = 128
        E = 8
        TOP_K = 1
        b, s, d = x.shape
        xf = x.reshape(-1, d)
        router_logits = xf @ Wr + br
        topk_logits, topk_idx = jax.lax.top_k(router_logits, TOP_K)
        topk_gates = jax.nn.softmax(topk_logits, axis=1)
        out = jnp.zeros((xf.shape[0], O), dtype=x.dtype)
        for k in range(TOP_K):
            idx_k = topk_idx[:, k]
            gate_k = topk_gates[:, k:k + 1]
            for e in range(E):
                h = jax.nn.relu(xf @ W1[e] + b1[e])
                oe = h @ W2[e] + b2[e]
                mask = (idx_k == e)[:, None]
                out = out + jnp.where(mask, gate_k * oe, 0.0)
        return out.reshape(b, s, O)
    h = _L0_tok_ref(x, L0_tok_W, L0_tok_b)
    h = h + _L0_attn_ref(_layernorm(h, axis=-1), L0_attn_wq, L0_attn_bq, L0_attn_wk, L0_attn_bk, L0_attn_wv, L0_attn_bv, L0_attn_qcw, L0_attn_qcb, L0_attn_kcw, L0_attn_kcb, L0_attn_vcw, L0_attn_vcb, L0_attn_wo, L0_attn_bo, L0_attn_w1, L0_attn_b1, L0_attn_w2, L0_attn_b2, L0_attn_ln1_g, L0_attn_ln1_b, L0_attn_ln2_g, L0_attn_ln2_b)
    h = h + _L0_ffn_ref(_layernorm(h, axis=-1), L0_ffn_Wg, L0_ffn_W1, L0_ffn_b1, L0_ffn_W2, L0_ffn_b2)
    h = h + _L1_attn_ref(_layernorm(h, axis=-1), L1_attn_w_qkv, L1_attn_temperature, L1_attn_w_out, L1_attn_b_out)
    h = h + _L1_ffn_ref(_layernorm(h, axis=-1), L1_ffn_Wr, L1_ffn_br, L1_ffn_W1, L1_ffn_b1, L1_ffn_W2, L1_ffn_b2)
    return h

_drawn_inputs = setup_inputs


def setup_inputs(seed=0):
    import zlib

    import numpy as np

    out = dict(_drawn_inputs(seed))
    spreads = {'L0_tok_b': (0.0, 2.0),
     'L0_attn_ln1_g': (1.0, 0.2),
     'L0_attn_ln1_b': (0.0, 0.1),
     'L0_attn_ln2_g': (1.0, 0.2),
     'L0_attn_ln2_b': (0.0, 0.1),
     'L0_ffn_b1': (0.0, 0.448),
     'L0_ffn_b2': (0.0, 0.325),
     'L1_attn_b_out': (0.0, 0.1),
     'L1_ffn_br': (0.0, 0.1),
     'L1_ffn_b1': (0.0, 0.512),
     'L1_ffn_b2': (0.0, 0.1)}
    factors = {'L0_tok_W': 4.928,
     'L0_attn_wq': 42.886,
     'L0_attn_bq': 200.0,
     'L0_attn_wk': 24.088,
     'L0_attn_bk': 200.0,
     'L0_attn_wv': 8.0,
     'L0_attn_bv': 8.0,
     'L0_attn_qcw': 43.539,
     'L0_attn_qcb': 200.0,
     'L0_attn_kcw': 26.26,
     'L0_attn_kcb': 200.0,
     'L0_attn_vcw': 8.0,
     'L0_attn_vcb': 8.0,
     'L0_attn_wo': 8.0,
     'L0_attn_bo': 4.272,
     'L0_attn_w1': 5.762,
     'L0_attn_b1': 8.0,
     'L0_attn_w2': 5.354,
     'L0_attn_b2': 4.408}
    for name, (base, spread) in spreads.items():
        noise = np.random.default_rng([zlib.crc32(name.encode()), seed]).standard_normal(out[name].shape)
        drawn = base * np.exp(spread * noise) if base else spread * noise
        out[name] = jnp.asarray(drawn.astype(out[name].dtype))
    for name, factor in factors.items():
        out[name] = (out[name] * factor).astype(out[name].dtype)
    return out
```

```python
from contextlib import ExitStack

import numpy as np
import concourse.bass as bass
from concourse import mybir

NB, LIN, D = 16, 250, 128
K = 128
L = LIN - K + 1
G, BG = 4, 4
GL = BG * L
T = NB * L
H0, DK = 8, 16
NE = 8
FF = 2 * D
F0 = 256
CAP = max(min(int(L * 2 / NE), L), 1)
SL = NB * CAP
HC = NE // 2 * CAP
J, DH = 8, 64
CH = J * L
F1 = 512
NT = (T + NE * 127) // 128 + 1
NT += NT % 2
LN_EPS = 1e-5
EPS = 1e-6
BIG = -3.0e38

ALU = mybir.AluOpType
ACT = mybir.ActivationFunctionType
AX = mybir.AxisListType.X
F32 = mybir.dt.float32
BF16 = mybir.dt.bfloat16
I32 = mybir.dt.int32
U32 = mybir.dt.uint32

WA = {}
_at = 0
for _n, _c in (("tok", D), ("wq", D), ("wk", D), ("wv", D), ("wo", D), ("w1", FF), ("w2", 2 * D),
               ("tok_b", 1), ("bq", 1), ("bk", 1), ("bv", 1), ("qcw", 3), ("kcw", 3), ("vcw", 3),
               ("qcb", 1), ("kcb", 1), ("vcb", 1), ("b1", 2), ("b2", 1), ("ln1_g", 1), ("ln1_b", 1),
               ("temp", 1), ("bo", D), ("ln2_g", D), ("ln2_b", D)):
    WA[_n] = (_at, _at + _c)
    _at += _c
NWA = _at
WB = {}
_at = 0
for _n, _c in (("wg", NE), ("eb1", 2 * NE), ("eb2", NE), ("ew1", NE * F0), ("ew2", NE * 2 * D),
               ("wqk", J * 2 * DH), ("wv1", 4 * 2 * DH), ("wout", 4 * D), ("bout", D), ("wr", NE), ("br", NE),
               ("fb2", NE * D)):
    WB[_n] = (_at, _at + _c)
    _at += _c
NWB = _at
CC = {}
_at = 0
for _n, _c in (("ident", 128), ("block", 128), ("block8", 8), ("slot", CAP), ("tri", 128), ("ones", 128),
               ("e8", NE), ("e8m", NE), ("thr", NB), ("tile", NT), ("mhalf", BG)):
    CC[_n] = (_at, _at + _c)
    _at += _c
NCC = _at
NSLOT = 17
STOP = None


def constants():
    c = np.zeros((128, NCC), np.float32)
    p = np.arange(128)

    def put(name, v):
        c[:, CC[name][0]:CC[name][1]] = v

    put("ident", np.eye(128))
    put("block", p[:, None] // DK == p[None] // DK)
    put("block8", p[:, None] // DK == np.arange(8)[None])
    put("slot", np.arange(CAP)[None])
    put("tri", p[:, None] < p[None])
    put("ones", 1.0)
    put("e8", np.arange(NE)[None])
    put("e8m", np.arange(NE)[None] - NE)
    put("thr", 128 * np.arange(NB)[None])
    put("tile", np.arange(NT)[None])
    put("mhalf", -0.5)
    return c


def build(nc, xT_d, wa_d, wb_d, fw1_d, fw2_d, fb1_d, c_d, out_d, stop=None):
    ctx = ExitStack()
    with ctx:
        def sb(name, shape, dt=F32):
            return ctx.enter_context(nc.sbuf_tensor(name, shape, dt))

        def sem(name):
            return ctx.enter_context(nc.semaphore(name))

        arena = sb("arena", [128, NSLOT * 2048])
        kv = sb("kv", [128, NB, D + H0])
        wa = sb("wa_sb", [128, NWA])
        wb = sb("wb_sb", [128, NWB])
        cc = sb("cc", [128, NCC])
        ps = [ctx.enter_context(nc.psum_tensor(f"ps{i}", [128, 512], F32)) for i in range(8)]
        sorted_x = nc.dram_tensor("sorted_x", [NT * 128, D], F32, kind="Internal").ap()
        sorted_y = nc.dram_tensor("sorted_y", [NT * 128, D], F32, kind="Internal").ap()

        def A(name):
            return wa[:, WA[name][0]:WA[name][1]]

        def B(name):
            return wb[:, WB[name][0]:WB[name][1]]

        def C(name, p=128):
            return cc[0:p, CC[name][0]:CC[name][1]]

        def region(slot, cols, p=128, off=0):
            return arena[0:p, slot * 2048 + off:slot * 2048 + off + cols]

        ident = C("ident")

        xT = region(0, NB * LIN).rearrange("p (b l) -> p b l", b=NB)
        filt = region(2, NB * (LIN + 1)).rearrange("p (b l) -> p b l", b=NB)
        gel = region(0, 2 * T).rearrange("p (c n) -> p c n", c=2)
        hid = region(2, 2 * T).rearrange("p (c n) -> p c n", c=2)
        yT = region(4, T)
        attT = region(4, T)
        h = region(5, NB * D, L).rearrange("p (b d) -> p b d", b=NB)
        z = region(6, NB * D, L).rearrange("p (b d) -> p b d", b=NB)
        zT = region(7, T)
        pad = [region(8 + i, NB * (L + 2)).rearrange("p (b l) -> p b l", b=NB) for i in range(3)]
        elu_t = [region(8 + i, T) for i in range(2)]
        cv = [region(11 + i, T) for i in range(3)]
        ktok = region(14, NB * D, L).rearrange("p (b d) -> p b d", b=NB)
        vtok = region(15, NB * D, L).rearrange("p (b d) -> p b d", b=NB)
        zb = region(16, NB * D, L).rearrange("p (b d) -> p b d", b=NB)
        att = region(10, NB * D, L).rearrange("p (b d) -> p b d", b=NB)
        r1 = region(9, NB * D, L).rearrange("p (b d) -> p b d", b=NB)
        x1T = region(11, T)
        y2T = region(12, T)
        onehot = region(13, NE * SL, L).rearrange("p (b e j) -> p b e j", b=NB, e=NE)
        gated = region(2, NE * SL, L).rearrange("p (b e j) -> p b e j", b=NB, e=NE)
        ex = region(8, NE * SL).rearrange("p (e b j) -> p e b j", b=NB, e=NE)
        hm = region(10, 4 * SL).rearrange("p (r c n) -> p r c n", r=2, c=2)
        oT = region(11, NE * SL).rearrange("p (b e j) -> p b e j", b=NB, e=NE)
        gatedT = region(0, 2 * NB * L, HC).rearrange("p (b l) -> p b l", b=2 * NB)
        otok = region(8, 2 * NB * D, HC).rearrange("p (b d) -> p b d", b=2 * NB)
        o = 8 * 2048
        qT, kT, vT, vm, es, esT, oc, oP = [], [], [], [], [], [], [], []
        for _ in range(2):
            for lst, cols, parts in ((qT, CH, DH), (kT, CH, DH), (vT, CH, DH), (vm, F1, L), (es, CH, L),
                                     (esT, CH, L), (oc, F1, L), (oP, GL, 128)):
                lst.append(arena[0:parts, o:o + cols])
                o += cols
        assert o <= 15 * 2048
        fw1 = region(0, NE * F1)
        fw2 = region(2, NE * F1)
        fb1 = region(15, NE * F1)
        xt = [region(8, 128, off=128 * i) for i in range(2)]
        xtT = [region(8, 128, off=256 + 128 * i) for i in range(2)]
        hb = [region(9, F1, off=512 * i) for i in range(2)]
        hbT = [region(9, F1, off=1024 + 512 * i) for i in range(2)]
        ot = [region(8, 128, off=512 + 128 * i) for i in range(2)]
        back = region(10, NB * D, L).rearrange("p (b d) -> p b d", b=NB)
        outT = region(4, T)

        tk = sb("tk", [128, 8, NB])
        tau, npow, norm = tk[:, 3, :], tk[:, 6, :], tk[:, 7, :]
        st = sb("st", [L, NB, 6])
        mv = sb("mv", [L, NB, 2])
        rv = sb("rv", [L, NB])
        rs = sb("rs", [L, NB])
        ks = sb("ks", [128, NB])
        rd = sb("rd", [L, NB, H0])
        sm = sb("sm", [L, 4, NB, NE])
        gate = sb("gate", [L, NB, NE])
        red = sb("red", [L, 4, NB])
        choice = sb("choice", [128, 4, L])
        top8 = sb("top8", [128, 8])
        posl = sb("posl", [L, NB * NE])
        ksc = sb("ksc", [128, 2])
        mx = sb("mx", [L, 2, 2, J])
        sums = sb("sums", [L, 2, 2, J])
        identb = sb("identb", [L, L], BF16)
        negd = sb("negd", [L, 4, L], BF16)
        trib = sb("trib", [L, L], BF16)
        onesb = sb("onesb", [L, 128], BF16)
        ohb = sb("ohb", [L, NB, NE], BF16)
        cnt = sb("cnt", [128, 4, NE])
        cmp1 = sb("cmp1", [128, NE, NB])
        cmp2 = sb("cmp2", [128, NT, NE])
        tl = sb("tl", [128, 2, NT])
        expert = sb("expert", [128, NT], I32)
        posi = sb("posi", [L, NB], I32)
        junk = sb("junk", [128, 1])

        def sems(text):
            return [sem(n) for n in text.split()]

        x_in = [sem(f"x_in{g}") for g in range(G)]
        x_ld = [sem(f"x_ld{p}") for p in range(2)]
        y_st = [sem(f"y_st{p}") for p in range(2)]
        wa_in, wb_in, cc_in, fw_in, fb_in, zero_set, zero_out = sems(
            "wa_in wb_in cc_in fw_in fb_in zero_set zero_out")
        tokz, tau_e, filt_y, y_tr, h_in, pads = sems("tokz tau_e filt_y y_tr h_in pads")
        stats = [sem(f"stats{i}") for i in range(6)]
        rstd = [sem(f"rstd{i}") for i in range(6)]
        norm_ = [sem(f"norm{i}") for i in range(6)]
        z_tr = [sem(f"z_tr{i}") for i in range(4)]
        z_ev = [sem(f"z_ev{i}") for i in range(4)]
        q_mm, k_mm, v_mm, q_ev, k_ev, v_ev = sems("q_mm k_mm v_mm q_ev k_ev v_ev")
        v_cv, q_min, k_min, q_exp, k_exp, q_elu, k_elu = sems("v_cv q_min k_min q_exp k_exp q_elu k_elu")
        k_tr, v_tr, k_tok, v_tok, kv_mm, kv_ev, nd_mm = sems("k_tr v_tr k_tok v_tok kv_mm kv_ev nd_mm")
        att_n, att_tr, att_ev, proj, zb_s, r1_s = sems("att_n att_tr att_ev proj zb_s r1_s")
        n1_tr, x1_ev, w1_mm, gel_ev, hid_s, w2_mm, y2_s, y2_tr, hpre, h_l0 = sems(
            "n1_tr x1_ev w1_mm gel_ev hid_s w2_mm y2_s y2_tr hpre h_l0")
        lg0_mm, ga_sub, ga_exp, gate_s, st_tr, pos_s, pos_tr, oneh, gat_s, ga_mm, ex_ev = sems(
            "lg0_mm ga_sub ga_exp gate_s st_tr pos_s pos_tr oneh gat_s ga_mm ex_ev")
        e1_mm, e1_ev, e2_mm, e2_ev, ot_tr, ot_ev, gt_tr, gt_ev, sc_mm, h_l1 = sems(
            "e1_mm e1_ev e2_mm e2_ev ot_tr ot_ev gt_tr gt_ev sc_mm h_l1")
        scale_e, scale_s, bf_s = sems("scale_e scale_s bf_s")
        qk_mm, vv_mm, q4_ev, k4_ev, v4_ev, vt_tr, vm_ev, sc4_mm, max_s, exp_s = sems(
            "qk_mm vv_mm q4_ev k4_ev v4_ev vt_tr vm_ev sc4_mm max_s exp_s")
        es_tr, es_evA, es_evD, av_mm, o_nrm, o_tr, o_ev, pr_mm, h_l2 = sems(
            "es_tr es_evA es_evD av_mm o_nrm o_tr o_ev pr_mm h_l2")
        lg1_mm, ohb_s, rank_mm, pos_i, exp_i, scat = sems("lg1_mm ohb_s rank_mm pos_i exp_i scat")
        x_tr, x_ev, h_mm, hb_s, hb_tr, hb_ev, o_mm, o_s = sems("x_tr x_ev h_mm hb_s hb_tr hb_ev o_mm o_s")
        back_in, h_l3, out_tr, out_ev, out_st = sems("back_in h_l3 out_tr out_ev out_st")
        dve_n, pool_n = sems("dve_n pool_n")
        stage = {None: 9, "tok": 1, "attn0": 2, "moe0": 3, "attn1": 4}[stop]
        h_done = {1: (h_in, G), 2: (h_l0, G), 3: (h_l1, G), 4: (h_l2, NB), 9: (h_l3, G)}[stage]
        block = ctx.enter_context(nc.Block())

        def grp(t, g):
            return t[:, BG * g:BG * g + BG]

        def col(t, b, n=L):
            return t[:, b * n:(b + 1) * n]

        @block.sync
        def _(sp):
            sp.dma_start(cc[:], c_d).then_inc(cc_in, 16)
            sp.dma_start(wa[:], wa_d).then_inc(wa_in, 16)
            for g in range(G):
                sp.dma_start(grp(xT, g), grp(xT_d, g)).then_inc(x_in[g], 16)
            sp.dma_start(wb[:], wb_d).then_inc(wb_in, 16)
            sp.wait_ge(zero_set, 1)
            sp.dma_start(sorted_x.rearrange("(p r) d -> p (r d)", p=128), region(15, NT * 128)).then_inc(zero_out, 16)
            if stage > 4:
                sp.wait_ge(sc_mm, NB)
                sp.dma_start(fw1, fw1_d).then_inc(fw_in, 16)
                sp.dma_start(fw2, fw2_d).then_inc(fw_in, 16)
                sp.dma_start(fb1, fb1_d).then_inc(fb_in, 16)
                sp.wait_ge(scat, 16 * NB)

                def tiles(i, first):
                    for p in range(2):
                        if not first:
                            sp.wait_ge(x_tr, i * 2 + p - 1)
                        sp.dma_start(xt[p], sorted_x[bass.ds((i * 2 + p) * 128, 128), :]).then_inc(x_ld[p], 16)
                    for p in range(2):
                        sp.wait_ge(o_s, i * 2 + p + 1)
                        sp.dma_start(sorted_y[bass.ds((i * 2 + p) * 128, 128), :], ot[p]).then_inc(y_st[p], 16)

                tiles(0, True)
                with sp.Fori(1, NT // 2) as i:
                    tiles(i, False)
                for p in range(2):
                    sp.wait_ge(y_st[p], 16 * NT // 2)
            for g in range(G):
                sp.wait_ge(out_ev, g + 1)
                sp.dma_start(out_d[:, GL * g:GL * g + GL], outT[:, GL * g:GL * g + GL]).then_inc(out_st, 16)
            sp.wait_ge(out_st, 16 * G)
            sp.wait_ge(zero_out, 16)

        @block.tensor
        def _(pe):
            mm = nc.tensor.matmul

            def tr(out, in_):
                p = in_.shape[0]
                return nc.tensor.transpose(out, in_, ident[0:p, 0:p])

            def to_features(src, sem_in, banks, sem_out):
                for g in range(G):
                    pe.wait_ge(sem_in, g + 1)
                    for i in range(BG):
                        last = tr(ps[banks + g][:, i * L:(i + 1) * L], src[:, BG * g + i, :])
                    last.then_inc(sem_out, 1)

            def to_tokens(src, sem_in, banks, sem_out):
                for g in range(G):
                    pe.wait_ge(sem_in, g + 1)
                    for i in range(BG):
                        last = tr(ps[banks + g][0:L, i * D:(i + 1) * D], col(src, BG * g + i))
                    last.then_inc(sem_out, 1)

            def store():
                s, n = h_done
                for g in range(G):
                    pe.wait_ge(s, g + 1 if n == G else n)
                    for i in range(BG):
                        last = tr(ps[g][:, i * L:(i + 1) * L], h[:, BG * g + i, :])
                    last.then_inc(out_tr, 1)

            pe.wait_ge(cc_in, 16)
            pe.wait_ge(wa_in, 16)
            for g in range(G):
                pe.wait_ge(x_in[g], 16)
            mm(ps[4][:, 0:NB], A("tok"), xT[:, :, LIN - 1], start=True, stop=True).then_inc(tokz, 1)
            to_tokens(yT, filt_y, 0, y_tr)
            if stage == 1:
                return store()
            to_features(z, norm_[0], 4, z_tr[0])
            for g in range(G):
                zg = zT[:, GL * g:GL * g + GL]
                pe.wait_ge(z_ev[0], g + 1)
                mm(ps[g][:, 0:GL], A("wq"), zg, start=True, stop=True).then_inc(q_mm, 1)
                mm(ps[4 + g][:, 0:GL], A("wk"), zg, start=True, stop=True).then_inc(k_mm, 1)
            for g in range(G):
                pe.wait_ge(q_ev, g + 1)
                mm(ps[g][:, 0:GL], A("wv"), zT[:, GL * g:GL * g + GL], start=True, stop=True).then_inc(v_mm, 1)
            to_tokens(cv[2], v_cv, 0, v_tr)
            to_tokens(cv[1], k_elu, 4, k_tr)
            for g in range(G):
                pe.wait_ge(k_tok, g + 1)
                pe.wait_ge(v_tok, g + 1)
                for i in range(BG):
                    b = BG * g + i
                    mm(ps[4 + g][:, i * D:(i + 1) * D], ktok[:, b, :], vtok[:, b, :], start=True, stop=True)
                    last = mm(ps[g][:, i:i + 1], ktok[:, b, :], C("ones", L)[:, 0:1], start=True, stop=True)
                last.then_inc(kv_mm, 1)
            for g in range(G):
                pe.wait_ge(kv_ev, g + 1)
                pe.wait_ge(q_elu, g + 1)
                for i in range(BG):
                    b = BG * g + i
                    last = mm(ps[(4, 0)[i // 2] + g][0:L, (i % 2) * (D + H0):(i % 2 + 1) * (D + H0)],
                              col(cv[0], b), kv[:, b, :], start=True, stop=True)
                last.then_inc(nd_mm, 1)
            to_features(att, att_n, 4, att_tr)
            for g in range(G):
                pe.wait_ge(att_ev, g + 1)
                for i in range(BG):
                    last = mm(ps[g][0:L, i * D:(i + 1) * D], col(attT, BG * g + i), A("wo"), start=True, stop=True)
                last.then_inc(proj, 1)
            to_features(r1, norm_[1], 4, n1_tr)
            for g in range(G):
                pe.wait_ge(x1_ev, g + 1)
                for c in range(2):
                    mm(ps[4 * c + g][:, 0:GL], A("w1")[:, c * D:(c + 1) * D], x1T[:, GL * g:GL * g + GL],
                       start=True, stop=True).then_inc(w1_mm, 1)
            for g in range(G):
                pe.wait_ge(hid_s, g + 1)
                for c in range(2):
                    last = mm(ps[g][:, 0:GL], A("w2")[:, c * D:(c + 1) * D], hid[:, c, GL * g:GL * g + GL],
                              start=c == 0, stop=c == 1)
                last.then_inc(w2_mm, 1)
            to_tokens(y2T, y2_s, 4, y2_tr)
            if stage == 2:
                return store()
            to_features(z, norm_[3], 0, z_tr[1])
            pe.wait_ge(wb_in, 16)
            pe.wait_ge(z_ev[1], G)
            for b in range(NB):
                last = mm(ps[4][0:L, b * NE:(b + 1) * NE], col(zT, b), B("wg"), start=True, stop=True)
            last.then_inc(lg0_mm, 1)
            pe.wait_ge(gate_s, 1)
            tr(ps[5][:, 0:L], gate[:].rearrange("p b e -> p (b e)")).then_inc(st_tr, 1)
            pe.wait_ge(pos_s, 1)
            tr(ps[6][0:L, 0:128], choice[:, 3, :]).then_inc(pos_tr, 1)
            for b in range(NB):
                pe.wait_ge(oneh, b // BG + 1)
                last = mm(ps[b // 2][:, (b % 2) * NE * CAP:(b % 2 + 1) * NE * CAP], z[:, b, :],
                          onehot[:, b, :, :].rearrange("p e j -> p (e j)"), start=True, stop=True)
                if b % 2:
                    last.then_inc(ga_mm, 1)

            def expert_up(e):
                for c in range(2):
                    mm(ps[2 * (e % 2) + c][:, 0:SL], B("ew1")[:, (2 * e + c) * D:(2 * e + c + 1) * D],
                       ex[:, e, :, :].rearrange("p b j -> p (b j)"), start=True, stop=True).then_inc(e1_mm, 1)

            def gates_across(c):
                pe.wait_ge(gat_s, c // 2 + 1)
                if c >= 2:
                    pe.wait_ge(gt_ev, c - 1)
                for n in range(4):
                    q = 4 * c + n
                    half = gated[:, q // 2, NE // 2 * (q % 2):NE // 2 * (q % 2 + 1), :]
                    last = tr(ps[6 + c % 2][0:HC, n * L:(n + 1) * L], half.rearrange("p e j -> p (e j)"))
                last.then_inc(gt_tr, 1)

            pe.wait_ge(ex_ev, NB // 2)
            expert_up(0)
            for e in range(NE):
                if e + 1 < NE:
                    expert_up(e + 1)
                gates_across(e)
                pe.wait_ge(e1_ev, 2 * e + 2)
                if e >= 2:
                    pe.wait_ge(e2_ev, e - 1)
                for c in range(2):
                    last = mm(ps[4 + e % 2][:, 0:SL], B("ew2")[:, (2 * e + c) * D:(2 * e + c + 1) * D],
                              hm[:, e % 2, c, :], start=c == 0, stop=c == 1)
                last.then_inc(e2_mm, 1)
            pe.wait_ge(e2_ev, NE)
            for c in range(2 * NB // 4):
                if c >= 4:
                    pe.wait_ge(ot_ev, c - 3)
                for n in range(4):
                    q = 4 * c + n
                    half = oT[:, q // 2, NE // 2 * (q % 2):NE // 2 * (q % 2 + 1), :]
                    last = tr(ps[c % 4][0:HC, n * D:(n + 1) * D], half.rearrange("p e j -> p (e j)"))
                last.then_inc(ot_tr, 1)
            pe.wait_ge(gt_ev, 2 * NB // 4)
            for b in range(NB):
                pe.wait_ge(ot_ev, b // 2 + 1)
                for n in range(2):
                    last = mm(ps[4 + b // BG][0:L, (b % BG) * D:(b % BG + 1) * D], gatedT[:, 2 * b + n, :],
                              otok[:, 2 * b + n, :], start=n == 0, stop=n == 1)
                last.then_inc(sc_mm, 1)
            if stage == 3:
                return store()
            to_features(z, norm_[4], 0, z_tr[2])
            pe.wait_ge(z_ev[2], G)
            pe.wait_ge(bf_s, 2)

            def attention(i, first):
                for p in range(2):
                    b, X = i * 2 + p, 4 * p
                    zb_ = zT[:, bass.ds(b * L, L)]
                    for j in range(J):
                        last = mm(ps[X + j // 4][:, (j % 4) * L:(j % 4 + 1) * L],
                                  B("wqk")[:, j * 2 * DH:(j + 1) * 2 * DH], zb_, start=True, stop=True)
                        if j % 4 == 3:
                            last.then_inc(qk_mm, 1)
                    if not first:
                        pe.wait_ge(h_l2, b - 1)
                    for j in range(4):
                        last = mm(ps[X + 2][:, j * L:(j + 1) * L], B("wv1")[:, j * 128:(j + 1) * 128], zb_,
                                  start=True, stop=True)
                    last.then_inc(vv_mm, 1)
                for p in range(2):
                    b, X = i * 2 + p, 4 * p
                    pe.wait_ge(q4_ev, b * 2 + 2)
                    pe.wait_ge(k4_ev, b * 2 + 2)
                    pe.wait_ge(v4_ev, b * 2 + 2)
                    for q in range(2):
                        mm(ps[X + q][0:L, 0:4 * L], identb[:], negd[:].rearrange("p a l -> p (a l)"),
                           start=True, stop=False, skip_group_check=True)
                        for a in range(4):
                            hh = 4 * q + a
                            last = mm(ps[X + q][0:L, a * L:(a + 1) * L], col(qT[p], hh), col(kT[p], hh),
                                      start=False, stop=True, skip_group_check=True)
                        last.then_inc(sc4_mm, 1)
                    for hh in range(J):
                        last = tr(ps[X + 3][0:L, hh * DH:(hh + 1) * DH], col(vT[p], hh))
                    last.then_inc(vt_tr, 1)
                for p in range(2):
                    b, X = i * 2 + p, 4 * p
                    pe.wait_ge(vm_ev, b + 1)
                    for q in range(2):
                        pe.wait_ge(exp_s, b * 2 + q + 1)
                        for a in range(4):
                            last = tr(ps[X + 2 + q][0:L, a * L:(a + 1) * L], col(es[p], 4 * q + a))
                        last.then_inc(es_tr, 1)
                    pe.wait_ge(es_evA, b + 1)
                    pe.wait_ge(es_evD, b + 1)
                    for hh in range(J):
                        last = mm(ps[X][0:L, hh * DH:(hh + 1) * DH], col(esT[p], hh), vm[p][:, hh * DH:(hh + 1) * DH],
                                  start=True, stop=True)
                    last.then_inc(av_mm, 1)
                for p in range(2):
                    b, X = i * 2 + p, 4 * p
                    pe.wait_ge(o_nrm, b + 1)
                    for m in range(4):
                        last = tr(ps[X + 1][:, m * L:(m + 1) * L], oc[p][:, m * 128:(m + 1) * 128])
                    last.then_inc(o_tr, 1)
                for p in range(2):
                    b, X = i * 2 + p, 4 * p
                    pe.wait_ge(o_ev, b + 1)
                    for m in range(4):
                        last = mm(ps[X + 2][0:L, 0:D], oP[p].rearrange("p (t m) -> p m t", m=4)[:, m, :],
                                  B("wout")[:, m * D:(m + 1) * D], start=m == 0, stop=m == 3)
                    last.then_inc(pr_mm, 1)

            attention(0, True)
            with pe.Fori(1, NB // 2) as i:
                attention(i, False)
            if stage == 4:
                return store()
            to_features(z, norm_[5], 0, z_tr[3])
            pe.wait_ge(z_ev[3], G)
            for b in range(NB):
                last = mm(ps[4][0:L, b * NE:(b + 1) * NE], col(zT, b), B("wr"), start=True, stop=True)
            last.then_inc(lg1_mm, 1)
            pe.wait_ge(ohb_s, 1)
            ohf = ohb[:].rearrange("p b e -> p (b e)")
            mm(ps[5][0:L, 0:NB * NE], trib[:], ohf, start=True, stop=False, skip_group_check=True)
            for s in range(1, NB):
                mm(ps[5][0:L, s * NE:NB * NE], onesb[:, 0:L], ohf[:, 0:(NB - s) * NE], start=False, stop=s == NB - 1,
                   skip_group_check=True)
            for b in range(NB):
                last = mm(ps[6][:, 0:NE], onesb[:], ohb[:, b, :], start=b == 0, stop=b == NB - 1)
            last.then_inc(rank_mm, 1)
            pe.wait_ge(fw_in, 32)
            pe.wait_ge(exp_i, 1)

            def tiles(i, first):
                es_ = [pe.value_load(expert[0:1, bass.ds(i * 2 + p, 1)], min_val=0, max_val=NE - 1) for p in range(2)]
                for p in range(2):
                    pe.wait_ge(x_ld[p], (i + 1) * 16)
                    tr(ps[4 * p][:, 0:128], xt[p]).then_inc(x_tr, 1)
                for p in range(2):
                    pe.wait_ge(x_ev, i * 2 + p + 1)
                    mm(ps[4 * p + 1][:, 0:F1], xtT[p], fw1[:, bass.ds(es_[p] * F1, F1)], start=True, stop=True)\
                        .then_inc(h_mm, 1)
                for p in range(2):
                    pe.wait_ge(hb_s, i * 2 + p + 1)
                    for c in range(4):
                        last = tr(ps[4 * p + 2][:, c * 128:(c + 1) * 128], hb[p][:, c * 128:(c + 1) * 128])
                    last.then_inc(hb_tr, 1)
                for p in range(2):
                    pe.wait_ge(hb_ev, i * 2 + p + 1)
                    if not first:
                        pe.wait_ge(o_s, i * 2 + p - 1)
                    for c in range(4):
                        last = mm(ps[4 * p + 3][:, 0:D], hbT[p][:, c * 128:(c + 1) * 128],
                                  fw2[:, bass.ds(es_[p] * F1 + c * D, D)], start=c == 0, stop=c == 3)
                    last.then_inc(o_mm, 1)

            tiles(0, True)
            with pe.Fori(1, NT // 2) as i:
                tiles(i, False)
            store()

        @block.scalar
        def _(act):
            fn = nc.scalar.activation

            def evacuate(banks, dst, sem_in, sem_out):
                for g in range(G):
                    act.wait_ge(sem_in, g + 1)
                    fn(dst[:, GL * g:GL * g + GL], ps[banks + g][:, 0:GL], ACT.Copy).then_inc(sem_out, 1)

            act.wait_ge(tokz, 1)
            act.wait_ge(tau_e, 1)
            fn(tk[:, 1, :], ps[4][:, 0:NB], ACT.Exp, bias=tk[:, 0, 0:1], scale=-0.1).then_inc(tau_e, 1)
            for g in range(G):
                act.wait_ge(y_tr, g + 1)
                fn(grp(h, g).rearrange("p b d -> p (b d)"), ps[g][0:L, :], ACT.Copy).then_inc(h_in, 1)
            if stage > 1:
                evacuate(4, zT, z_tr[0], z_ev[0])
                act.wait_ge(pads, 1)
                for g in range(G):
                    for (mm_s, bank, name, dst, ev) in ((q_mm, g, "bq", 0, q_ev), (k_mm, 4 + g, "bk", 1, k_ev)):
                        act.wait_ge(mm_s, g + 1)
                        fn(grp(pad[dst], g)[:, :, 2:], ps[bank][:, 0:GL].rearrange("p (b l) -> p b l", b=BG),
                           ACT.Identity, bias=A(name)).then_inc(ev, 1)
                for g in range(G):
                    act.wait_ge(v_mm, g + 1)
                    fn(grp(pad[2], g)[:, :, 2:], ps[g][:, 0:GL].rearrange("p (b l) -> p b l", b=BG),
                       ACT.Identity, bias=A("bv")).then_inc(v_ev, 1)
                for g in range(G):
                    for (min_s, t, ex_s) in ((q_min, elu_t[0], q_exp), (k_min, elu_t[1], k_exp)):
                        act.wait_ge(min_s, g + 1)
                        fn(t[:, GL * g:GL * g + GL], t[:, GL * g:GL * g + GL], ACT.Exp).then_inc(ex_s, 1)
                for g in range(G):
                    act.wait_ge(k_tr, g + 1)
                    fn(grp(ktok, g).rearrange("p b d -> p (b d)"), ps[4 + g][0:L, :], ACT.Copy).then_inc(k_tok, 1)
                evacuate(4, attT, att_tr, att_ev)
                for g in range(G):
                    act.wait_ge(n1_tr, g + 1)
                    fn(x1T[:, GL * g:GL * g + GL], ps[4 + g][:, 0:GL], ACT.Identity, bias=A("ln1_b"), scale=A("ln1_g"))\
                        .then_inc(x1_ev, 1)
                for g in range(G):
                    for c in range(2):
                        act.wait_ge(w1_mm, 2 * g + c + 1)
                        fn(gel[:, c, GL * g:GL * g + GL], ps[4 * c + g][:, 0:GL], ACT.Gelu, bias=A("b1")[:, c:c + 1])\
                            .then_inc(gel_ev, 1)
            if stage > 2:
                evacuate(0, zT, z_tr[1], z_ev[1])
                act.wait_ge(ga_sub, 1)
                fn(sm[:, 1], sm[:, 0], ACT.Exp).then_inc(ga_exp, 1)
                fn(ksc[:, 0:1], A("temp"), ACT.Exp).then_inc(scale_e, 1)
                for n in range(NB // 2):
                    act.wait_ge(ga_mm, n + 1)
                    fn(ex[:, :, 2 * n:2 * n + 2, :].rearrange("p e b j -> p b e j"),
                       ps[n][:, 0:2 * NE * CAP].rearrange("p (b e j) -> p b e j", b=2, e=NE), ACT.Copy).then_inc(ex_ev, 1)
                for e in range(NE):
                    if e >= 2:
                        act.wait_ge(e2_mm, e - 1)
                    for c in range(2):
                        act.wait_ge(e1_mm, 2 * e + c + 1)
                        fn(hm[:, e % 2, c, :], ps[2 * (e % 2) + c][:, 0:SL], ACT.Gelu,
                           bias=B("eb1")[:, 2 * e + c:2 * e + c + 1]).then_inc(e1_ev, 1)
                for c in range(2 * NB // 4):
                    act.wait_ge(ot_tr, c + 1)
                    fn(otok[:, 4 * c:4 * c + 4, :].rearrange("p q d -> p (q d)"), ps[c % 4][0:HC, :], ACT.Copy)\
                        .then_inc(ot_ev, 1)
            if stage > 3:
                evacuate(0, zT, z_tr[2], z_ev[2])
                act.wait_ge(scale_s, 1)

                def attention(i, first):
                    for p in range(2):
                        b, X = i * 2 + p, 4 * p
                        for q in range(2):
                            act.wait_ge(qk_mm, b * 2 + q + 1)
                            fn(qT[p].rearrange("p (t j) -> p j t", j=J)[:, 4 * q:4 * q + 4, :],
                               ps[X + q][0:DH, 0:4 * L].rearrange("p (j t) -> p j t", j=4), ACT.Copy).then_inc(q4_ev, 1)
                        act.wait_ge(vv_mm, b + 1)
                        for q in range(2):
                            fn(vT[p].rearrange("p (t j q) -> p j t q", j=4, q=2)[:, :, :, q],
                               ps[X + 2][q * DH:(q + 1) * DH, 0:4 * L].rearrange("p (j t) -> p j t", j=4), ACT.Copy)\
                                .then_inc(v4_ev, 1)
                    for p in range(2):
                        b, X = i * 2 + p, 4 * p
                        for q in range(2):
                            act.wait_ge(max_s, b * 2 + q + 1)
                            for a in range(4):
                                hh = 4 * q + a
                                last = fn(col(es[p], hh), ps[X + q][0:L, a * L:(a + 1) * L], ACT.Exp,
                                          bias=mx[:, p, 1, hh:hh + 1], scale=ksc[0:L, 0:1],
                                          accum_out=sums[:, p, 0, hh:hh + 1])
                            last.then_inc(exp_s, 1)
                    for p in range(2):
                        b, X = i * 2 + p, 4 * p
                        act.wait_ge(es_tr, b * 2 + 1)
                        fn(esT[p][:, 0:4 * L], ps[X + 2][0:L, 0:4 * L], ACT.Copy).then_inc(es_evA, 1)

                attention(0, True)
                with act.Fori(1, NB // 2) as i:
                    attention(i, False)
            if stage > 4:
                evacuate(0, zT, z_tr[3], z_ev[3])

                def tiles(i, first):
                    for p in range(2):
                        act.wait_ge(x_tr, i * 2 + p + 1)
                        fn(xtT[p], ps[4 * p][:, 0:128], ACT.Copy).then_inc(x_ev, 1)
                    for p in range(2):
                        act.wait_ge(hb_tr, i * 2 + p + 1)
                        fn(hbT[p], ps[4 * p + 2][:, :], ACT.Relu).then_inc(hb_ev, 1)

                tiles(0, True)
                with act.Fori(1, NT // 2) as i:
                    tiles(i, False)
            evacuate(0, outT, out_tr, out_ev)

        @block.gpsimd
        def _(pool):
            count = [0]

            def own(ins):
                count[0] += 1
                ins.then_inc(pool_n, 1)
                pool.wait_ge(pool_n, count[0])

            def rsqrt(n):
                for g in range(G):
                    pool.wait_ge(stats[n], g + 1)
                    own(nc.gpsimd.tensor_scalar(rv[:, BG * g:BG * g + BG], mv[:, BG * g:BG * g + BG, 1], LN_EPS, None, ALU.add))
                    nc.gpsimd.tensor_tensor(rs[:, BG * g:BG * g + BG], rv[:, BG * g:BG * g + BG], C("mhalf", L), ALU.pow)\
                        .then_inc(rstd[n], 1)

            nc.gpsimd.memset(region(15, NT * 128), 0.0).then_inc(zero_set, 1)
            for i in range(3):
                last = nc.gpsimd.memset(pad[i][:, :, 0:2], 0.0)
            last.then_inc(pads, 1)
            pool.wait_ge(cc_in, 16)
            pool.wait_ge(wa_in, 16)
            if stage > 1:
                rsqrt(0)
                pool.wait_ge(zero_out, 16)
                for g in range(G):
                    pool.wait_ge(norm_[0], g + 1)
                    nc.gpsimd.tensor_tensor(grp(zb, g), grp(z, g), A("bo")[0:L, None, :].to_broadcast([L, BG, D]),
                                            ALU.add).then_inc(zb_s, 1)
                u = region(3, GL).rearrange("p (b l) -> p b l", b=BG)
                for g in range(G):
                    pool.wait_ge(v_ev, g + 1)
                    src, dst = grp(pad[2], g), col(cv[2], g, GL).rearrange("p (b l) -> p b l", b=BG)
                    w = A("vcw")
                    own(nc.gpsimd.tensor_scalar(dst, src[:, :, 0:L], w[:, 0:1], A("vcb"), ALU.mult, ALU.add))
                    for j in (1, 2):
                        own(nc.gpsimd.tensor_scalar(u, src[:, :, j:j + L], w[:, j:j + 1], None, ALU.mult))
                        last = nc.gpsimd.tensor_tensor(dst, dst, u, ALU.add)
                        if j == 1:
                            own(last)
                    last.then_inc(v_cv, 1)
                    pool.wait_ge(v_cv, g + 1)
                for g in range(G):
                    nc.gpsimd.tensor_tensor(grp(h, g), grp(h, g), A("ln2_b")[0:L, None, :].to_broadcast([L, BG, D]),
                                            ALU.add).then_inc(hpre, 1)
                rsqrt(1)
                for g in range(G):
                    pool.wait_ge(gel_ev, 2 * g + 2)
                    nc.gpsimd.tensor_tensor(hid[:, :, GL * g:GL * g + GL], gel[:, :, GL * g:GL * g + GL],
                                            gel[:, :, GL * g:GL * g + GL], ALU.mult).then_inc(hid_s, 1)
                rsqrt(2)
            if stage > 2:
                rsqrt(3)
                for g in range(G):
                    pool.wait_ge(oneh, g + 1)
                    nc.gpsimd.tensor_tensor(grp(gated, g).rearrange("p b e j -> p (b e) j"),
                                            grp(onehot, g).rearrange("p b e j -> p (b e) j"),
                                            grp(gate, g).rearrange("p b e -> p (b e)")[:, :, None]
                                            .to_broadcast([L, BG * NE, CAP]), ALU.mult).then_inc(gat_s, 1)
            if stage > 3:
                rsqrt(4)
            if stage > 4:
                rsqrt(5)
                pool.wait_ge(norm_[5], G)
                pool.wait_ge(pos_i, 1)
                for b in range(NB):
                    nc.gpsimd.indirect_dma_start(sorted_x, bass.IndirectOffsetOnAxis(ap=posi[:, b:b + 1], axis=0),
                                                 z[:, b, :], None).then_inc(scat, 16)
                for p in range(2):
                    pool.wait_ge(y_st[p], 16 * NT // 2)
                for b in range(NB):
                    nc.gpsimd.indirect_dma_start(back[:, b, :], None, sorted_y,
                                                 bass.IndirectOffsetOnAxis(ap=posi[:, b:b + 1], axis=0)).then_inc(back_in, 16)
                pool.wait_ge(back_in, 16 * NB)

        @block.vector
        def _(dve):
            V = nc.vector
            count = [0]

            def own(ins):
                count[0] += 1
                ins.then_inc(dve_n, 1)
                dve.wait_ge(dve_n, count[0])

            def layer_stats(n, src_of, wait, every=True):
                for g in range(G):
                    if wait is not None:
                        dve.wait_ge(wait, g + 1)
                    for i in range(BG):
                        last = V.bn_stats(st[:, BG * g + i, :], src_of(BG * g + i))
                    own(last)
                    for i in range(BG):
                        last = V.bn_aggr(mv[:, BG * g + i, :], st[:, BG * g + i, :])
                    last.then_inc(stats[n], 1)

            def layer_norm(n, src, dst):
                for g in range(G):
                    dve.wait_ge(stats[n], g + 1)
                    dve.wait_ge(rstd[n], g + 1)
                    for b in range(BG * g, BG * g + BG):
                        last = V.tensor_scalar(dst[:, b, :], src[:, b, :], mv[:, b, 0:1], rs[:, b:b + 1],
                                               ALU.subtract, ALU.mult)
                    last.then_inc(norm_[n], 1)

            dve.wait_ge(wa_in, 16)
            V.tensor_scalar(tk[:, 0, 0:1], A("tok_b"), -0.1, 3.0, ALU.mult, ALU.add).then_inc(tau_e, 1)
            own(V.memset(filt[:, :, 0:1], 0.0))
            dve.wait_ge(tau_e, 2)
            own(V.tensor_scalar(tk[:, 2, :], tk[:, 1, :], 1.0, None, ALU.add))
            own(V.reciprocal(tau, tk[:, 2, :]))
            own(V.tensor_scalar(tk[:, 5, :], tau, 1.0, None, ALU.add))
            own(V.tensor_tensor(tk[:, 4, :], tau, tau, ALU.mult))
            n = 2
            while n < K:
                own(V.scalar_tensor_tensor(tk[:, 5, :], tk[:, 4, :], 1.0, tk[:, 5, :], ALU.add, ALU.mult))
                own(V.tensor_tensor(tk[:, 4, :], tk[:, 4, :], tk[:, 4, :], ALU.mult))
                n *= 2
            assert n == K
            own(V.reciprocal(norm, tk[:, 5, :]))
            own(V.tensor_scalar(npow, tk[:, 4, :], -1.0, None, ALU.mult))
            for g in range(G):
                dve.wait_ge(x_in[g], 16)
                bs = range(BG * g, BG * g + BG)
                for b in bs:
                    last = V.tensor_tensor_scan(filt[:, b, 1:], tau[:, b:b + 1].to_broadcast([128, LIN]), xT[:, b, :],
                                                0.0, ALU.mult, ALU.add)
                own(last)
                for b in bs:
                    last = V.scalar_tensor_tensor(col(yT, b), filt[:, b, 0:L], npow[:, b:b + 1], filt[:, b, K:K + L],
                                                  ALU.mult, ALU.add)
                own(last)
                for b in bs:
                    last = V.tensor_scalar(col(yT, b), col(yT, b), norm[:, b:b + 1], None, ALU.mult)
                last.then_inc(filt_y, 1)
            if stage > 1:
                layer_stats(0, lambda b: h[:, b, :], h_in)
                layer_norm(0, h, z)
                for g in range(G):
                    for (src, t, dst, ev, w, cb, mn) in ((pad[0], elu_t[0], cv[0], q_ev, "qcw", "qcb", q_min),
                                                        (pad[1], elu_t[1], cv[1], k_ev, "kcw", "kcb", k_min)):
                        dve.wait_ge(ev, g + 1)
                        s, d = grp(src, g), col(dst, g, GL)
                        d3 = d.rearrange("p (b l) -> p b l", b=BG)
                        own(V.tensor_scalar(d3, s[:, :, 0:L], A(w)[:, 0:1], A(cb), ALU.mult, ALU.add))
                        for j in (1, 2):
                            own(V.scalar_tensor_tensor(d3, s[:, :, j:j + L], A(w)[:, j:j + 1], d3, ALU.mult, ALU.add))
                        V.tensor_scalar(col(t, g, GL), d, 0.0, None, ALU.min).then_inc(mn, 1)
                for g in range(G):
                    for (t, dst, xs, el) in ((elu_t[1], cv[1], k_exp, k_elu), (elu_t[0], cv[0], q_exp, q_elu)):
                        dve.wait_ge(xs, g + 1)
                        d = col(dst, g, GL)
                        V.scalar_tensor_tensor(d, d, 0.0, col(t, g, GL), ALU.max, ALU.add).then_inc(el, 1)
                dve.wait_ge(zero_out, 16)
                for g in range(G):
                    dve.wait_ge(v_tr, g + 1)
                    V.tensor_copy(grp(vtok, g).rearrange("p b d -> p (b d)"), ps[g][0:L, :]).then_inc(v_tok, 1)
                for g in range(G):
                    dve.wait_ge(kv_mm, g + 1)
                    own(V.tensor_scalar(ks[:, BG * g:BG * g + BG], ps[g][:, 0:BG], EPS, None, ALU.add))
                    V.tensor_tensor(grp(kv, g)[:, :, 0:D], ps[4 + g][:, :].rearrange("p (b d) -> p b d", b=BG),
                                    C("block")[:, None, :].to_broadcast([128, BG, D]), ALU.mult)
                    V.tensor_tensor(grp(kv, g)[:, :, D:], C("block8")[:, None, :].to_broadcast([128, BG, H0]),
                                    ks[:, BG * g:BG * g + BG, None].to_broadcast([128, BG, H0]), ALU.mult).then_inc(kv_ev, 1)
                for g in range(G):
                    dve.wait_ge(nd_mm, g + 1)
                    for n in range(2):
                        b = BG * g + 2 * n
                        nd = ps[(4, 0)[n] + g][0:L, 0:2 * (D + H0)].rearrange("p (b d) -> p b d", b=2)
                        own(V.reciprocal(rd[:, b:b + 2, :], nd[:, :, D:]))
                        last = V.tensor_tensor(att[:, b:b + 2, :].rearrange("p b (h d) -> p b h d", d=DK),
                                               nd[:, :, 0:D].rearrange("p b (h d) -> p b h d", d=DK),
                                               rd[:, b:b + 2, :, None].to_broadcast([L, 2, H0, DK]), ALU.mult)
                    last.then_inc(att_n, 1)
                for g in range(G):
                    dve.wait_ge(proj, g + 1)
                    dve.wait_ge(zb_s, g + 1)
                    V.tensor_tensor(grp(r1, g), ps[g][0:L, :].rearrange("p (b d) -> p b d", b=BG), grp(zb, g), ALU.add)\
                        .then_inc(r1_s, 1)
                layer_stats(1, lambda b: r1[:, b, :], r1_s)
                layer_norm(1, r1, r1)
                for g in range(G):
                    dve.wait_ge(w2_mm, g + 1)
                    V.scalar_tensor_tensor(col(y2T, g, GL), ps[g][:, 0:GL], A("b2"), col(x1T, g, GL), ALU.add, ALU.add)\
                        .then_inc(y2_s, 1)
                pb = lambda b: ps[4 + b // BG][0:L, (b % BG) * D:(b % BG + 1) * D]
                layer_stats(2, pb, y2_tr)
                for g in range(G):
                    dve.wait_ge(stats[2], g + 1)
                    dve.wait_ge(rstd[2], g + 1)
                    dve.wait_ge(hpre, g + 1)
                    for b in range(BG * g, BG * g + BG):
                        last = V.scalar_tensor_tensor(r1[:, b, :], pb(b), mv[:, b, 0:1], A("ln2_g")[0:L, :],
                                                      ALU.subtract, ALU.mult)
                    own(last)
                    for b in range(BG * g, BG * g + BG):
                        last = V.scalar_tensor_tensor(h[:, b, :], r1[:, b, :], rs[:, b:b + 1], h[:, b, :],
                                                      ALU.mult, ALU.add)
                    last.then_inc(h_l0, 1)
            if stage > 2:
                layer_stats(3, lambda b: h[:, b, :], h_l0)
                layer_norm(3, h, z)
                lg = ps[4][0:L, 0:NB * NE].rearrange("p (b e) -> p b e", b=NB)
                wide = lambda r: r[:, :, None].to_broadcast([L, NB, NE])
                dve.wait_ge(lg0_mm, 1)
                own(V.tensor_reduce(red[:, 0], lg, AX, ALU.max))
                V.tensor_tensor(sm[:, 0], lg, wide(red[:, 0]), ALU.subtract).then_inc(ga_sub, 1)
                dve.wait_ge(ga_exp, 1)
                own(V.tensor_reduce(red[:, 1], sm[:, 1], AX, ALU.add))
                own(V.reciprocal(red[:, 2], red[:, 1]))
                V.tensor_tensor(gate[:], sm[:, 1], wide(red[:, 2]), ALU.mult).then_inc(gate_s, 1)
                dve.wait_ge(st_tr, 1)
                own(V.tensor_copy(choice[:, 0, :], ps[5][:, 0:L]))
                for n in range(0, CAP, 8):
                    own(V.max(top8[:], choice[:, 0, :]))
                    if CAP - n < 8:
                        own(V.memset(top8[:, CAP - n:8], -1.0))
                    own(V.match_replace(choice[:, 0, :], top8[:], choice[:, 0, :], -1.0))
                own(V.tensor_scalar(choice[:, 1, :], choice[:, 0, :], -1.0, None, ALU.is_equal))
                own(V.tensor_tensor_scan(choice[:, 2, :], C("ones")[:, 0:L], choice[:, 1, :], 0.0, ALU.mult, ALU.add))
                own(V.tensor_tensor(choice[:, 3, :], choice[:, 2, :], choice[:, 1, :], ALU.mult))
                V.tensor_scalar(choice[:, 3, :], choice[:, 3, :], -1.0, None, ALU.add).then_inc(pos_s, 1)
                dve.wait_ge(pos_tr, 1)
                own(V.tensor_copy(posl[:], ps[6][0:L, 0:128]))
                nbe = BG * NE
                for g in range(G):
                    V.tensor_tensor(grp(onehot, g).rearrange("p b e j -> p (b e) j"),
                                    posl[:, g * nbe:(g + 1) * nbe, None].to_broadcast([L, nbe, CAP]),
                                    C("slot", L)[:, None, :].to_broadcast([L, nbe, CAP]), ALU.is_equal).then_inc(oneh, 1)
                for e in range(NE):
                    dve.wait_ge(gt_tr, e + 1)
                    V.tensor_copy(gatedT[:, 4 * e:4 * e + 4, :].rearrange("p q l -> p (q l)"), ps[6 + e % 2][0:HC, 0:4 * L])\
                        .then_inc(gt_ev, 1)
                    dve.wait_ge(e2_mm, e + 1)
                    V.tensor_scalar(oT[:, :, e, :], ps[4 + e % 2][:, 0:SL].rearrange("p (b j) -> p b j", b=NB),
                                    B("eb2")[:, e:e + 1], None, ALU.add).then_inc(e2_ev, 1)
                for g in range(G):
                    dve.wait_ge(sc_mm, BG * g + BG)
                    V.tensor_tensor(grp(h, g), ps[4 + g][0:L, :].rearrange("p (b d) -> p b d", b=BG), grp(h, g), ALU.add)\
                        .then_inc(h_l1, 1)
            if stage > 3:
                layer_stats(4, lambda b: h[:, b, :], h_l1)
                layer_norm(4, h, z)
                V.tensor_copy(identb[:], C("ident", L)[:, 0:L]).then_inc(bf_s, 1)
                V.tensor_scalar(negd[:], C("ident", L)[:, None, 0:L].to_broadcast([L, 4, L]), BIG, None, ALU.mult)\
                    .then_inc(bf_s, 1)
                dve.wait_ge(scale_e, 1)
                V.tensor_scalar(ksc[:, 1:2], ksc[:, 0:1], -1.0, None, ALU.mult).then_inc(scale_s, 1)
                dve.wait_ge(scale_s, 1)
                base = count[0]

                def attention(i, first):
                    done = [0]

                    def own2(ins):
                        done[0] += 1
                        ins.then_inc(dve_n, 1)
                        dve.wait_ge(dve_n, i * 8 + base + done[0])

                    for p in range(2):
                        b, X = i * 2 + p, 4 * p
                        for q in range(2):
                            dve.wait_ge(qk_mm, b * 2 + q + 1)
                            dve.wait_ge(q4_ev, b * 2 + q + 1)
                            V.tensor_copy(kT[p].rearrange("p (t j) -> p j t", j=J)[:, 4 * q:4 * q + 4, :],
                                          ps[X + q][DH:128, 0:4 * L].rearrange("p (j t) -> p j t", j=4)).then_inc(k4_ev, 1)
                    for p in range(2):
                        b, X = i * 2 + p, 4 * p
                        for q in range(2):
                            dve.wait_ge(sc4_mm, b * 2 + q + 1)
                            own2(V.tensor_reduce(mx[:, p, 0, 4 * q:4 * q + 4],
                                                 ps[X + q][0:L, 0:4 * L].rearrange("p (a l) -> p a l", a=4), AX, ALU.max))
                            V.tensor_scalar(mx[:, p, 1, 4 * q:4 * q + 4], mx[:, p, 0, 4 * q:4 * q + 4], ksc[0:L, 1:2], None,
                                            ALU.mult).then_inc(max_s, 1)
                        dve.wait_ge(vt_tr, b + 1)
                        V.tensor_copy(vm[p], ps[X + 3][0:L, :]).then_inc(vm_ev, 1)
                    for p in range(2):
                        b, X = i * 2 + p, 4 * p
                        dve.wait_ge(es_tr, b * 2 + 2)
                        V.tensor_copy(esT[p][:, 4 * L:], ps[X + 3][0:L, 0:4 * L]).then_inc(es_evD, 1)
                        dve.wait_ge(exp_s, b * 2 + 2)
                        own2(V.reciprocal(sums[:, p, 1, :], sums[:, p, 0, :]))
                        dve.wait_ge(av_mm, b + 1)
                        V.tensor_tensor(oc[p].rearrange("p (h d) -> p h d", h=J),
                                        ps[X][0:L, :].rearrange("p (h d) -> p h d", h=J),
                                        sums[:, p, 1, :, None].to_broadcast([L, J, DH]), ALU.mult).then_inc(o_nrm, 1)
                    for p in range(2):
                        b, X = i * 2 + p, 4 * p
                        dve.wait_ge(o_tr, b + 1)
                        for r in range(2):
                            for n in range(2):
                                cnt_n = (L - n + 1) // 2
                                par, at = (r + n) % 2, (r * L + n) // 2
                                src = ps[X + 1][r * DH:(r + 1) * DH, 0:4 * L].rearrange("p (m n) -> p m n", m=4)
                                dst = oP[p][par * DH:(par + 1) * DH, :].rearrange("p (m n) -> p m n", m=4)
                                last = V.tensor_copy(dst[:, :, at:at + cnt_n], src[:, :, bass.ds(n, cnt_n, step=2)])
                        last.then_inc(o_ev, 1)
                    for p in range(2):
                        b, X = i * 2 + p, 4 * p
                        dve.wait_ge(pr_mm, b + 1)
                        hb_ = h[:, bass.ds(b, 1), :].rearrange("p b d -> p (b d)")
                        own2(V.tensor_tensor(hb_, ps[X + 2][0:L, 0:D], hb_, ALU.add))
                        V.tensor_tensor(hb_, hb_, B("bout")[0:L, :], ALU.add).then_inc(h_l2, 1)
                    assert done[0] == 8

                attention(0, True)
                with dve.Fori(1, NB // 2) as i:
                    attention(i, False)
                count[0] += 8 * NB // 2
            if stage > 4:
                dve.wait_ge(h_l2, NB)
                layer_stats(5, lambda b: h[:, b, :], None)
                layer_norm(5, h, z)
                own(V.tensor_copy(trib[:], C("tri", L)[:, 0:L]))
                own(V.tensor_copy(onesb[:], C("ones", L)))
                over_b = lambda c: c[:, None, :].to_broadcast([L, NB, NE])
                dve.wait_ge(lg1_mm, 1)
                own(V.tensor_tensor(sm[:, 0], lg, over_b(B("br")[0:L, :]), ALU.add))
                own(V.tensor_reduce(red[:, 0], sm[:, 0], AX, ALU.max))
                own(V.tensor_tensor(sm[:, 1], sm[:, 0], wide(red[:, 0]), ALU.is_equal))
                own(V.scalar_tensor_tensor(sm[:, 2], sm[:, 1], -float(NE), over_b(C("e8", L)), ALU.mult, ALU.add))
                own(V.tensor_reduce(red[:, 1], sm[:, 2], AX, ALU.min))
                own(V.tensor_tensor(sm[:, 3], over_b(C("e8m", L)), wide(red[:, 1]), ALU.is_equal))
                V.tensor_copy(ohb[:], sm[:, 3]).then_inc(ohb_s, 1)
                dve.wait_ge(rank_mm, 1)
                own(V.tensor_copy(cnt[:, 0, :], ps[6][:, 0:NE]))
                own(V.tensor_tensor(cmp1[:], cnt[:, 0, :, None].to_broadcast([128, NE, NB]),
                                    C("thr")[:, None, :].to_broadcast([128, NE, NB]), ALU.is_gt))
                own(V.tensor_reduce(cnt[:, 1, :], cmp1[:], AX, ALU.add))
                own(V.tensor_tensor_scan(cnt[:, 2, :], C("ones")[:, 0:NE], cnt[:, 1, :], 0.0, ALU.mult, ALU.add))
                own(V.tensor_tensor(cnt[:, 3, :], cnt[:, 2, :], cnt[:, 1, :], ALU.subtract))
                own(V.tensor_scalar(cnt[:, 3, :], cnt[:, 3, :], 128.0, None, ALU.mult))
                own(V.tensor_tensor(sm[:, 0], ps[5][0:L, 0:NB * NE].rearrange("p (b e) -> p b e", b=NB),
                                    over_b(cnt[0:L, 3, :]), ALU.add))
                own(V.tensor_tensor(sm[:, 1], sm[:, 0], sm[:, 3], ALU.mult))
                own(V.tensor_reduce(red[:, 2], sm[:, 1], AX, ALU.add))
                V.tensor_copy(posi[:], red[:, 2]).then_inc(pos_i, 1)
                own(V.tensor_tensor(cmp2[:], cnt[:, 2, None, :].to_broadcast([128, NT, NE]),
                                    C("tile")[:, :, None].to_broadcast([128, NT, NE]), ALU.is_le))
                own(V.tensor_reduce(tl[:, 0, :], cmp2[:], AX, ALU.add))
                V.tensor_scalar(expert[:], tl[:, 0, :], float(NE - 1), None, ALU.min).then_inc(exp_i, 1)
                dve.wait_ge(exp_i, 1)
                dve.wait_ge(fb_in, 16)

                def tiles(i, first):
                    es_ = [dve.value_load(expert[0:1, bass.ds(i * 2 + p, 1)], min_val=0, max_val=NE - 1)
                           for p in range(2)]
                    for p in range(2):
                        dve.wait_ge(h_mm, i * 2 + p + 1)
                        V.tensor_tensor(hb[p], ps[4 * p + 1][:, :], fb1[:, bass.ds(es_[p] * F1, F1)], ALU.add)\
                            .then_inc(hb_s, 1)
                    for p in range(2):
                        dve.wait_ge(o_mm, i * 2 + p + 1)
                        if not first:
                            dve.wait_ge(y_st[p], i * 16)
                        V.tensor_tensor(ot[p], ps[4 * p + 3][:, 0:D], B("fb2")[:, bass.ds(es_[p] * D, D)], ALU.add)\
                            .then_inc(o_s, 1)

                tiles(0, True)
                with dve.Fori(1, NT // 2) as i:
                    tiles(i, False)
                dve.wait_ge(back_in, 16 * NB)
                for g in range(G):
                    V.tensor_tensor(grp(h, g), grp(back, g), grp(h, g), ALU.add).then_inc(h_l3, 1)


def kernel(**inputs):
    import numpy as _np
    import concourse.bacc as _bacc
    from concourse import mybir as _mybir
    from concourse.bass_utils import run_bass_kernel_spmd as _run

    a = {k: _np.asarray(v) for k, v in inputs.items()}

    def column(v):
        return v.reshape(-1, 1)

    def rows(v):
        return _np.broadcast_to(v.reshape(1, -1), (128, v.size))

    p0 = "L0_attn_"
    part_a = {
        "tok": a["L0_tok_W"].T, "tok_b": column(a["L0_tok_b"]),
        "w1": a[p0 + "w1"].T, "w2": a[p0 + "w2"].T.reshape(2, D, D).transpose(1, 0, 2).reshape(D, 2 * D),
        "b1": a[p0 + "b1"].reshape(2, D).T, "b2": column(a[p0 + "b2"]),
        "ln1_g": column(a[p0 + "ln1_g"]), "ln1_b": column(a[p0 + "ln1_b"]),
        "temp": _np.broadcast_to(a["L1_attn_temperature"].reshape(1, 1), (128, 1)),
        "bo": rows(a[p0 + "bo"]), "ln2_g": rows(a[p0 + "ln2_g"]), "ln2_b": rows(a[p0 + "ln2_b"]),
    }
    for n in "qkvo":
        part_a["w" + n] = a[p0 + "w" + n].T
    for n in "qkv":
        part_a["b" + n] = column(a[p0 + "b" + n])
        part_a[n + "cw"] = _np.tile(a[p0 + n + "cw"], (H0, 1))
        part_a[n + "cb"] = _np.tile(column(a[p0 + n + "cb"]), (H0, 1))
    wqkv = a["L1_attn_w_qkv"]
    part_b = {
        "wg": a["L0_ffn_Wg"], "eb1": a["L0_ffn_b1"].reshape(2 * NE, D).T, "eb2": a["L0_ffn_b2"].T,
        "ew1": a["L0_ffn_W1"].transpose(1, 0, 2).reshape(D, NE * F0),
        "ew2": a["L0_ffn_W2"].reshape(NE * 2, D, D).transpose(1, 0, 2).reshape(D, NE * 2 * D),
        "wqk": wqkv[:, 0:2 * J * DH].reshape(D, 2, J, DH).transpose(0, 2, 1, 3).reshape(D, 2 * J * DH),
        "wv1": wqkv[:, 2 * J * DH:],
        "wout": a["L1_attn_w_out"].reshape(4, D, D).transpose(1, 0, 2).reshape(D, 4 * D),
        "bout": rows(a["L1_attn_b_out"]), "wr": a["L1_ffn_Wr"], "br": rows(a["L1_ffn_br"]),
        "fb2": rows(a["L1_ffn_b2"]),
    }
    arrays = {
        "xT": a["x"].transpose(2, 0, 1),
        "wa": _np.concatenate([part_a[n] for n in WA], axis=1),
        "wb": _np.concatenate([part_b[n] for n in WB], axis=1),
        "fw1": a["L1_ffn_W1"].transpose(1, 0, 2).reshape(D, NE * F1),
        "fw2": a["L1_ffn_W2"].reshape(NE * 4, D, D).transpose(1, 0, 2).reshape(D, NE * 4 * D),
        "fb1": rows(a["L1_ffn_b1"]),
        "consts": constants(),
    }
    arrays = {k: _np.ascontiguousarray(v) for k, v in arrays.items()}
    nc = _bacc.Bacc("TRN2", target_bir_lowering=False, num_devices=1)
    args = [nc.dram_tensor(k, v.shape, _mybir.dt.from_np(v.dtype), kind="ExternalInput").ap() for k, v in arrays.items()]
    args.append(nc.dram_tensor("outT", (D, T), _mybir.dt.float32, kind="ExternalOutput").ap())
    build(nc, *args, stop=STOP)
    r = _run(nc, [arrays], core_ids=[0])
    return r.results[0]["outT"].reshape(D, NB, L).transpose(1, 2, 0)
```

```python
from contextlib import ExitStack

import numpy as np
import concourse.bass as bass
from concourse import mybir

NB, LIN, D = 16, 250, 128
K = 128
L = LIN - K + 1
G, BG = 4, 4
GL = BG * L
T = NB * L
H0, DK = 8, 16
NE = 8
FF = 2 * D
F0 = 256
CAP = max(min(int(L * 2 / NE), L), 1)
SL = NB * CAP
HC = NE // 2 * CAP
J, DH = 8, 64
CH = J * L
F1 = 512
NT = (T + NE * 127) // 128
LN_EPS = 1e-5
EPS = 1e-6
BIG = -3.0e38

ALU = mybir.AluOpType
ACT = mybir.ActivationFunctionType
AX = mybir.AxisListType.X
F32 = mybir.dt.float32
FR = mybir.dt.float32r
BF16 = mybir.dt.bfloat16
I32 = mybir.dt.int32
U32 = mybir.dt.uint32

WA = {}
_at = 0
for _n, _c in (("tok", D), ("wq", D), ("wk", D), ("wv", D), ("wo", D), ("w1", FF), ("w2", 2 * D),
               ("tok_b", 1), ("bq", 1), ("bk", 1), ("bv", 1), ("qcw", 3), ("kcw", 3), ("vcw", 3),
               ("qcb", 1), ("kcb", 1), ("vcb", 1), ("b1", 2), ("b2", 1), ("ln1_g", 1), ("ln1_b", 1),
               ("temp", 1), ("bo", D), ("ln2_g", D), ("ln2_b", D)):
    WA[_n] = (_at, _at + _c)
    _at += _c
NWA = _at
WB = {}
_at = 0
for _n, _c in (("wg", NE), ("eb1", 2 * NE), ("eb2", NE), ("ew1", NE * F0), ("ew2", NE * 2 * D),
               ("wout", 4 * D), ("bout", D), ("wr", NE), ("br", NE)):
    WB[_n] = (_at, _at + _c)
    _at += _c
NWB = _at
CC = {}
_at = 0
for _n, _c in (("ident", 128), ("block", 128), ("block8", 8), ("slot", CAP), ("tri", 128), ("ones", 128),
               ("e8", NE), ("e8m", NE), ("thr", NB), ("tile", NT), ("mhalf", BG), ("first", NT + 1), ("token", NB), ("r128", 128), ("none", 1)):
    CC[_n] = (_at, _at + _c)
    _at += _c
NCC = _at
NT_LOOP = (NT - 1) // 4 * 4
NSLOT = 17
P2 = 2 * L
NQKV = 3 * J * DH
STOP = None


def constants():
    c = np.zeros((128, NCC), np.float32)
    p = np.arange(128)

    def put(name, v):
        c[:, CC[name][0]:CC[name][1]] = v

    put("ident", np.eye(128))
    put("block", p[:, None] // DK == p[None] // DK)
    put("block8", p[:, None] // DK == np.arange(8)[None])
    put("slot", np.arange(CAP)[None])
    put("tri", p[:, None] < p[None])
    put("ones", 1.0)
    put("e8", np.arange(NE)[None])
    put("e8m", np.arange(NE)[None] - NE)
    put("thr", 128 * np.arange(NB)[None])
    put("tile", np.arange(NT)[None])
    put("mhalf", -0.5)
    put("first", 128 * np.arange(NT + 1)[None])
    put("token", 1 + p[:, None] + L * np.arange(NB)[None])
    put("r128", np.arange(128)[None] - 128)
    put("none", T + 1 + p[:, None])
    return c


def build(nc, xT_d, wa_d, wb_d, fw1_d, fw2_d, fb_d, wqkv_d, c_d, out_d, stop=None):
    ctx = ExitStack()
    with ctx:
        def sb(name, shape, dt=F32):
            return ctx.enter_context(nc.sbuf_tensor(name, shape, dt))

        def sem(name):
            return ctx.enter_context(nc.semaphore(name))

        arena = sb("arena", [128, NSLOT * 2048 + 128])
        z_hi, z_lo = sb("z_hi", [128, T], FR), sb("z_lo", [128, T], FR)
        w_hi, w_lo = sb("w_hi", [128, NQKV], FR), sb("w_lo", [128, NQKV], FR)
        wa = sb("wa_sb", [128, NWA])
        wb = sb("wb_sb", [128, NWB])
        cc = sb("cc", [128, NCC])
        ps = [ctx.enter_context(nc.psum_tensor(f"ps{i}", [128, 512], F32)) for i in range(8)]
        rows_d = nc.dram_tensor("rows", [T, 2 * D], F32, kind="Internal").ap()

        def A(name):
            return wa[:, WA[name][0]:WA[name][1]]

        def B(name):
            return wb[:, WB[name][0]:WB[name][1]]

        def C(name, p=128):
            return cc[0:p, CC[name][0]:CC[name][1]]

        def region(slot, cols, p=128, off=0):
            return arena[0:p, slot * 2048 + off:slot * 2048 + off + cols]

        ident = C("ident")

        xT = region(0, NB * LIN).rearrange("p (b l) -> p b l", b=NB)
        filt = region(2, NB * (LIN + 1)).rearrange("p (b l) -> p b l", b=NB)
        gel = region(0, 2 * T).rearrange("p (c n) -> p c n", c=2)
        hid = region(2, 2 * T).rearrange("p (c n) -> p c n", c=2)
        yT = region(4, T)
        attT = region(4, T)
        h = region(5, NB * D, L).rearrange("p (b d) -> p b d", b=NB)
        z = region(6, NB * D, L).rearrange("p (b d) -> p b d", b=NB)
        zT = region(7, T)
        pad = [region(8 + i, NB * (L + 2)).rearrange("p (b l) -> p b l", b=NB) for i in range(3)]
        elu_t = [region(8 + i, T) for i in range(2)]
        cv = [region(11 + i, T) for i in range(3)]
        ktok = region(14, NB * D, L).rearrange("p (b d) -> p b d", b=NB)
        vtok = region(15, NB * D, L).rearrange("p (b d) -> p b d", b=NB)
        zb = region(0, NB * D, L).rearrange("p (b d) -> p b d", b=NB)
        att = region(10, NB * D, L).rearrange("p (b d) -> p b d", b=NB)
        r1 = region(9, NB * D, L).rearrange("p (b d) -> p b d", b=NB)
        x1T = region(11, T)
        y2T = region(12, T)
        kv = region(16, NB * (D + H0), off=0).rearrange("p (b d) -> p b d", b=NB)
        wqkv = region(15, NQKV)
        onehot = region(13, NE * SL, L).rearrange("p (b e j) -> p b e j", b=NB, e=NE)
        gated = region(2, NE * SL, L).rearrange("p (b e j) -> p b e j", b=NB, e=NE)
        ex = region(8, NE * SL).rearrange("p (e b j) -> p e b j", b=NB, e=NE)
        hm = region(10, 4 * SL).rearrange("p (r c n) -> p r c n", r=2, c=2)
        oT = region(11, NE * SL).rearrange("p (b e j) -> p b e j", b=NB, e=NE)
        gatedT = region(0, 2 * NB * L, HC).rearrange("p (b l) -> p b l", b=2 * NB)
        otok = region(8, 2 * NB * D, HC).rearrange("p (b d) -> p b d", b=2 * NB)
        o = 8 * 2048
        vm, es, esT, oc, oP = [], [], [], [], []
        qT, kT, vT = [arena[0:DH, o + 2 * CH * n:o + 2 * CH * (n + 1)] for n in range(3)]
        o += 6 * CH
        for _ in range(2):
            for lst, cols, parts in ((vm, F1, L), (es, CH, L), (esT, CH, L), (oc, F1, L), (oP, GL, 128)):
                lst.append(arena[0:parts, o:o + cols])
                o += cols
        assert o <= 15 * 2048
        fw1 = region(0, NE * F1)
        fw2 = region(2, NE * F1)
        fb = region(14, NE * (F1 + D), off=1024)
        row = [region(8, 2 * D, off=2 * D * i) for i in range(4)]
        xtT = [region(8, 128, off=1024 + 128 * i) for i in range(2)]
        ot = [region(8, 128, off=1280 + 128 * i) for i in range(4)]
        hb = [region(9, F1, off=512 * i) for i in range(2)]
        hbT = [region(9, F1, off=1024 + 512 * i) for i in range(2)]
        slot_of = region(10, NB * 128, L).rearrange("p (b r) -> p b r", b=NB)
        reach = region(11, NB * (NT + 1), L).rearrange("p (b t) -> p b t", b=NB)
        tile_of = region(11, NB * NT, L, off=512).rearrange("p (b t) -> p b t", b=NB)

        tk = sb("tk", [128, 8, NB])
        tau, npow, norm = tk[:, 3, :], tk[:, 6, :], tk[:, 7, :]
        st = sb("st", [L, NB, 6])
        mv = sb("mv", [L, NB, 2])
        rv = sb("rv", [L, NB])
        rs = sb("rs", [L, NB])
        ks = sb("ks", [128, NB])
        rd = sb("rd", [L, NB, H0])
        sm = sb("sm", [L, 4, NB, NE])
        gate = sb("gate", [L, NB, NE])
        red = sb("red", [L, 4, NB])
        choice = sb("choice", [128, 4, L])
        top8 = sb("top8", [128, 8])
        posl = sb("posl", [L, NB * NE])
        ksc = sb("ksc", [128, 2])
        mx = sb("mx", [L, 2, 2, J])
        sums = sb("sums", [L, 2, 2, J])
        identb = sb("identb", [L, L], BF16)
        negd = sb("negd", [L, 4, L], BF16)
        trib = sb("trib", [L, L], BF16)
        onesb = sb("onesb", [L, 128], BF16)
        ohb = sb("ohb", [L, NB, NE], BF16)
        cnt = sb("cnt", [128, 4, NE])
        cmp1 = sb("cmp1", [128, NE, NB])
        cmp2 = sb("cmp2", [128, NT, NE])
        tl = sb("tl", [128, 2, NT])
        expert = sb("expert", [128, NT + 4], I32)
        held = sb("held", [128, 4, NT])
        take, give = sb("take", [128, NT], I32), sb("give", [128, NT], I32)

        def sems(text):
            return [sem(n) for n in text.split()]

        x_in = [sem(f"x_in{g}") for g in range(G)]
        x_ld = [sem(f"x_ld{p}") for p in range(4)]
        y_st = [sem(f"y_st{p}") for p in range(4)]
        wa_in, wb_in, cc_in, fw_in, fb_in, wqkv_in, w_split, rows_st = sems(
            "wa_in wb_in cc_in fw_in fb_in wqkv_in w_split rows_st")
        tokz, tau_e, filt_y, y_tr, h_in, pads = sems("tokz tau_e filt_y y_tr h_in pads")
        stats = [sem(f"stats{i}") for i in range(6)]
        rstd = [sem(f"rstd{i}") for i in range(6)]
        norm_ = [sem(f"norm{i}") for i in range(6)]
        z_tr = [sem(f"z_tr{i}") for i in range(4)]
        z_ev = [sem(f"z_ev{i}") for i in range(4)]
        q_mm, k_mm, v_mm, q_ev, k_ev, v_ev = sems("q_mm k_mm v_mm q_ev k_ev v_ev")
        v_cv, q_min, k_min, q_exp, k_exp, q_elu, k_elu = sems("v_cv q_min k_min q_exp k_exp q_elu k_elu")
        k_tr, v_tr, k_tok, v_tok, kv_mm, kv_ev, nd_mm = sems("k_tr v_tr k_tok v_tok kv_mm kv_ev nd_mm")
        att_n, att_tr, att_ev, proj, zb_s, r1_s = sems("att_n att_tr att_ev proj zb_s r1_s")
        n1_tr, x1_ev, w1_mm, gel_ev, hid_s, w2_mm, y2_s, y2_tr, hpre, h_l0 = sems(
            "n1_tr x1_ev w1_mm gel_ev hid_s w2_mm y2_s y2_tr hpre h_l0")
        lg0_mm, ga_sub, ga_exp, gate_s, st_tr, pos_s, pos_tr, oneh, gat_s, ga_mm, ex_ev = sems(
            "lg0_mm ga_sub ga_exp gate_s st_tr pos_s pos_tr oneh gat_s ga_mm ex_ev")
        e1_mm, e1_ev, e2_mm, e2_ev, ot_tr, ot_ev, gt_tr, gt_ev, sc_mm, h_l1 = sems(
            "e1_mm e1_ev e2_mm e2_ev ot_tr ot_ev gt_tr gt_ev sc_mm h_l1")
        scale_e, scale_s, bf_s = sems("scale_e scale_s bf_s")
        qk_mm, vv_mm, q4_ev, k4_ev, v4_ev, vt_tr, vm_ev, sc4_mm, max_s, exp_s = sems(
            "qk_mm vv_mm q4_ev k4_ev v4_ev vt_tr vm_ev sc4_mm max_s exp_s")
        es_tr, es_evA, es_evD, av_mm, o_nrm, o_tr, o_ev, pr_mm, h_l2 = sems(
            "es_tr es_evA es_evD av_mm o_nrm o_tr o_ev pr_mm h_l2")
        lg1_mm, ohb_s, rank_mm, slot_s, held_mm, exp_i, take_s, give_s = sems(
            "lg1_mm ohb_s rank_mm slot_s held_mm exp_i take_s give_s")
        x_tr, x_ev, h_mm, hb_s, hb_tr, hb_ev, o_mm, o_s = sems("x_tr x_ev h_mm hb_s hb_tr hb_ev o_mm o_s")
        out_st, z_lo_s = sems("out_st z_lo_s")
        dve_n, pool_n = sems("dve_n pool_n")
        stage = {None: 9, "tok": 1, "attn0": 2, "moe0": 3, "attn1": 4}[stop]
        h_done = {1: (h_in, G), 2: (h_l0, G), 3: (h_l1, G), 4: (h_l2, NB), 9: (None, 0)}[stage]
        block = ctx.enter_context(nc.Block())

        def grp(t, g):
            return t[:, BG * g:BG * g + BG]

        def col(t, b, n=L):
            return t[:, b * n:(b + 1) * n]

        def chunks(t, f):
            return t.rearrange("p (b t j) -> p j b t", b=2, j=J)[:, 2 * f:2 * f + 2]

        @block.sync
        def _(sp):
            sp.dma_start(cc[:], c_d).then_inc(cc_in, 16)
            sp.dma_start(wa[:], wa_d).then_inc(wa_in, 16)
            for g in range(G):
                sp.dma_start(grp(xT, g), grp(xT_d, g)).then_inc(x_in[g], 16)
            sp.dma_start(wqkv, wqkv_d).then_inc(wqkv_in, 16)
            sp.dma_start(wb[:], wb_d).then_inc(wb_in, 16)

            def by_tokens(dst, src, signal):
                d = dst.rearrange("(b l) c -> l b c", b=NB)
                for lo, hi in ((0, 120), (120, L)):
                    sp.dma_start(d[lo:hi], src[lo:hi]).then_inc(signal, 16)

            if stage > 4:
                sp.wait_ge(sc_mm, NB)
                sp.dma_start(fw1, fw1_d).then_inc(fw_in, 16)
                sp.dma_start(fw2, fw2_d).then_inc(fw_in, 16)
                sp.dma_start(fb, fb_d).then_inc(fb_in, 16)
                sp.wait_ge(h_l2, NB)
                by_tokens(rows_d[:, D:], h, rows_st)
                sp.wait_ge(norm_[5], G)
                by_tokens(rows_d[:, 0:D], z, rows_st)
                for q in range(4):
                    sp.wait_ge(y_st[q], 16 * ((NT - q + 3) // 4))
            else:
                sp.wait_ge(h_done[0], h_done[1])
                by_tokens(out_d, h, out_st)
                sp.wait_ge(out_st, 32)

        @block.tensor
        def _(pe):
            mm = nc.tensor.matmul

            def tr(out, in_):
                p = in_.shape[0]
                return nc.tensor.transpose(out, in_, ident[0:p, 0:p])

            def to_features(src, sem_in, banks, sem_out):
                for g in range(G):
                    pe.wait_ge(sem_in, g + 1)
                    for i in range(BG):
                        last = tr(ps[banks + g][:, i * L:(i + 1) * L], src[:, BG * g + i, :])
                    last.then_inc(sem_out, 1)

            def to_tokens(src, sem_in, banks, sem_out):
                for g in range(G):
                    pe.wait_ge(sem_in, g + 1)
                    for i in range(BG):
                        last = tr(ps[banks + g][0:L, i * D:(i + 1) * D], col(src, BG * g + i))
                    last.then_inc(sem_out, 1)

            pe.wait_ge(cc_in, 16)
            pe.wait_ge(wa_in, 16)
            for g in range(G):
                pe.wait_ge(x_in[g], 16)
            mm(ps[4][:, 0:NB], A("tok"), xT[:, :, LIN - 1], start=True, stop=True).then_inc(tokz, 1)
            to_tokens(yT, filt_y, 0, y_tr)
            if stage == 1:
                return
            to_features(z, norm_[0], 4, z_tr[0])
            for g in range(G):
                zg = zT[:, GL * g:GL * g + GL]
                pe.wait_ge(z_ev[0], g + 1)
                mm(ps[g][:, 0:GL], A("wq"), zg, start=True, stop=True).then_inc(q_mm, 1)
                mm(ps[4 + g][:, 0:GL], A("wk"), zg, start=True, stop=True).then_inc(k_mm, 1)
            for g in range(G):
                pe.wait_ge(q_ev, g + 1)
                mm(ps[g][:, 0:GL], A("wv"), zT[:, GL * g:GL * g + GL], start=True, stop=True).then_inc(v_mm, 1)
            to_tokens(cv[2], v_cv, 0, v_tr)
            to_tokens(cv[1], k_elu, 4, k_tr)
            for g in range(G):
                pe.wait_ge(k_tok, g + 1)
                pe.wait_ge(v_tok, g + 1)
                for i in range(BG):
                    b = BG * g + i
                    mm(ps[4 + g][:, i * D:(i + 1) * D], ktok[:, b, :], vtok[:, b, :], start=True, stop=True)
                    last = mm(ps[g][:, i:i + 1], ktok[:, b, :], C("ones", L)[:, 0:1], start=True, stop=True)
                last.then_inc(kv_mm, 1)
            for g in range(G):
                pe.wait_ge(kv_ev, g + 1)
                pe.wait_ge(q_elu, g + 1)
                for i in range(BG):
                    b = BG * g + i
                    last = mm(ps[(4, 0)[i // 2] + g][0:L, (i % 2) * (D + H0):(i % 2 + 1) * (D + H0)],
                              col(cv[0], b), kv[:, b, :], start=True, stop=True)
                last.then_inc(nd_mm, 1)
            to_features(att, att_n, 4, att_tr)
            for g in range(G):
                pe.wait_ge(att_ev, g + 1)
                for i in range(BG):
                    last = mm(ps[g][0:L, i * D:(i + 1) * D], col(attT, BG * g + i), A("wo"), start=True, stop=True)
                last.then_inc(proj, 1)
            to_features(r1, norm_[1], 4, n1_tr)
            for g in range(G):
                pe.wait_ge(x1_ev, g + 1)
                for c in range(2):
                    mm(ps[4 * c + g][:, 0:GL], A("w1")[:, c * D:(c + 1) * D], x1T[:, GL * g:GL * g + GL],
                       start=True, stop=True).then_inc(w1_mm, 1)
            for g in range(G):
                pe.wait_ge(hid_s, g + 1)
                for c in range(2):
                    last = mm(ps[g][:, 0:GL], A("w2")[:, c * D:(c + 1) * D], hid[:, c, GL * g:GL * g + GL],
                              start=c == 0, stop=c == 1)
                last.then_inc(w2_mm, 1)
            to_tokens(y2T, y2_s, 4, y2_tr)
            if stage == 2:
                return
            to_features(z, norm_[3], 0, z_tr[1])
            pe.wait_ge(wb_in, 16)
            pe.wait_ge(z_ev[1], G)
            for b in range(NB):
                last = mm(ps[4][0:L, b * NE:(b + 1) * NE], col(zT, b), B("wg"), start=True, stop=True)
            last.then_inc(lg0_mm, 1)
            pe.wait_ge(gate_s, 1)
            tr(ps[5][:, 0:L], gate[:].rearrange("p b e -> p (b e)")).then_inc(st_tr, 1)
            pe.wait_ge(pos_s, 1)
            tr(ps[6][0:L, 0:128], choice[:, 3, :]).then_inc(pos_tr, 1)
            for b in range(NB):
                pe.wait_ge(oneh, b // BG + 1)
                last = mm(ps[b // 2][:, (b % 2) * NE * CAP:(b % 2 + 1) * NE * CAP], z[:, b, :],
                          onehot[:, b, :, :].rearrange("p e j -> p (e j)"), start=True, stop=True)
                if b % 2:
                    last.then_inc(ga_mm, 1)

            def expert_up(e):
                for c in range(2):
                    mm(ps[2 * (e % 2) + c][:, 0:SL], B("ew1")[:, (2 * e + c) * D:(2 * e + c + 1) * D],
                       ex[:, e, :, :].rearrange("p b j -> p (b j)"), start=True, stop=True).then_inc(e1_mm, 1)

            def gates_across(c):
                pe.wait_ge(gat_s, c // 2 + 1)
                if c >= 2:
                    pe.wait_ge(gt_ev, c - 1)
                for n in range(4):
                    q = 4 * c + n
                    half = gated[:, q // 2, NE // 2 * (q % 2):NE // 2 * (q % 2 + 1), :]
                    last = tr(ps[6 + c % 2][0:HC, n * L:(n + 1) * L], half.rearrange("p e j -> p (e j)"))
                last.then_inc(gt_tr, 1)

            pe.wait_ge(ex_ev, NB // 2)
            expert_up(0)
            for e in range(NE):
                if e + 1 < NE:
                    expert_up(e + 1)
                gates_across(e)
                pe.wait_ge(e1_ev, 2 * e + 2)
                if e >= 2:
                    pe.wait_ge(e2_ev, e - 1)
                for c in range(2):
                    last = mm(ps[4 + e % 2][:, 0:SL], B("ew2")[:, (2 * e + c) * D:(2 * e + c + 1) * D],
                              hm[:, e % 2, c, :], start=c == 0, stop=c == 1)
                last.then_inc(e2_mm, 1)
            pe.wait_ge(e2_ev, NE)
            for c in range(2 * NB // 4):
                if c >= 4:
                    pe.wait_ge(ot_ev, c - 3)
                for n in range(4):
                    q = 4 * c + n
                    half = oT[:, q // 2, NE // 2 * (q % 2):NE // 2 * (q % 2 + 1), :]
                    last = tr(ps[c % 4][0:HC, n * D:(n + 1) * D], half.rearrange("p e j -> p (e j)"))
                last.then_inc(ot_tr, 1)
            pe.wait_ge(gt_ev, 2 * NB // 4)
            for b in range(NB):
                pe.wait_ge(ot_ev, b // 2 + 1)
                for n in range(2):
                    last = mm(ps[4 + b // BG][0:L, (b % BG) * D:(b % BG + 1) * D], gatedT[:, 2 * b + n, :],
                              otok[:, 2 * b + n, :], start=n == 0, stop=n == 1)
                last.then_inc(sc_mm, 1)
            if stage == 3:
                return
            to_features(z, norm_[4], 0, z_tr[2])
            pe.wait_ge(z_ev[2], G)
            pe.wait_ge(bf_s, 2)

            def fill(bank, i, col0):
                for n in range(2):
                    cols = slice(col0 + n * 128, col0 + (n + 1) * 128)
                    for m, (w, zz) in enumerate(((w_hi, z_hi), (w_hi, z_lo), (w_lo, z_hi))):
                        last = mm(bank[:, n * P2:(n + 1) * P2], w[:, cols], zz[:, bass.ds(i * P2, P2)],
                                  start=m == 0, stop=m == 2)
                return last

            def queries_keys(i, p):
                if p == 1:
                    pe.wait_ge(q4_ev, i * 4 + 2)
                    pe.wait_ge(k4_ev, i * 4 + 2)
                for n in range(2):
                    fill(ps[4 + n], i, (2 * p + n) * 256).then_inc(qk_mm, 1)

            def values(i):
                pe.wait_ge(q4_ev, i * 4 + 4)
                pe.wait_ge(k4_ev, i * 4 + 4)
                for n in range(2):
                    fill(ps[4 + n], i, 2 * J * DH + n * 256).then_inc(vv_mm, 1)

            def values_across(i):
                for p in range(2):
                    for hh in range(J):
                        last = tr(ps[6 + p][0:L, hh * DH:(hh + 1) * DH], col(vT, p * J + hh))
                    last.then_inc(vt_tr, 1)

            def scores(i, p):
                for q in range(2):
                    bank = ps[2 * p + q]
                    mm(bank[0:L, 0:4 * L], identb[:], negd[:].rearrange("p a l -> p (a l)"),
                       start=True, stop=False, skip_group_check=True)
                    for a in range(4):
                        hh = 4 * q + a
                        last = mm(bank[0:L, a * L:(a + 1) * L], col(qT, p * J + hh), col(kT, p * J + hh),
                                  start=False, stop=True, skip_group_check=True)
                    last.then_inc(sc4_mm, 1)

            def weights_across(i, p):
                b = i * 2 + p
                if isinstance(i, int) and i == 0:
                    pe.wait_ge(vm_ev, 2)
                elif p == 0:
                    pe.wait_ge(h_l2, b)
                for q in range(2):
                    pe.wait_ge(exp_s, b * 2 + q + 1)
                    for a in range(4):
                        last = tr(ps[6 + q][0:L, a * L:(a + 1) * L], col(es[p], 4 * q + a))
                    last.then_inc(es_tr, 1)

            def weighted(i, p):
                b = i * 2 + p
                if p == 0:
                    pe.wait_ge(vm_ev, b + 2)
                pe.wait_ge(es_evA, b + 1)
                pe.wait_ge(es_evD, b + 1)
                for hh in range(J):
                    last = mm(ps[2 * p][0:L, hh * DH:(hh + 1) * DH], col(esT[p], hh), vm[p][:, hh * DH:(hh + 1) * DH],
                              start=True, stop=True)
                last.then_inc(av_mm, 1)

            def output_across(i, p, ahead):
                b = i * 2 + p
                pe.wait_ge(o_nrm, b + 1)
                if ahead and p == 0:
                    pe.wait_ge(v4_ev, b * 2 + 8)
                for m in range(4):
                    last = tr(ps[4 + p][:, m * L:(m + 1) * L], oc[p][:, m * 128:(m + 1) * 128])
                last.then_inc(o_tr, 1)

            def attention(i, ahead):
                if ahead:
                    queries_keys(i + 1, 0)
                weights_across(i, 0)
                if ahead:
                    queries_keys(i + 1, 1)
                weighted(i, 0)
                weights_across(i, 1)
                if ahead:
                    values(i + 1)
                weighted(i, 1)
                output_across(i, 0, ahead)
                if ahead:
                    values_across(i + 1)
                    scores(i + 1, 0)
                output_across(i, 1, ahead)
                if ahead:
                    scores(i + 1, 1)
                for p in range(2):
                    b = i * 2 + p
                    pe.wait_ge(o_ev, b + 1)
                    if ahead and p == 0:
                        pe.wait_ge(vm_ev, b + 4)
                    for m in range(4):
                        last = mm(ps[6 + p][0:L, 0:D], oP[p].rearrange("p (t m) -> p m t", m=4)[:, m, :],
                                  B("wout")[:, m * D:(m + 1) * D], start=m == 0, stop=m == 3)
                    last.then_inc(pr_mm, 1)

            pe.wait_ge(w_split, 2)
            pe.wait_ge(z_lo_s, G)
            queries_keys(0, 0)
            queries_keys(0, 1)
            values(0)
            scores(0, 0)
            scores(0, 1)
            pe.wait_ge(v4_ev, 4)
            values_across(0)
            attention(0, True)
            with pe.Fori(1, NB // 2 - 1) as i:
                attention(i, True)
            attention(NB // 2 - 1, False)
            if stage == 4:
                return
            to_features(z, norm_[5], 0, z_tr[3])
            pe.wait_ge(z_ev[3], G)
            for b in range(NB):
                last = mm(ps[4][0:L, b * NE:(b + 1) * NE], col(zT, b), B("wr"), start=True, stop=True)
            last.then_inc(lg1_mm, 1)
            pe.wait_ge(ohb_s, 1)
            ohf = ohb[:].rearrange("p b e -> p (b e)")
            mm(ps[5][0:L, 0:NB * NE], trib[:], ohf, start=True, stop=False, skip_group_check=True)
            for s in range(1, NB):
                mm(ps[5][0:L, s * NE:NB * NE], onesb[:, 0:L], ohf[:, 0:(NB - s) * NE], start=False, stop=s == NB - 1,
                   skip_group_check=True)
            for b in range(NB):
                last = mm(ps[6][:, 0:NE], onesb[:], ohb[:, b, :], start=b == 0, stop=b == NB - 1)
            last.then_inc(rank_mm, 1)
            pe.wait_ge(slot_s, 1)
            for b in range(NB):
                last = mm(ps[6][:, 0:NT], slot_of[:, b, :], tile_of[:, b, :], start=b == 0, stop=b == NB - 1)
            last.then_inc(held_mm, 1)
            pe.wait_ge(fw_in, 32)
            pe.wait_ge(exp_i, 1)

            def up(t, q):
                p, t4 = q % 2, (t - q) // 4 if isinstance(t, int) else None
                pe.wait_ge(x_ld[q], 16 * (t4 + 1) if t4 is not None else (t - q + 4) * 4)
                tr(ps[p][:, 0:128], row[q][:, 0:D]).then_inc(x_tr, 1)
                e = pe.value_load(expert[0:1, bass.ds(t, 1)], min_val=0, max_val=NE - 1)
                pe.wait_ge(x_ev, t + 1)
                mm(ps[2 + p][:, 0:F1], xtT[p], fw1[:, bass.ds(e * F1, F1)], start=True, stop=True).then_inc(h_mm, 1)

            def down(t, q, first):
                p = q % 2
                e = pe.value_load(expert[0:1, bass.ds(t, 1)], min_val=0, max_val=NE - 1)
                pe.wait_ge(hb_s, t + 1)
                for c in range(4):
                    last = tr(ps[4 + p][:, c * 128:(c + 1) * 128], hb[p][:, c * 128:(c + 1) * 128])
                last.then_inc(hb_tr, 1)
                return e

            def out(t, q, first, e):
                p = q % 2
                pe.wait_ge(hb_ev, t + 1)
                if not first:
                    pe.wait_ge(o_s, t - 1)
                for c in range(4):
                    last = mm(ps[6 + p][:, 0:D], hbT[p][:, c * 128:(c + 1) * 128],
                              fw2[:, bass.ds(e * F1 + c * D, D)], start=c == 0, stop=c == 3)
                last.then_inc(o_mm, 1)

            def step(t, q, ahead=True):
                first = isinstance(t, int) and t < 2
                e = down(t, q, first)
                if ahead:
                    up(t + 1, (q + 1) % 4)
                out(t, q, first, e)

            up(0, 0)
            for t in range(4):
                step(t, t)
            with pe.Fori(4, NT_LOOP, 4) as t:
                for q in range(4):
                    step(t + q, q)
            for t in range(NT_LOOP, NT):
                step(t, t % 4, ahead=t < NT - 1)

        @block.scalar
        def _(act):
            fn = nc.scalar.activation

            def evacuate(banks, dst, sem_in, sem_out):
                for g in range(G):
                    act.wait_ge(sem_in, g + 1)
                    fn(dst[:, GL * g:GL * g + GL], ps[banks + g][:, 0:GL], ACT.Copy).then_inc(sem_out, 1)

            act.wait_ge(tokz, 1)
            act.wait_ge(tau_e, 1)
            fn(tk[:, 1, :], ps[4][:, 0:NB], ACT.Exp, bias=tk[:, 0, 0:1], scale=-0.1).then_inc(tau_e, 1)
            for g in range(G):
                act.wait_ge(y_tr, g + 1)
                fn(grp(h, g).rearrange("p b d -> p (b d)"), ps[g][0:L, :], ACT.Copy).then_inc(h_in, 1)
            if stage > 1:
                evacuate(4, zT, z_tr[0], z_ev[0])
                act.wait_ge(pads, 1)
                for g in range(G):
                    for (mm_s, bank, name, dst, ev) in ((q_mm, g, "bq", 0, q_ev), (k_mm, 4 + g, "bk", 1, k_ev)):
                        act.wait_ge(mm_s, g + 1)
                        fn(grp(pad[dst], g)[:, :, 2:], ps[bank][:, 0:GL].rearrange("p (b l) -> p b l", b=BG),
                           ACT.Identity, bias=A(name)).then_inc(ev, 1)
                for g in range(G):
                    act.wait_ge(v_mm, g + 1)
                    fn(grp(pad[2], g)[:, :, 2:], ps[g][:, 0:GL].rearrange("p (b l) -> p b l", b=BG),
                       ACT.Identity, bias=A("bv")).then_inc(v_ev, 1)
                for g in range(G):
                    for (min_s, t, ex_s) in ((q_min, elu_t[0], q_exp), (k_min, elu_t[1], k_exp)):
                        act.wait_ge(min_s, g + 1)
                        fn(t[:, GL * g:GL * g + GL], t[:, GL * g:GL * g + GL], ACT.Exp).then_inc(ex_s, 1)
                for g in range(G):
                    act.wait_ge(k_tr, g + 1)
                    fn(grp(ktok, g).rearrange("p b d -> p (b d)"), ps[4 + g][0:L, :], ACT.Copy).then_inc(k_tok, 1)
                evacuate(4, attT, att_tr, att_ev)
                for g in range(G):
                    act.wait_ge(n1_tr, g + 1)
                    fn(x1T[:, GL * g:GL * g + GL], ps[4 + g][:, 0:GL], ACT.Identity, bias=A("ln1_b"), scale=A("ln1_g"))\
                        .then_inc(x1_ev, 1)
                for g in range(G):
                    for c in range(2):
                        act.wait_ge(w1_mm, 2 * g + c + 1)
                        fn(gel[:, c, GL * g:GL * g + GL], ps[4 * c + g][:, 0:GL], ACT.Gelu, bias=A("b1")[:, c:c + 1])\
                            .then_inc(gel_ev, 1)
            if stage > 2:
                evacuate(0, zT, z_tr[1], z_ev[1])
                act.wait_ge(ga_sub, 1)
                fn(sm[:, 1], sm[:, 0], ACT.Exp).then_inc(ga_exp, 1)
                fn(ksc[:, 0:1], A("temp"), ACT.Exp).then_inc(scale_e, 1)
                for n in range(NB // 2):
                    act.wait_ge(ga_mm, n + 1)
                    fn(ex[:, :, 2 * n:2 * n + 2, :].rearrange("p e b j -> p b e j"),
                       ps[n][:, 0:2 * NE * CAP].rearrange("p (b e j) -> p b e j", b=2, e=NE), ACT.Copy).then_inc(ex_ev, 1)
                for e in range(NE):
                    if e >= 2:
                        act.wait_ge(e2_mm, e - 1)
                    for c in range(2):
                        act.wait_ge(e1_mm, 2 * e + c + 1)
                        fn(hm[:, e % 2, c, :], ps[2 * (e % 2) + c][:, 0:SL], ACT.Gelu,
                           bias=B("eb1")[:, 2 * e + c:2 * e + c + 1]).then_inc(e1_ev, 1)
                for c in range(2 * NB // 4):
                    act.wait_ge(ot_tr, c + 1)
                    fn(otok[:, 4 * c:4 * c + 4, :].rearrange("p q d -> p (q d)"), ps[c % 4][0:HC, :], ACT.Copy)\
                        .then_inc(ot_ev, 1)
            if stage > 3:
                for g in range(G):
                    act.wait_ge(z_tr[2], g + 1)
                    fn(z_hi[:, GL * g:GL * g + GL], ps[g][:, 0:GL], ACT.Copy).then_inc(z_ev[2], 1)
                act.wait_ge(scale_s, 1)

                def queries(i, p):
                    for q in range(2):
                        act.wait_ge(qk_mm, (i * 2 + p) * 2 + q + 1)
                        fn(chunks(qT, 2 * p + q), ps[4 + q][0:DH, 0:2 * P2].rearrange("p (j b t) -> p j b t", j=2, b=2),
                           ACT.Copy).then_inc(q4_ev, 1)

                def values(i):
                    for n in range(2):
                        act.wait_ge(vv_mm, i * 2 + n + 1)
                        for q in range(2):
                            fn(vT.rearrange("p (b t j q) -> p j b t q", b=2, j=4, q=2)[:, 2 * n:2 * n + 2, :, :, q],
                               ps[4 + n][q * DH:(q + 1) * DH, 0:2 * P2].rearrange("p (j b t) -> p j b t", j=2, b=2),
                               ACT.Copy).then_inc(v4_ev, 1)

                def values_rows():
                    for p in range(2):
                        fn(vm[p], ps[6 + p][0:L, :], ACT.Copy).then_inc(vm_ev, 1)

                def exponents(i, p, quads):
                    for q in quads:
                        act.wait_ge(max_s, (i * 2 + p) * 2 + q + 1)
                        for a in range(4):
                            hh = 4 * q + a
                            last = fn(col(es[p], hh), ps[2 * p + q][0:L, a * L:(a + 1) * L], ACT.Exp,
                                      bias=mx[:, p, 1, hh:hh + 1], scale=ksc[0:L, 0:1],
                                      accum_out=sums[:, p, 0, hh:hh + 1])
                        last.then_inc(exp_s, 1)

                def weights_across(i, p):
                    act.wait_ge(es_tr, (i * 2 + p) * 2 + 1)
                    fn(esT[p][:, 0:4 * L], ps[6][0:L, 0:4 * L], ACT.Copy).then_inc(es_evA, 1)

                def attention(i, ahead):
                    exponents(i, 0, (0, 1))
                    exponents(i, 1, (0,))
                    if ahead:
                        queries(i + 1, 0)
                    exponents(i, 1, (1,))
                    weights_across(i, 0)
                    if ahead:
                        queries(i + 1, 1)
                    weights_across(i, 1)
                    if ahead:
                        values(i + 1)
                        act.wait_ge(vt_tr, i * 2 + 4)
                        values_rows()

                queries(0, 0)
                queries(0, 1)
                values(0)
                act.wait_ge(vt_tr, 2)
                values_rows()
                attention(0, True)
                with act.Fori(1, NB // 2 - 1) as i:
                    attention(i, True)
                attention(NB // 2 - 1, False)
            if stage > 4:
                evacuate(0, zT, z_tr[3], z_ev[3])

                def up(t, q):
                    act.wait_ge(x_tr, t + 1)
                    fn(xtT[q % 2], ps[q % 2][:, 0:128], ACT.Copy).then_inc(x_ev, 1)

                def down(t, q):
                    act.wait_ge(hb_tr, t + 1)
                    fn(hbT[q % 2], ps[4 + q % 2][:, :], ACT.Relu).then_inc(hb_ev, 1)

                def step(t, q, ahead=True):
                    down(t, q)
                    if ahead:
                        up(t + 1, (q + 1) % 4)

                up(0, 0)
                for t in range(4):
                    step(t, t)
                with act.Fori(4, NT_LOOP, 4) as t:
                    for q in range(4):
                        step(t + q, q)
                for t in range(NT_LOOP, NT):
                    step(t, t % 4, ahead=t < NT - 1)

        @block.gpsimd
        def _(pool):
            count = [0]

            def own(ins):
                count[0] += 1
                ins.then_inc(pool_n, 1)
                pool.wait_ge(pool_n, count[0])

            def rsqrt(n):
                for g in range(G):
                    pool.wait_ge(stats[n], g + 1)
                    own(nc.gpsimd.tensor_scalar(rv[:, BG * g:BG * g + BG], mv[:, BG * g:BG * g + BG, 1], LN_EPS, None, ALU.add))
                    nc.gpsimd.tensor_tensor(rs[:, BG * g:BG * g + BG], rv[:, BG * g:BG * g + BG], C("mhalf", L), ALU.pow)\
                        .then_inc(rstd[n], 1)

            for i in range(3):
                last = nc.gpsimd.memset(pad[i][:, :, 0:2], 0.0)
            last.then_inc(pads, 1)
            pool.wait_ge(cc_in, 16)
            pool.wait_ge(wa_in, 16)
            if stage > 1:
                pool.wait_ge(wqkv_in, 16)
                nc.gpsimd.tensor_copy(w_hi[:], wqkv).then_inc(w_split, 1)
                pool.wait_ge(w_split, 1)
                nc.gpsimd.tensor_tensor(w_lo[:], wqkv, w_hi[:].bitcast(F32), ALU.subtract).then_inc(w_split, 1)
                rsqrt(0)
                for g in range(G):
                    pool.wait_ge(norm_[0], g + 1)
                    nc.gpsimd.tensor_tensor(grp(zb, g), grp(z, g), A("bo")[0:L, None, :].to_broadcast([L, BG, D]),
                                            ALU.add).then_inc(zb_s, 1)
                u = region(3, GL).rearrange("p (b l) -> p b l", b=BG)
                for g in range(G):
                    pool.wait_ge(v_ev, g + 1)
                    src, dst = grp(pad[2], g), col(cv[2], g, GL).rearrange("p (b l) -> p b l", b=BG)
                    w = A("vcw")
                    own(nc.gpsimd.tensor_scalar(dst, src[:, :, 0:L], w[:, 0:1], A("vcb"), ALU.mult, ALU.add))
                    for j in (1, 2):
                        own(nc.gpsimd.tensor_scalar(u, src[:, :, j:j + L], w[:, j:j + 1], None, ALU.mult))
                        last = nc.gpsimd.tensor_tensor(dst, dst, u, ALU.add)
                        if j == 1:
                            own(last)
                    last.then_inc(v_cv, 1)
                    pool.wait_ge(v_cv, g + 1)
                for g in range(G):
                    nc.gpsimd.tensor_tensor(grp(h, g), grp(h, g), A("ln2_b")[0:L, None, :].to_broadcast([L, BG, D]),
                                            ALU.add).then_inc(hpre, 1)
                rsqrt(1)
                for g in range(G):
                    pool.wait_ge(gel_ev, 2 * g + 2)
                    nc.gpsimd.tensor_tensor(hid[:, :, GL * g:GL * g + GL], gel[:, :, GL * g:GL * g + GL],
                                            gel[:, :, GL * g:GL * g + GL], ALU.mult).then_inc(hid_s, 1)
                rsqrt(2)
            if stage > 2:
                rsqrt(3)
                for g in range(G):
                    pool.wait_ge(oneh, g + 1)
                    nc.gpsimd.tensor_tensor(grp(gated, g).rearrange("p b e j -> p (b e) j"),
                                            grp(onehot, g).rearrange("p b e j -> p (b e) j"),
                                            grp(gate, g).rearrange("p b e -> p (b e)")[:, :, None]
                                            .to_broadcast([L, BG * NE, CAP]), ALU.mult).then_inc(gat_s, 1)
            if stage > 3:
                rsqrt(4)
            if stage > 4:
                rsqrt(5)
                pool.wait_ge(rows_st, 64)
                pool.wait_ge(take_s, 1)

                def gather(t):
                    if t >= 4:
                        pool.wait_ge(o_s, t - 3)
                    nc.gpsimd.indirect_dma_start(row[t % 4], None, rows_d,
                                                 bass.IndirectOffsetOnAxis(ap=take[:, t:t + 1], axis=0))\
                        .then_inc(x_ld[t % 4], 16)

                for t in range(4):
                    gather(t)
                pool.wait_ge(give_s, 1)
                for t in range(NT):
                    pool.wait_ge(o_s, t + 1)
                    nc.gpsimd.indirect_dma_start(out_d, bass.IndirectOffsetOnAxis(ap=give[:, t:t + 1], axis=0),
                                                 ot[t % 4], None, bounds_check=T - 1, oob_is_err=False)\
                        .then_inc(y_st[t % 4], 16)
                    if t + 4 < NT:
                        gather(t + 4)

        @block.vector
        def _(dve):
            V = nc.vector
            count = [0]

            def own(ins):
                count[0] += 1
                ins.then_inc(dve_n, 1)
                dve.wait_ge(dve_n, count[0])

            def layer_stats(n, src_of, wait, every=True):
                for g in range(G):
                    if wait is not None:
                        dve.wait_ge(wait, g + 1)
                    for i in range(BG):
                        last = V.bn_stats(st[:, BG * g + i, :], src_of(BG * g + i))
                    own(last)
                    for i in range(BG):
                        last = V.bn_aggr(mv[:, BG * g + i, :], st[:, BG * g + i, :])
                    last.then_inc(stats[n], 1)

            def layer_norm(n, src, dst):
                for g in range(G):
                    dve.wait_ge(stats[n], g + 1)
                    dve.wait_ge(rstd[n], g + 1)
                    for b in range(BG * g, BG * g + BG):
                        last = V.tensor_scalar(dst[:, b, :], src[:, b, :], mv[:, b, 0:1], rs[:, b:b + 1],
                                               ALU.subtract, ALU.mult)
                    last.then_inc(norm_[n], 1)

            dve.wait_ge(wa_in, 16)
            V.tensor_scalar(tk[:, 0, 0:1], A("tok_b"), -0.1, 3.0, ALU.mult, ALU.add).then_inc(tau_e, 1)
            own(V.memset(filt[:, :, 0:1], 0.0))
            dve.wait_ge(tau_e, 2)
            own(V.tensor_scalar(tk[:, 2, :], tk[:, 1, :], 1.0, None, ALU.add))
            own(V.reciprocal(tau, tk[:, 2, :]))
            own(V.tensor_scalar(tk[:, 5, :], tau, 1.0, None, ALU.add))
            own(V.tensor_tensor(tk[:, 4, :], tau, tau, ALU.mult))
            n = 2
            while n < K:
                own(V.scalar_tensor_tensor(tk[:, 5, :], tk[:, 4, :], 1.0, tk[:, 5, :], ALU.add, ALU.mult))
                own(V.tensor_tensor(tk[:, 4, :], tk[:, 4, :], tk[:, 4, :], ALU.mult))
                n *= 2
            assert n == K
            own(V.reciprocal(norm, tk[:, 5, :]))
            own(V.tensor_scalar(npow, tk[:, 4, :], -1.0, None, ALU.mult))
            for g in range(G):
                dve.wait_ge(x_in[g], 16)
                bs = range(BG * g, BG * g + BG)
                for b in bs:
                    last = V.tensor_tensor_scan(filt[:, b, 1:], tau[:, b:b + 1].to_broadcast([128, LIN]), xT[:, b, :],
                                                0.0, ALU.mult, ALU.add)
                own(last)
                for b in bs:
                    last = V.scalar_tensor_tensor(col(yT, b), filt[:, b, 0:L], npow[:, b:b + 1], filt[:, b, K:K + L],
                                                  ALU.mult, ALU.add)
                own(last)
                for b in bs:
                    last = V.tensor_scalar(col(yT, b), col(yT, b), norm[:, b:b + 1], None, ALU.mult)
                last.then_inc(filt_y, 1)
            if stage > 1:
                layer_stats(0, lambda b: h[:, b, :], h_in)
                layer_norm(0, h, z)
                for g in range(G):
                    for (src, t, dst, ev, w, cb, mn) in ((pad[0], elu_t[0], cv[0], q_ev, "qcw", "qcb", q_min),
                                                        (pad[1], elu_t[1], cv[1], k_ev, "kcw", "kcb", k_min)):
                        dve.wait_ge(ev, g + 1)
                        s, d = grp(src, g), col(dst, g, GL)
                        d3 = d.rearrange("p (b l) -> p b l", b=BG)
                        own(V.tensor_scalar(d3, s[:, :, 0:L], A(w)[:, 0:1], A(cb), ALU.mult, ALU.add))
                        for j in (1, 2):
                            own(V.scalar_tensor_tensor(d3, s[:, :, j:j + L], A(w)[:, j:j + 1], d3, ALU.mult, ALU.add))
                        V.tensor_scalar(col(t, g, GL), d, 0.0, None, ALU.min).then_inc(mn, 1)
                for g in range(G):
                    for (t, dst, xs, el) in ((elu_t[1], cv[1], k_exp, k_elu), (elu_t[0], cv[0], q_exp, q_elu)):
                        dve.wait_ge(xs, g + 1)
                        d = col(dst, g, GL)
                        V.scalar_tensor_tensor(d, d, 0.0, col(t, g, GL), ALU.max, ALU.add).then_inc(el, 1)
                dve.wait_ge(w_split, 2)
                for g in range(G):
                    dve.wait_ge(v_tr, g + 1)
                    V.tensor_copy(grp(vtok, g).rearrange("p b d -> p (b d)"), ps[g][0:L, :]).then_inc(v_tok, 1)
                for g in range(G):
                    dve.wait_ge(kv_mm, g + 1)
                    own(V.tensor_scalar(ks[:, BG * g:BG * g + BG], ps[g][:, 0:BG], EPS, None, ALU.add))
                    V.tensor_tensor(grp(kv, g)[:, :, 0:D], ps[4 + g][:, :].rearrange("p (b d) -> p b d", b=BG),
                                    C("block")[:, None, :].to_broadcast([128, BG, D]), ALU.mult)
                    V.tensor_tensor(grp(kv, g)[:, :, D:], C("block8")[:, None, :].to_broadcast([128, BG, H0]),
                                    ks[:, BG * g:BG * g + BG, None].to_broadcast([128, BG, H0]), ALU.mult).then_inc(kv_ev, 1)
                for g in range(G):
                    dve.wait_ge(nd_mm, g + 1)
                    for n in range(2):
                        b = BG * g + 2 * n
                        nd = ps[(4, 0)[n] + g][0:L, 0:2 * (D + H0)].rearrange("p (b d) -> p b d", b=2)
                        own(V.reciprocal(rd[:, b:b + 2, :], nd[:, :, D:]))
                        last = V.tensor_tensor(att[:, b:b + 2, :].rearrange("p b (h d) -> p b h d", d=DK),
                                               nd[:, :, 0:D].rearrange("p b (h d) -> p b h d", d=DK),
                                               rd[:, b:b + 2, :, None].to_broadcast([L, 2, H0, DK]), ALU.mult)
                    last.then_inc(att_n, 1)
                for g in range(G):
                    dve.wait_ge(proj, g + 1)
                    dve.wait_ge(zb_s, g + 1)
                    V.tensor_tensor(grp(r1, g), ps[g][0:L, :].rearrange("p (b d) -> p b d", b=BG), grp(zb, g), ALU.add)\
                        .then_inc(r1_s, 1)
                layer_stats(1, lambda b: r1[:, b, :], r1_s)
                layer_norm(1, r1, r1)
                for g in range(G):
                    dve.wait_ge(w2_mm, g + 1)
                    V.scalar_tensor_tensor(col(y2T, g, GL), ps[g][:, 0:GL], A("b2"), col(x1T, g, GL), ALU.add, ALU.add)\
                        .then_inc(y2_s, 1)
                pb = lambda b: ps[4 + b // BG][0:L, (b % BG) * D:(b % BG + 1) * D]
                layer_stats(2, pb, y2_tr)
                for g in range(G):
                    dve.wait_ge(stats[2], g + 1)
                    dve.wait_ge(rstd[2], g + 1)
                    dve.wait_ge(hpre, g + 1)
                    for b in range(BG * g, BG * g + BG):
                        last = V.scalar_tensor_tensor(r1[:, b, :], pb(b), mv[:, b, 0:1], A("ln2_g")[0:L, :],
                                                      ALU.subtract, ALU.mult)
                    own(last)
                    for b in range(BG * g, BG * g + BG):
                        last = V.scalar_tensor_tensor(h[:, b, :], r1[:, b, :], rs[:, b:b + 1], h[:, b, :],
                                                      ALU.mult, ALU.add)
                    last.then_inc(h_l0, 1)
            if stage > 2:
                layer_stats(3, lambda b: h[:, b, :], h_l0)
                layer_norm(3, h, z)
                lg = ps[4][0:L, 0:NB * NE].rearrange("p (b e) -> p b e", b=NB)
                wide = lambda r: r[:, :, None].to_broadcast([L, NB, NE])
                dve.wait_ge(lg0_mm, 1)
                own(V.tensor_reduce(red[:, 0], lg, AX, ALU.max))
                V.tensor_tensor(sm[:, 0], lg, wide(red[:, 0]), ALU.subtract).then_inc(ga_sub, 1)
                dve.wait_ge(ga_exp, 1)
                own(V.tensor_reduce(red[:, 1], sm[:, 1], AX, ALU.add))
                own(V.reciprocal(red[:, 2], red[:, 1]))
                V.tensor_tensor(gate[:], sm[:, 1], wide(red[:, 2]), ALU.mult).then_inc(gate_s, 1)
                dve.wait_ge(st_tr, 1)
                own(V.tensor_copy(choice[:, 0, :], ps[5][:, 0:L]))
                for n in range(0, CAP, 8):
                    own(V.max(top8[:], choice[:, 0, :]))
                    if CAP - n < 8:
                        own(V.memset(top8[:, CAP - n:8], -1.0))
                    own(V.match_replace(choice[:, 0, :], top8[:], choice[:, 0, :], -1.0))
                own(V.tensor_scalar(choice[:, 1, :], choice[:, 0, :], -1.0, None, ALU.is_equal))
                own(V.tensor_tensor_scan(choice[:, 2, :], C("ones")[:, 0:L], choice[:, 1, :], 0.0, ALU.mult, ALU.add))
                own(V.tensor_tensor(choice[:, 3, :], choice[:, 2, :], choice[:, 1, :], ALU.mult))
                V.tensor_scalar(choice[:, 3, :], choice[:, 3, :], -1.0, None, ALU.add).then_inc(pos_s, 1)
                dve.wait_ge(pos_tr, 1)
                own(V.tensor_copy(posl[:], ps[6][0:L, 0:128]))
                nbe = BG * NE
                for g in range(G):
                    V.tensor_tensor(grp(onehot, g).rearrange("p b e j -> p (b e) j"),
                                    posl[:, g * nbe:(g + 1) * nbe, None].to_broadcast([L, nbe, CAP]),
                                    C("slot", L)[:, None, :].to_broadcast([L, nbe, CAP]), ALU.is_equal).then_inc(oneh, 1)
                for e in range(NE):
                    dve.wait_ge(gt_tr, e + 1)
                    V.tensor_copy(gatedT[:, 4 * e:4 * e + 4, :].rearrange("p q l -> p (q l)"), ps[6 + e % 2][0:HC, 0:4 * L])\
                        .then_inc(gt_ev, 1)
                    dve.wait_ge(e2_mm, e + 1)
                    V.tensor_scalar(oT[:, :, e, :], ps[4 + e % 2][:, 0:SL].rearrange("p (b j) -> p b j", b=NB),
                                    B("eb2")[:, e:e + 1], None, ALU.add).then_inc(e2_ev, 1)
                for g in range(G):
                    dve.wait_ge(sc_mm, BG * g + BG)
                    V.tensor_tensor(grp(h, g), ps[4 + g][0:L, :].rearrange("p (b d) -> p b d", b=BG), grp(h, g), ALU.add)\
                        .then_inc(h_l1, 1)
            if stage > 3:
                layer_stats(4, lambda b: h[:, b, :], h_l1)
                layer_norm(4, h, z)
                for g in range(G):
                    dve.wait_ge(z_ev[2], g + 1)
                    V.tensor_tensor(col(z_lo, g, GL), ps[g][:, 0:GL], col(z_hi, g, GL).bitcast(F32), ALU.subtract)\
                        .then_inc(z_lo_s, 1)
                V.tensor_copy(identb[:], C("ident", L)[:, 0:L]).then_inc(bf_s, 1)
                V.tensor_scalar(negd[:], C("ident", L)[:, None, 0:L].to_broadcast([L, 4, L]), BIG, None, ALU.mult)\
                    .then_inc(bf_s, 1)
                dve.wait_ge(scale_e, 1)
                V.tensor_scalar(ksc[:, 1:2], ksc[:, 0:1], -1.0, None, ALU.mult).then_inc(scale_s, 1)
                dve.wait_ge(scale_s, 1)
                base = count[0] + 4

                def keys(i, p):
                    for q in range(2):
                        dve.wait_ge(qk_mm, (i * 2 + p) * 2 + q + 1)
                        V.tensor_copy(chunks(kT, 2 * p + q),
                                      ps[4 + q][DH:128, 0:2 * P2].rearrange("p (j b t) -> p j b t", j=2, b=2))\
                            .then_inc(k4_ev, 1)

                def attention(i, ahead):
                    done = [0]

                    def own2(ins):
                        done[0] += 1
                        ins.then_inc(dve_n, 1)
                        dve.wait_ge(dve_n, i * 8 + base + done[0])

                    def maxima(i, p, own_=own2):
                        for q in range(2):
                            dve.wait_ge(sc4_mm, (i * 2 + p) * 2 + q + 1)
                            own_(V.tensor_reduce(mx[:, p, 0, 4 * q:4 * q + 4],
                                                 ps[2 * p + q][0:L, 0:4 * L].rearrange("p (a l) -> p a l", a=4), AX, ALU.max))
                            V.tensor_scalar(mx[:, p, 1, 4 * q:4 * q + 4], mx[:, p, 0, 4 * q:4 * q + 4], ksc[0:L, 1:2], None,
                                            ALU.mult).then_inc(max_s, 1)

                    def output(p):
                        dve.wait_ge(o_tr, i * 2 + p + 1)
                        for r in range(2):
                            for n in range(2):
                                cnt_n = (L - n + 1) // 2
                                par, at = (r + n) % 2, (r * L + n) // 2
                                src = ps[4 + p][r * DH:(r + 1) * DH, 0:4 * L].rearrange("p (m n) -> p m n", m=4)
                                dst = oP[p][par * DH:(par + 1) * DH, :].rearrange("p (m n) -> p m n", m=4)
                                last = V.tensor_copy(dst[:, :, at:at + cnt_n], src[:, :, bass.ds(n, cnt_n, step=2)])
                        last.then_inc(o_ev, 1)

                    if i is None:
                        maxima(0, 0, own)
                        maxima(0, 1, own)
                        return
                    for p in range(2):
                        b = i * 2 + p
                        if ahead and p == 0:
                            keys(i + 1, 0)
                        dve.wait_ge(es_tr, b * 2 + 2)
                        V.tensor_copy(esT[p][:, 4 * L:], ps[7][0:L, 0:4 * L]).then_inc(es_evD, 1)
                        if ahead and p == 0:
                            keys(i + 1, 1)
                        dve.wait_ge(exp_s, b * 2 + 2)
                        own2(V.reciprocal(sums[:, p, 1, :], sums[:, p, 0, :]))
                        dve.wait_ge(av_mm, b + 1)
                        V.tensor_tensor(oc[p].rearrange("p (h d) -> p h d", h=J),
                                        ps[2 * p][0:L, :].rearrange("p (h d) -> p h d", h=J),
                                        sums[:, p, 1, :, None].to_broadcast([L, J, DH]), ALU.mult).then_inc(o_nrm, 1)
                    output(0)
                    if ahead:
                        maxima(i + 1, 0)
                    output(1)
                    if ahead:
                        maxima(i + 1, 1)
                    for p in range(2):
                        b = i * 2 + p
                        dve.wait_ge(pr_mm, b + 1)
                        hb_ = h[:, bass.ds(b, 1), :].rearrange("p b d -> p (b d)")
                        own2(V.tensor_tensor(hb_, ps[6 + p][0:L, 0:D], hb_, ALU.add))
                        V.tensor_tensor(hb_, hb_, B("bout")[0:L, :], ALU.add).then_inc(h_l2, 1)
                    assert done[0] == (8 if ahead else 4)

                keys(0, 0)
                keys(0, 1)
                attention(None, True)
                attention(0, True)
                with dve.Fori(1, NB // 2 - 1) as i:
                    attention(i, True)
                attention(NB // 2 - 1, False)
                count[0] += 8 * NB // 2 - 4
            if stage > 4:
                dve.wait_ge(h_l2, NB)
                layer_stats(5, lambda b: h[:, b, :], None)
                layer_norm(5, h, z)
                own(V.tensor_copy(trib[:], C("tri", L)[:, 0:L]))
                own(V.tensor_copy(onesb[:], C("ones", L)))
                over_b = lambda c: c[:, None, :].to_broadcast([L, NB, NE])
                dve.wait_ge(lg1_mm, 1)
                own(V.tensor_tensor(sm[:, 0], lg, over_b(B("br")[0:L, :]), ALU.add))
                own(V.tensor_reduce(red[:, 0], sm[:, 0], AX, ALU.max))
                own(V.tensor_tensor(sm[:, 1], sm[:, 0], wide(red[:, 0]), ALU.is_equal))
                own(V.scalar_tensor_tensor(sm[:, 2], sm[:, 1], -float(NE), over_b(C("e8", L)), ALU.mult, ALU.add))
                own(V.tensor_reduce(red[:, 1], sm[:, 2], AX, ALU.min))
                own(V.tensor_tensor(sm[:, 3], over_b(C("e8m", L)), wide(red[:, 1]), ALU.is_equal))
                V.tensor_copy(ohb[:], sm[:, 3]).then_inc(ohb_s, 1)
                dve.wait_ge(rank_mm, 1)
                own(V.tensor_copy(cnt[:, 0, :], ps[6][:, 0:NE]))
                own(V.tensor_tensor(cmp1[:], cnt[:, 0, :, None].to_broadcast([128, NE, NB]),
                                    C("thr")[:, None, :].to_broadcast([128, NE, NB]), ALU.is_gt))
                own(V.tensor_reduce(cnt[:, 1, :], cmp1[:], AX, ALU.add))
                own(V.tensor_tensor_scan(cnt[:, 2, :], C("ones")[:, 0:NE], cnt[:, 1, :], 0.0, ALU.mult, ALU.add))
                own(V.tensor_tensor(cnt[:, 3, :], cnt[:, 2, :], cnt[:, 1, :], ALU.subtract))
                own(V.tensor_scalar(cnt[:, 3, :], cnt[:, 3, :], 128.0, None, ALU.mult))
                own(V.tensor_tensor(sm[:, 0], ps[5][0:L, 0:NB * NE].rearrange("p (b e) -> p b e", b=NB),
                                    over_b(cnt[0:L, 3, :]), ALU.add))
                own(V.tensor_tensor(sm[:, 1], sm[:, 0], sm[:, 3], ALU.mult))
                own(V.tensor_reduce(red[:, 2], sm[:, 1], AX, ALU.add))
                own(V.tensor_tensor(reach, red[:, 2, :, None].to_broadcast([L, NB, NT + 1]),
                                    C("first", L)[:, None, :].to_broadcast([L, NB, NT + 1]), ALU.is_ge))
                own(V.tensor_reduce(red[:, 3], reach, AX, ALU.add))
                own(V.scalar_tensor_tensor(red[:, 1], red[:, 3], -128.0, red[:, 2], ALU.mult, ALU.add))
                V.tensor_tensor(slot_of, red[:, 1, :, None].to_broadcast([L, NB, 128]),
                                C("r128", L)[:, None, :].to_broadcast([L, NB, 128]), ALU.is_equal)
                own(V.tensor_tensor(tile_of, reach[:, :, 0:NT], reach[:, :, 1:], ALU.subtract))
                V.tensor_tensor(tile_of, tile_of, C("token", L)[:, :, None].to_broadcast([L, NB, NT]), ALU.mult)\
                    .then_inc(slot_s, 1)
                own(V.tensor_tensor(cmp2[:], cnt[:, 2, None, :].to_broadcast([128, NT, NE]),
                                    C("tile")[:, :, None].to_broadcast([128, NT, NE]), ALU.is_le))
                own(V.tensor_reduce(tl[:, 0, :], cmp2[:], AX, ALU.add))
                V.tensor_scalar(expert[:, 0:NT], tl[:, 0, :], float(NE - 1), None, ALU.min).then_inc(exp_i, 1)
                dve.wait_ge(exp_i, 1)
                dve.wait_ge(fb_in, 16)

                dve.wait_ge(held_mm, 1)
                own(V.tensor_copy(held[:, 0, :], ps[6][:, 0:NT]))
                own(V.tensor_scalar(held[:, 1, :], held[:, 0, :], -1.0, None, ALU.add))
                V.tensor_scalar(take[:], held[:, 1, :], 0.0, None, ALU.max).then_inc(take_s, 1)
                own(V.tensor_scalar(held[:, 2, :], held[:, 0, :], 0.0, None, ALU.is_equal))
                own(V.scalar_tensor_tensor(held[:, 3, :], held[:, 2, :], C("none"), held[:, 1, :], ALU.mult, ALU.add))
                V.tensor_copy(give[:], held[:, 3, :]).then_inc(give_s, 1)

                def up(t, q):
                    e = dve.value_load(expert[0:1, bass.ds(t, 1)], min_val=0, max_val=NE - 1)
                    dve.wait_ge(h_mm, t + 1)
                    V.tensor_tensor(hb[q % 2], ps[2 + q % 2][:, :], fb[:, bass.ds(e * F1, F1)], ALU.add).then_inc(hb_s, 1)

                def out(t, q, first):
                    e = dve.value_load(expert[0:1, bass.ds(t, 1)], min_val=0, max_val=NE - 1)
                    dve.wait_ge(o_mm, t + 1)
                    if not first:
                        dve.wait_ge(y_st[q], (t - q) * 4)
                    own3(V.tensor_tensor(ot[q], ps[6 + q % 2][:, 0:D], fb[:, bass.ds(NE * F1 + e * D, D)], ALU.add), t)
                    V.tensor_tensor(ot[q], ot[q], row[q][:, D:], ALU.add).then_inc(o_s, 1)

                def own3(ins, t):
                    ins.then_inc(dve_n, 1)
                    dve.wait_ge(dve_n, t + 1 + count[0])

                def step(t, q, ahead=True):
                    if ahead:
                        up(t + 1, (q + 1) % 4)
                    out(t, q, isinstance(t, int) and t < 4)

                up(0, 0)
                for t in range(4):
                    step(t, t)
                with dve.Fori(4, NT_LOOP, 4) as t:
                    for q in range(4):
                        step(t + q, q)
                for t in range(NT_LOOP, NT):
                    step(t, t % 4, ahead=t < NT - 1)


def kernel(**inputs):
    import numpy as _np
    import concourse.bacc as _bacc
    from concourse import mybir as _mybir
    from concourse.bass_utils import run_bass_kernel_spmd as _run

    a = {k: _np.asarray(v) for k, v in inputs.items()}

    def column(v):
        return v.reshape(-1, 1)

    def rows(v):
        return _np.broadcast_to(v.reshape(1, -1), (128, v.size))

    p0 = "L0_attn_"
    part_a = {
        "tok": a["L0_tok_W"].T, "tok_b": column(a["L0_tok_b"]),
        "w1": a[p0 + "w1"].T, "w2": a[p0 + "w2"].T.reshape(2, D, D).transpose(1, 0, 2).reshape(D, 2 * D),
        "b1": a[p0 + "b1"].reshape(2, D).T, "b2": column(a[p0 + "b2"]),
        "ln1_g": column(a[p0 + "ln1_g"]), "ln1_b": column(a[p0 + "ln1_b"]),
        "temp": _np.broadcast_to(a["L1_attn_temperature"].reshape(1, 1), (128, 1)),
        "bo": rows(a[p0 + "bo"]), "ln2_g": rows(a[p0 + "ln2_g"]), "ln2_b": rows(a[p0 + "ln2_b"]),
    }
    for n in "qkvo":
        part_a["w" + n] = a[p0 + "w" + n].T
    for n in "qkv":
        part_a["b" + n] = column(a[p0 + "b" + n])
        part_a[n + "cw"] = _np.tile(a[p0 + n + "cw"], (H0, 1))
        part_a[n + "cb"] = _np.tile(column(a[p0 + n + "cb"]), (H0, 1))
    wqkv = a["L1_attn_w_qkv"]
    part_b = {
        "wg": a["L0_ffn_Wg"], "eb1": a["L0_ffn_b1"].reshape(2 * NE, D).T, "eb2": a["L0_ffn_b2"].T,
        "ew1": a["L0_ffn_W1"].transpose(1, 0, 2).reshape(D, NE * F0),
        "ew2": a["L0_ffn_W2"].reshape(NE * 2, D, D).transpose(1, 0, 2).reshape(D, NE * 2 * D),
        "wout": a["L1_attn_w_out"].reshape(4, D, D).transpose(1, 0, 2).reshape(D, 4 * D),
        "bout": rows(a["L1_attn_b_out"]), "wr": a["L1_ffn_Wr"], "br": rows(a["L1_ffn_br"]),
    }
    arrays = {
        "xT": a["x"].transpose(2, 0, 1),
        "wa": _np.concatenate([part_a[n] for n in WA], axis=1),
        "wb": _np.concatenate([part_b[n] for n in WB], axis=1),
        "fw1": a["L1_ffn_W1"].transpose(1, 0, 2).reshape(D, NE * F1),
        "fw2": a["L1_ffn_W2"].reshape(NE * 4, D, D).transpose(1, 0, 2).reshape(D, NE * 4 * D),
        "fb": rows(_np.concatenate([a["L1_ffn_b1"].reshape(-1), a["L1_ffn_b2"].reshape(-1)])),
        "wqkv": _np.concatenate([wqkv[:, 0:2 * J * DH].reshape(D, 2, J, DH).transpose(0, 2, 1, 3).reshape(D, 2 * J * DH),
                                 wqkv[:, 2 * J * DH:]], axis=1),
        "consts": constants(),
    }
    arrays = {k: _np.ascontiguousarray(v) for k, v in arrays.items()}
    nc = _bacc.Bacc("TRN2", target_bir_lowering=False, num_devices=1)
    args = [nc.dram_tensor(k, v.shape, _mybir.dt.from_np(v.dtype), kind="ExternalInput").ap() for k, v in arrays.items()]
    args.append(nc.dram_tensor("out", (T, D), _mybir.dt.float32, kind="ExternalOutput").ap())
    build(nc, *args, stop=STOP)
    r = _run(nc, [arrays], core_ids=[0])
    return r.results[0]["out"].reshape(NB, L, D)
```

```python
from contextlib import ExitStack

import numpy as np
import concourse.bass as bass
from concourse import mybir

NB, LIN, D = 16, 250, 128
K = 128
L = LIN - K + 1
G, BG = 4, 4
GL = BG * L
T = NB * L
H0, DK = 8, 16
NE = 8
FF = 2 * D
F0 = 256
CAP = max(min(int(L * 2 / NE), L), 1)
SL = NB * CAP
HC = NE // 2 * CAP
J, DH = 8, 64
CH = J * L
F1 = 512
NT = (T + NE * 127) // 128
LN_EPS = 1e-5
EPS = 1e-6
BIG = -3.0e38

ALU = mybir.AluOpType
ACT = mybir.ActivationFunctionType
AX = mybir.AxisListType.X
F32 = mybir.dt.float32
FR = mybir.dt.float32r
BF16 = mybir.dt.bfloat16
I32 = mybir.dt.int32

WA = {}
_at = 0
for _n, _c in (("wqkv", 3 * D), ("wo", D), ("w1", FF), ("w2", 2 * D),
               ("bq", 1), ("qcw", 3), ("qcb", 1), ("b1", 2), ("b2", 1), ("ln1_g", 1), ("ln1_b", 1),
               ("temp", 1), ("bo", D), ("ln2_g", D), ("ln2_b", D)):
    WA[_n] = (_at, _at + _c)
    _at += _c
NWA = _at
WB = {}
_at = 0
for _n, _c in (("wg", NE), ("eb1", 2 * NE), ("eb2", NE), ("ew1", NE * F0), ("ew2", NE * 2 * D),
               ("wout", 4 * D), ("bout", D), ("wr", NE), ("br", NE)):
    WB[_n] = (_at, _at + _c)
    _at += _c
NWB = _at
WT = {"tok": (0, D), "tok_b": (D, D + 1), "feat": (D + 1, D + 1 + NB)}
WC = {"taps": (0, 9 * D), "b": (9 * D, 11 * D), "cb": (11 * D, 13 * D)}
CC = {}
_at = 0
for _n, _c in (("ident", 128), ("block", 128), ("block8", 8), ("slot", CAP), ("tri", 128), ("ones", 128),
               ("e8", NE), ("e8m", NE), ("thr", NB), ("tile", NT), ("mhalf", BG), ("first", NT + 1),
               ("token", 1), ("batch", NB), ("r128", 128), ("none", 1), ("tap0", 1), ("tap1", 1)):
    CC[_n] = (_at, _at + _c)
    _at += _c
NCC = _at
BODY = 8
NT_LOOP = 4 + (NT - 5) // BODY * BODY
NSLOT = 17
LQ = L + 1
LZ = L + 3
P2 = 2 * L
NQKV = 3 * J * DH


def constants():
    c = np.zeros((128, NCC), np.float32)
    p = np.arange(128)

    def put(name, v):
        c[:, CC[name][0]:CC[name][1]] = v

    put("ident", np.eye(128))
    put("block", p[:, None] // DK == p[None] // DK)
    put("block8", p[:, None] // DK == np.arange(8)[None])
    put("slot", np.arange(CAP)[None])
    put("tri", p[:, None] < p[None])
    put("ones", 1.0)
    put("e8", np.arange(NE)[None])
    put("e8m", np.arange(NE)[None] - NE)
    put("thr", 128 * np.arange(NB)[None])
    put("tile", np.arange(NT)[None])
    put("mhalf", -0.5)
    put("first", 128 * np.arange(NT + 1)[None])
    put("token", 1 + p[:, None])
    put("batch", np.arange(NB)[None])
    put("r128", np.arange(128)[None] - 128)
    put("tap0", p[:, None] >= 2)
    put("tap1", p[:, None] >= 1)
    put("none", T + 1 + p[:, None])
    return c


def build(nc, wt_d, xT_d, wa_d, wc_d, wb_d, fw1_d, fw2_d, fb_d, wqkv_d, c_d, out_d):
    ctx = ExitStack()
    with ctx:
        def sb(name, shape, dt=F32):
            return ctx.enter_context(nc.sbuf_tensor(name, shape, dt))

        def sem(name):
            return ctx.enter_context(nc.semaphore(name))

        arena = sb("arena", [128, NSLOT * 2048 + 128])
        z_hi, z_lo = sb("z_hi", [128, NB * LZ], FR), sb("z_lo", [128, NB * LZ], FR)
        w_hi, w_lo = sb("w_hi", [128, NQKV], FR), sb("w_lo", [128, NQKV], FR)
        wa = sb("wa_sb", [128, NWA])
        wb = sb("wb_sb", [128, NWB])
        wt = sb("wt_sb", [128, D + 1 + NB])
        cc = sb("cc", [128, NCC])
        ps = [ctx.enter_context(nc.psum_tensor(f"ps{i}", [128, 512], F32)) for i in range(8)]
        rows_d = nc.dram_tensor("rows", [T, 2 * D], F32, kind="Internal").ap()

        def A(name):
            return wa[:, WA[name][0]:WA[name][1]]

        def W(name):
            return wt[:, WT[name][0]:WT[name][1]]

        def B(name):
            return wb[:, WB[name][0]:WB[name][1]]

        def C(name, p=128):
            return cc[0:p, CC[name][0]:CC[name][1]]

        def region(slot, cols, p=128, off=0):
            return arena[0:p, slot * 2048 + off:slot * 2048 + off + cols]

        ident = C("ident")

        xT = region(0, NB * LIN).rearrange("p (b l) -> p b l", b=NB)
        filt = region(2, NB * (LIN + 1)).rearrange("p (b l) -> p b l", b=NB)
        gel = region(0, 2 * T).rearrange("p (c n) -> p c n", c=2)
        hid = region(2, 2 * T).rearrange("p (c n) -> p c n", c=2)
        yT = region(4, T)
        attT = region(4, T)
        h = region(5, NB * D, L).rearrange("p (b d) -> p b d", b=NB)
        z = region(6, NB * D, L).rearrange("p (b d) -> p b d", b=NB)
        zT = region(7, T)
        z_pad = [t[:].rearrange("p (b l) -> p b l", b=NB) for t in (z_hi, z_lo)]
        w_taps = region(8, 9 * D)
        kv_bias = region(8, 2 * D, L, off=9 * D)
        wc = region(9, 13 * D)
        q_e, qf = region(10, T), region(11, T)
        kvt = region(12, NB * 2 * D, L).rearrange("p (b d) -> p b d", b=NB)
        k_e = region(14, NB * D, L).rearrange("p (b d) -> p b d", b=NB)
        zb = region(0, NB * D, L).rearrange("p (b d) -> p b d", b=NB)
        att = region(10, NB * D, L).rearrange("p (b d) -> p b d", b=NB)
        r1 = region(9, NB * D, L).rearrange("p (b d) -> p b d", b=NB)
        x1T = region(11, T)
        y2T = region(12, T)
        kv = region(16, NB * (D + H0), off=0).rearrange("p (b d) -> p b d", b=NB)
        wqkv = region(15, NQKV)
        onehot = region(13, NE * SL, L).rearrange("p (b e j) -> p b e j", b=NB, e=NE)
        gated = region(2, NE * SL, L).rearrange("p (b e j) -> p b e j", b=NB, e=NE)
        ex = region(8, NE * SL).rearrange("p (e b j) -> p e b j", b=NB, e=NE)
        hm = region(10, 4 * SL).rearrange("p (r c n) -> p r c n", r=2, c=2)
        oT = region(11, NE * SL).rearrange("p (b e j) -> p b e j", b=NB, e=NE)
        gatedT = region(0, 2 * NB * L, HC).rearrange("p (b l) -> p b l", b=2 * NB)
        otok = region(8, 2 * NB * D, HC).rearrange("p (b d) -> p b d", b=2 * NB)
        o = 8 * 2048
        vm, es, esT, oP = [], [], [], []
        qT, kT, vT = [arena[0:DH, o + 2 * CH * n:o + 2 * CH * (n + 1)] for n in range(3)]
        o += 6 * CH
        for _ in range(2):
            for lst, cols, parts in ((vm, F1, L), (es, CH, L), (esT, CH, L), (oP, GL, 128)):
                lst.append(arena[0:parts, o:o + cols])
                o += cols
        assert o <= 15 * 2048
        fw1 = region(0, NE * F1)
        fw2 = region(2, NE * F1)
        fb = region(14, NE * (F1 + D), off=1024)
        row = [region(8, 2 * D, off=2 * D * i) for i in range(4)]
        h_kept = [region(12, D, off=D * i) for i in range(4)]
        xtT = [region(8, 128, off=1024 + 128 * i) for i in range(2)]
        ot = [region(8, 128, off=1280 + 128 * i) for i in range(4)]
        hb = [region(9, F1, off=512 * i) for i in range(2)]
        hbT = [region(9, F1, off=1024 + 512 * i) for i in range(2)]
        slot_of = region(10, NB * 64, L).bitcast(BF16).rearrange("p (b r) -> p b r", b=NB)
        tile_of = region(10, NB * NT, L, off=NB * 64).bitcast(BF16).rearrange("p (b t) -> p b t", b=NB)
        reach = region(11, NB * (NT + 1), L).rearrange("p (b t) -> p b t", b=NB)
        in_tile = region(11, NB * NT, L, off=512).rearrange("p (b t) -> p b t", b=NB)

        tk = sb("tk", [128, 8, NB])
        tau, npow, norm = tk[:, 3, :], tk[:, 6, :], tk[:, 7, :]
        q_fix = sb("q_fix", [128, 5])
        st = sb("st", [L, NB, 6])
        mv = sb("mv", [L, NB, 2])
        rv = sb("rv", [L, NB])
        rs = sb("rs", [L, NB])
        shift = sb("shift", [L, NB])
        ks = sb("ks", [128, NB])
        rd = sb("rd", [L, NB, H0])
        sm = sb("sm", [L, 4, NB, NE])
        gate = sb("gate", [L, NB, NE])
        red = sb("red", [L, 4, NB])
        choice = sb("choice", [128, 4, L])
        top8 = sb("top8", [128, 8])
        posl = sb("posl", [L, NB * NE])
        ksc = sb("ksc", [128, 2])
        mx = sb("mx", [L, 2, 2, J])
        sums = sb("sums", [L, 2, 2, J])
        identb = sb("identb", [L, L], BF16)
        negd = sb("negd", [L, 4, L], BF16)
        trib = sb("trib", [L, L], BF16)
        onesb = sb("onesb", [L, 128], BF16)
        ohb = sb("ohb", [L, NB, NE], BF16)
        cnt = sb("cnt", [128, 4, NE])
        cmp1 = sb("cmp1", [128, NE, NB])
        cmp2 = sb("cmp2", [128, NT, NE])
        tl = sb("tl", [128, 2, NT])
        expert = sb("expert", [128, NT + BODY], I32)
        held = sb("held", [128, 4, NT])
        take, give = sb("take", [128, NT], I32), sb("give", [128, NT], I32)

        def sems(text):
            return [sem(n) for n in text.split()]

        x_in = [sem(f"x_in{g}") for g in range(G)]
        x_ld = [sem(f"x_ld{p}") for p in range(4)]
        y_st = [sem(f"y_st{p}") for p in range(4)]
        wa_in, wb_in, cc_in, fw_in, fb_in, wqkv_in, w_split, rows_st = sems(
            "wa_in wb_in cc_in fw_in fb_in wqkv_in w_split rows_st")
        wt_in, wc_in, taps_s, taps_hi, taps_lo, bias_s, q_fixed, win_s = sems(
            "wt_in wc_in taps_s taps_hi taps_lo bias_s q_fixed win_s")
        tokz, tau_e, filt_y, y_tr, h_in, pads = sems("tokz tau_e filt_y y_tr h_in pads")
        stats = [sem(f"stats{i}") for i in range(6)]
        rstd = [sem(f"rstd{i}") for i in range(6)]
        norm_ = [sem(f"norm{i}") for i in range(6)]
        z_tr = [sem(f"z_tr{i}") for i in range(4)]
        z_ev = [sem(f"z_ev{i}") for i in range(4)]
        q_mm, q_ev, kvp_mm, kvp_s, q_exp, k_exp, q_elu, k_elu = sems("q_mm q_ev kvp_mm kvp_s q_exp k_exp q_elu k_elu")
        kv_mm, kv_ev, nd_mm, zlo_ev = sems("kv_mm kv_ev nd_mm zlo_ev")
        att_n, att_tr, att_ev, proj, zb_s, r1_s = sems("att_n att_tr att_ev proj zb_s r1_s")
        n1_tr, x1_ev, w1_mm, gel_ev, hid_s, w2_mm, y2_s, y2_tr, hpre, h_l0 = sems(
            "n1_tr x1_ev w1_mm gel_ev hid_s w2_mm y2_s y2_tr hpre h_l0")
        lg0_mm, ga_sub, ga_exp, gate_s, st_tr, pos_s, pos_tr, oneh, gat_s, ga_mm, ex_ev = sems(
            "lg0_mm ga_sub ga_exp gate_s st_tr pos_s pos_tr oneh gat_s ga_mm ex_ev")
        e1_mm, e1_ev, e2_mm, e2_ev, ot_tr, ot_ev, gt_tr, gt_ev, sc_mm, h_l1 = sems(
            "e1_mm e1_ev e2_mm e2_ev ot_tr ot_ev gt_tr gt_ev sc_mm h_l1")
        scale_e, scale_s, bf_s = sems("scale_e scale_s bf_s")
        qk_mm, vv_mm, q4_ev, k4_ev, v4_ev, vt_tr, vm_ev, sc4_mm, max_s, exp_s = sems(
            "qk_mm vv_mm q4_ev k4_ev v4_ev vt_tr vm_ev sc4_mm max_s exp_s")
        rec_s, es_n, es_tr, es_evA, es_evD, av_mm, o_ev, pr_mm, h_l2 = sems(
            "rec_s es_n es_tr es_evA es_evD av_mm o_ev pr_mm h_l2")
        lg1_mm, ohb_s, rank_mm, slot_s, held_mm, exp_i, take_s, give_s = sems(
            "lg1_mm ohb_s rank_mm slot_s held_mm exp_i take_s give_s")
        x_tr, x_ev, h_keep, h_mm, hb_s, hb_tr, hb_ev, o_mm, o_s = sems("x_tr x_ev h_keep h_mm hb_s hb_tr hb_ev o_mm o_s")
        z_lo_s = sem("z_lo_s")
        dve_n, pool_n, act_n = sems("dve_n pool_n act_n")
        block = ctx.enter_context(nc.Block())

        nd_banks = ((6, 0), (7, 1), (2, 4), (3, 5))

        def grp(t, g):
            return t[:, BG * g:BG * g + BG]

        def qk_banks(i, half):
            at = 4 + 2 * half if isinstance(i, int) and i == 0 else 4 - 4 * half
            return ps[at:at + 2]

        def v_banks(i):
            return ps[4:6] if isinstance(i, int) and i == 0 else ps[0:2]

        def out_banks(p):
            return ps[4:6] if p == 0 else ps[2:4]

        def col(t, b, n=L):
            return t[:, b * n:(b + 1) * n]

        def chunks(t, f):
            return t.rearrange("p (b t j) -> p j b t", b=2, j=J)[:, 2 * f:2 * f + 2]

        @block.sync
        def _(sp):
            sp.dma_start(wt[:], wt_d).then_inc(wt_in, 16)
            sp.dma_start(grp(xT, 0), grp(xT_d, 0)).then_inc(x_in[0], 16)
            sp.dma_start(cc[:], c_d).then_inc(cc_in, 16)
            sp.dma_start(grp(xT, 1), grp(xT_d, 1)).then_inc(x_in[1], 16)
            sp.dma_start(wa[:], wa_d).then_inc(wa_in, 16)
            sp.dma_start(wc, wc_d).then_inc(wc_in, 16)
            for g in range(2, G):
                sp.dma_start(grp(xT, g), grp(xT_d, g)).then_inc(x_in[g], 16)
            sp.dma_start(wb[:], wb_d).then_inc(wb_in, 16)
            sp.dma_start(wqkv, wqkv_d).then_inc(wqkv_in, 16)

            def by_tokens(dst, src, signal):
                d = dst.rearrange("(b l) c -> l b c", b=NB)
                for lo, hi in ((0, 120), (120, L)):
                    sp.dma_start(d[lo:hi], src[lo:hi]).then_inc(signal, 16)

            sp.wait_ge(sc_mm, NB)
            sp.wait_ge(w_split, 2)
            sp.dma_start(fw1, fw1_d).then_inc(fw_in, 16)
            sp.dma_start(fw2, fw2_d).then_inc(fw_in, 16)
            sp.dma_start(fb, fb_d).then_inc(fb_in, 16)
            sp.wait_ge(h_l2, NB)
            by_tokens(rows_d[:, D:], h, rows_st)
            sp.wait_ge(norm_[5], G)
            by_tokens(rows_d[:, 0:D], z, rows_st)
            for q in range(4):
                sp.wait_ge(y_st[q], 16 * ((NT - q + 3) // 4))

        @block.tensor
        def _(pe):
            mm = nc.tensor.matmul

            def tr(out, in_):
                p = in_.shape[0]
                return nc.tensor.transpose(out, in_, ident[0:p, 0:p])

            def in_turn(first, second):
                first(0)
                for g in range(1, G):
                    first(g)
                    second(g - 1)
                second(G - 1)

            def group_to_features(g, src, sem_in, bank, sem_out):
                pe.wait_ge(sem_in, g + 1)
                for i in range(BG):
                    last = tr(bank[:, i * L:(i + 1) * L], src[:, BG * g + i, :])
                last.then_inc(sem_out, 1)

            def group_to_tokens(g, src, sem_in, bank, sem_out):
                pe.wait_ge(sem_in, g + 1)
                for i in range(BG):
                    last = tr(bank[0:L, i * D:(i + 1) * D], col(src, BG * g + i))
                last.then_inc(sem_out, 1)

            pe.wait_ge(wt_in, 16)
            mm(ps[4][:, 0:NB], W("tok"), W("feat"), start=True, stop=True).then_inc(tokz, 1)
            pe.wait_ge(cc_in, 16)

            parts = ((w_hi, z_pad[0]), (w_hi, z_pad[1]), (w_lo, z_pad[0]))

            def queries(g):
                pe.wait_ge(zlo_ev, g + 1)
                if g == 0:
                    pe.wait_ge(taps_lo, 1)
                if g >= 2:
                    pe.wait_ge(q_ev, g - 1)
                out = ps[g % 2][:, 0:BG * LQ].rearrange("p (b l) -> p b l", b=BG)
                for n in range(9):
                    (w, zp), j = parts[n % 3], n // 3
                    last = mm(out, w[:, j * 3 * D:j * 3 * D + D], grp(zp, g)[:, :, j:j + LQ], start=n == 0, stop=n == 8)
                last.then_inc(q_mm, 1)

            def keys_values(g):
                if g >= 2:
                    pe.wait_ge(kvp_s, 2 * (g - 1))
                for i in range(BG):
                    out = ps[2 + 2 * (g % 2) + i // 2][0:LQ, (i % 2) * 2 * D:(i % 2 + 1) * 2 * D]
                    for n in range(9):
                        (w, zp), j = parts[n % 3], n // 3
                        last = mm(out, zp[:, BG * g + i, j:j + LQ], w[:, j * 3 * D + D:(j + 1) * 3 * D],
                                  start=n == 0, stop=n == 8)
                    if i % 2:
                        last.then_inc(kvp_mm, 1)

            def z_across(g):
                if g >= 2:
                    pe.wait_ge(zlo_ev, g - 1)
                group_to_features(g, z, norm_[0], ps[6 + g % 2], z_tr[0])

            def y_across(g):
                group_to_tokens(g, yT, filt_y, ps[(0, 1, 2, 5)[g]], y_tr)

            y_across(0)
            y_across(1)
            z_across(0)
            y_across(2)
            z_across(1)
            pe.wait_ge(h_in, 3)
            queries(0)
            keys_values(0)
            y_across(3)
            z_across(2)
            queries(1)
            pe.wait_ge(h_in, 4)
            keys_values(1)
            z_across(3)
            for g in (2, 3):
                queries(g)
                keys_values(g)
            for g in range(G):
                pe.wait_ge(k_elu, g + 1)
                if g == 0:
                    pe.wait_ge(zlo_ev, G)
                    pe.wait_ge(q_exp, G)
                    pe.wait_ge(q_ev, G)
                if g == 2:
                    pe.wait_ge(kvp_s, 2 * G)
                for i in range(BG):
                    b = BG * g + i
                    k_b = kvt[:, b, 0:D]
                    mm(ps[nd_banks[g][0]][:, i * D:(i + 1) * D], k_b, kvt[:, b, D:], start=True, stop=True)
                    last = mm(ps[nd_banks[g][1]][:, i:i + 1], k_b, C("ones", L)[:, 0:1], start=True, stop=True)
                last.then_inc(kv_mm, 1)
            for g in range(G):
                pe.wait_ge(kv_ev, g + 1)
                pe.wait_ge(q_elu, g + 1)
                for i in range(BG):
                    b = BG * g + i
                    last = mm(ps[nd_banks[g][i // 2]][0:L, (i % 2) * (D + H0):(i % 2 + 1) * (D + H0)],
                              col(qf, b), kv[:, b, :], start=True, stop=True)
                last.then_inc(nd_mm, 1)
            for g in range(G):
                group_to_features(g, att, att_n, ps[nd_banks[g][0]], att_tr)
            for g in range(G):
                pe.wait_ge(att_ev, g + 1)
                for i in range(BG):
                    last = mm(ps[g][0:L, i * D:(i + 1) * D], col(attT, BG * g + i), A("wo"), start=True, stop=True)
                last.then_inc(proj, 1)
            def mlp_up(g):
                pe.wait_ge(x1_ev, g + 1)
                for c in range(2):
                    mm(ps[4 * c + g][:, 0:GL], A("w1")[:, c * D:(c + 1) * D], x1T[:, GL * g:GL * g + GL],
                       start=True, stop=True).then_inc(w1_mm, 1)

            in_turn(lambda g: group_to_features(g, r1, norm_[1], ps[4 + g], n1_tr), mlp_up)
            def mlp_down(g):
                pe.wait_ge(hid_s, g + 1)
                for c in range(2):
                    last = mm(ps[g][:, 0:GL], A("w2")[:, c * D:(c + 1) * D], hid[:, c, GL * g:GL * g + GL],
                              start=c == 0, stop=c == 1)
                last.then_inc(w2_mm, 1)

            in_turn(mlp_down, lambda g: group_to_tokens(g, y2T, y2_s, ps[4 + g], y2_tr))
            pe.wait_ge(wb_in, 16)

            def gate_logits(g):
                pe.wait_ge(z_ev[1], g + 1)
                if g == 0:
                    pe.wait_ge(norm_[2], 1)
                for b in range(BG * g, BG * g + BG):
                    last = mm(ps[4][0:L, b * NE:(b + 1) * NE], col(zT, b), B("wg"), start=True, stop=True)
                last.then_inc(lg0_mm, 1)

            in_turn(lambda g: group_to_features(g, z, norm_[3], ps[g], z_tr[1]), gate_logits)
            pe.wait_ge(gate_s, 1)
            tr(ps[5][:, 0:L], gate[:].rearrange("p b e -> p (b e)")).then_inc(st_tr, 1)
            pe.wait_ge(pos_s, 1)
            tr(ps[6][0:L, 0:128], choice[:, 3, :]).then_inc(pos_tr, 1)
            for b in range(NB):
                pe.wait_ge(oneh, b // BG + 1)
                last = mm(ps[b // 2][:, (b % 2) * NE * CAP:(b % 2 + 1) * NE * CAP], z[:, b, :],
                          onehot[:, b, :, :].rearrange("p e j -> p (e j)"), start=True, stop=True)
                if b % 2:
                    last.then_inc(ga_mm, 1)

            def expert_up(e):
                for c in range(2):
                    mm(ps[2 * (e % 2) + c][:, 0:SL], B("ew1")[:, (2 * e + c) * D:(2 * e + c + 1) * D],
                       ex[:, e, :, :].rearrange("p b j -> p (b j)"), start=True, stop=True).then_inc(e1_mm, 1)

            def gates_across(c):
                pe.wait_ge(gat_s, c // 2 + 1)
                if c >= 2:
                    pe.wait_ge(gt_ev, c - 1)
                for n in range(4):
                    q = 4 * c + n
                    half = gated[:, q // 2, NE // 2 * (q % 2):NE // 2 * (q % 2 + 1), :]
                    last = tr(ps[6 + c % 2][0:HC, n * L:(n + 1) * L], half.rearrange("p e j -> p (e j)"))
                last.then_inc(gt_tr, 1)

            pe.wait_ge(ex_ev, NB // 2)
            expert_up(0)
            for e in range(NE):
                if e + 1 < NE:
                    expert_up(e + 1)
                gates_across(e)
                pe.wait_ge(e1_ev, 2 * e + 2)
                if e >= 2:
                    pe.wait_ge(e2_ev, e - 1)
                for c in range(2):
                    last = mm(ps[4 + e % 2][:, 0:SL], B("ew2")[:, (2 * e + c) * D:(2 * e + c + 1) * D],
                              hm[:, e % 2, c, :], start=c == 0, stop=c == 1)
                last.then_inc(e2_mm, 1)
            pe.wait_ge(e2_ev, NE)
            for c in range(2 * NB // 4):
                if c >= 4:
                    pe.wait_ge(ot_ev, c - 3)
                for n in range(4):
                    q = 4 * c + n
                    half = oT[:, q // 2, NE // 2 * (q % 2):NE // 2 * (q % 2 + 1), :]
                    last = tr(ps[c % 4][0:HC, n * D:(n + 1) * D], half.rearrange("p e j -> p (e j)"))
                last.then_inc(ot_tr, 1)
            pe.wait_ge(gt_ev, 2 * NB // 4)
            for b in range(NB):
                pe.wait_ge(ot_ev, b // 2 + 1)
                for n in range(2):
                    last = mm(ps[4 + b // BG][0:L, (b % BG) * D:(b % BG + 1) * D], gatedT[:, 2 * b + n, :],
                              otok[:, 2 * b + n, :], start=n == 0, stop=n == 1)
                last.then_inc(sc_mm, 1)
            def z_across_1(g):
                group_to_features(g, z, norm_[4], ps[g], z_tr[2])

            def fill(bank, i, col0):
                for n in range(2):
                    cols = slice(col0 + n * 128, col0 + (n + 1) * 128)
                    for m, (w, zz) in enumerate(((w_hi, z_hi), (w_hi, z_lo), (w_lo, z_hi))):
                        last = mm(bank[:, n * P2:(n + 1) * P2], w[:, cols], zz[:, bass.ds(i * P2, P2)],
                                  start=m == 0, stop=m == 2)
                return last

            def queries_keys(i, p):
                first = isinstance(i, int) and i == 0
                if p == 0 and not first:
                    pe.wait_ge(vm_ev, i * 2)
                for n in range(2):
                    fill(qk_banks(i, p)[n], i, (2 * p + n) * 256).then_inc(qk_mm, 1)

            def values(i):
                before = 2 if isinstance(i, int) and i == 0 else i * 4 + 4
                pe.wait_ge(q4_ev, before)
                pe.wait_ge(k4_ev, before)
                for n in range(2):
                    fill(v_banks(i)[n], i, 2 * J * DH + n * 256).then_inc(vv_mm, 1)

            def values_across(i):
                for p in range(2):
                    for hh in range(J):
                        last = tr(ps[4 + p][0:L, hh * DH:(hh + 1) * DH], col(vT, p * J + hh))
                    last.then_inc(vt_tr, 1)

            def scores(i, p):
                for q in range(2):
                    bank = ps[2 * p + q]
                    mm(bank[0:L, 0:4 * L], identb[:], negd[:].rearrange("p a l -> p (a l)"),
                       start=True, stop=False, skip_group_check=True)
                    for a in range(4):
                        hh = 4 * q + a
                        last = mm(bank[0:L, a * L:(a + 1) * L], col(qT, p * J + hh), col(kT, p * J + hh),
                                  start=False, stop=True, skip_group_check=True)
                    last.then_inc(sc4_mm, 1)

            def weights_across(i, p):
                b = i * 2 + p
                if p == 0 and not (isinstance(i, int) and i == 0):
                    pe.wait_ge(h_l2, b)
                for q in range(2):
                    pe.wait_ge(es_n, b * 2 + q + 1)
                    for a in range(4):
                        last = tr(ps[6 + q][0:L, a * L:(a + 1) * L], col(es[p], 4 * q + a))
                    last.then_inc(es_tr, 1)

            def weighted(i, p, ahead):
                b = i * 2 + p
                if p == 0 and ahead:
                    pe.wait_ge(q4_ev, i * 4 + 6)
                    pe.wait_ge(k4_ev, i * 4 + 6)
                pe.wait_ge(es_evD, i * 3 + 2 + p)
                if p == 1:
                    pe.wait_ge(es_evA, i + 1)
                for hh in range(J):
                    if hh == J - 1 and p == 1 and ahead:
                        pe.wait_ge(v4_ev, i * 4 + 8)
                        pe.wait_ge(o_ev, b)
                    last = mm(out_banks(p)[hh // 4][0:DH, (hh % 4) * L:(hh % 4 + 1) * L], vm[p][:, hh * DH:(hh + 1) * DH],
                              col(esT[p], hh), start=True, stop=True)
                last.then_inc(av_mm, 1)

            def project(i, p):
                for m in range(4):
                    last = mm(ps[6 + p][0:L, 0:D], oP[p].rearrange("p (t m) -> p m t", m=4)[:, m, :],
                              B("wout")[:, m * D:(m + 1) * D], start=m == 0, stop=m == 3)
                last.then_inc(pr_mm, 1)

            def attention(i, ahead):
                if ahead:
                    queries_keys(i + 1, 0)
                weights_across(i, 0)
                if ahead:
                    queries_keys(i + 1, 1)
                weighted(i, 0, ahead)
                weights_across(i, 1)
                if ahead:
                    values(i + 1)
                weighted(i, 1, ahead)
                if ahead:
                    values_across(i + 1)
                    scores(i + 1, 0)
                else:
                    pe.wait_ge(o_ev, i * 2 + 1)
                project(i, 0)
                pe.wait_ge(o_ev, i * 2 + 2)
                project(i, 1)
                if ahead:
                    scores(i + 1, 1)
                else:
                    for g in range(2):
                        group_to_features(g, z, norm_[5], ps[g], z_tr[3])

            z_across_1(0)
            z_across_1(1)
            pe.wait_ge(w_split, 2)
            pe.wait_ge(z_lo_s, 1)
            pe.wait_ge(z_ev[2], 1)
            queries_keys(0, 0)
            z_across_1(2)
            queries_keys(0, 1)
            values(0)
            pe.wait_ge(bf_s, 2)
            pe.wait_ge(q4_ev, 4)
            pe.wait_ge(k4_ev, 4)
            pe.wait_ge(z_lo_s, 2)
            scores(0, 0)
            z_across_1(3)
            pe.wait_ge(v4_ev, 4)
            values_across(0)
            pe.wait_ge(z_lo_s, G)
            pe.wait_ge(z_ev[2], G)
            scores(0, 1)
            attention(0, True)
            with pe.Fori(1, NB // 2 - 1) as i:
                attention(i, True)
            attention(NB // 2 - 1, False)
            def router(g):
                pe.wait_ge(z_ev[3], g + 1)
                for b in range(BG * g, BG * g + BG):
                    last = mm(ps[4][0:L, b * NE:(b + 1) * NE], col(zT, b), B("wr"), start=True, stop=True)
                last.then_inc(lg1_mm, 1)

            group_to_features(2, z, norm_[5], ps[2], z_tr[3])
            for g in range(3):
                router(g)
            group_to_features(3, z, norm_[5], ps[3], z_tr[3])
            router(3)
            pe.wait_ge(ohb_s, 1)
            ohf = ohb[:].rearrange("p b e -> p (b e)")
            mm(ps[5][0:L, 0:NB * NE], trib[:], ohf, start=True, stop=False, skip_group_check=True)
            for s in range(1, NB):
                mm(ps[5][0:L, s * NE:NB * NE], onesb[:, 0:L], ohf[:, 0:(NB - s) * NE], start=False, stop=s == NB - 1,
                   skip_group_check=True)
            for b in range(NB):
                last = mm(ps[6][:, 0:NE], onesb[:], ohb[:, b, :], start=b == 0, stop=b == NB - 1)
            last.then_inc(rank_mm, 1)
            for b in range(NB):
                pe.wait_ge(slot_s, b // BG + 1)
                last = mm(ps[6][:, 0:2 * NT], slot_of[:, b, :], tile_of[:, b, :], start=b == 0, stop=b == NB - 1)
            last.then_inc(held_mm, 1)
            pe.wait_ge(fw_in, 32)
            pe.wait_ge(exp_i, 1)

            def tokens_across(t, q):
                pe.wait_ge(x_ld[q], (t // 4 + 1) * 16 if isinstance(t, int) else (t - q + 4) * 4)
                tr(ps[q % 2][:, 0:128], row[q][:, 0:D]).then_inc(x_tr, 1)

            def expert_of(t):
                return pe.value_load(expert[0:1, bass.ds(t, 1)], min_val=0, max_val=NE - 1)

            def up(t, q, e):
                p = q % 2
                pe.wait_ge(x_ev, t + 1)
                mm(ps[2 + p][:, 0:F1], xtT[p], fw1[:, bass.ds(e * F1, F1)], start=True, stop=True).then_inc(h_mm, 1)

            def hidden_across(t, q):
                p = q % 2
                pe.wait_ge(hb_s, t + 1)
                for c in range(4):
                    last = tr(ps[4 + p][:, c * 128:(c + 1) * 128], hb[p][:, c * 128:(c + 1) * 128])
                last.then_inc(hb_tr, 1)

            def out(t, q, first, e):
                p = q % 2
                pe.wait_ge(hb_ev, t + 1)
                if not first:
                    pe.wait_ge(o_s, t - 1)
                for c in range(4):
                    last = mm(ps[6 + p][:, 0:D], hbT[p][:, c * 128:(c + 1) * 128],
                              fw2[:, bass.ds(e * F1 + c * D, D)], start=c == 0, stop=c == 3)
                last.then_inc(o_mm, 1)

            def steps(t0, n):
                e = {2: expert_of(t0 + 2)}
                for q in range(n):
                    t = t0 + q
                    left = NT - 1 - t if isinstance(t, int) else NT
                    if left >= 2:
                        up(t + 2, (q + 2) % 4, e[q + 2])
                    if left >= 3:
                        tokens_across(t + 3, (q + 3) % 4)
                    if left >= 1:
                        hidden_across(t + 1, (q + 1) % 4)
                    if q == 0:
                        e[0] = expert_of(t)
                    out(t, q % 4, isinstance(t, int) and t < 2, e[q])
                    if q == 0 and n > 1:
                        e[1] = expert_of(t + 1)
                    if q + 1 < n:
                        e[q + 3] = expert_of(t + 3)

            tokens_across(0, 0)
            tokens_across(1, 1)
            up(0, 0, expert_of(0))
            tokens_across(2, 2)
            up(1, 1, expert_of(1))
            hidden_across(0, 0)
            steps(0, 4)
            with pe.Fori(4, NT_LOOP, BODY) as t:
                steps(t, BODY)
            steps(NT_LOOP, NT - NT_LOOP)

        @block.scalar
        def _(act):
            fn = nc.scalar.activation

            def evacuate(bank, dst, sem_in, sem_out, g):
                act.wait_ge(sem_in, g + 1)
                fn(dst[:, GL * g:GL * g + GL], ps[bank][:, 0:GL], ACT.Copy).then_inc(sem_out, 1)

            def normalise(n, src_of, dst, g):
                act.wait_ge(rstd[n], g + 1)
                for b in range(BG * g, BG * g + BG):
                    last = fn(dst[:, b, :], src_of(b), ACT.Identity, bias=shift[:, b:b + 1], scale=rs[:, b:b + 1])
                last.then_inc(norm_[n], 1)

            def in_turn(first, second):
                first(0)
                for g in range(1, G):
                    first(g)
                    second(g - 1)
                second(G - 1)

            h_row = lambda b: h[:, b, :]

            act.wait_ge(tokz, 1)
            act.wait_ge(tau_e, 1)
            fn(tk[:, 1, :], ps[4][:, 0:NB], ACT.Exp, bias=tk[:, 0, 0:1], scale=-0.1).then_inc(tau_e, 1)

            def scale_y(g):
                act.wait_ge(win_s, g + 1)
                for b in range(BG * g, BG * g + BG):
                    last = fn(col(yT, b), col(yT, b), ACT.Copy, scale=norm[:, b:b + 1])
                last.then_inc(filt_y, 1)

            def h_rows(g):
                act.wait_ge(y_tr, g + 1)
                fn(grp(h, g).rearrange("p b d -> p (b d)"), ps[(0, 1, 2, 5)[g]][0:L, :], ACT.Copy).then_inc(h_in, 1)

            def z_high(g):
                if g == 0:
                    act.wait_ge(pads, 1)
                act.wait_ge(z_tr[0], g + 1)
                fn(grp(z_pad[0], g)[:, :, 2:2 + L], ps[6 + g % 2][:, 0:GL].rearrange("p (b l) -> p b l", b=BG), ACT.Copy)\
                    .then_inc(z_ev[0], 1)

            def q_parts(g):
                act.wait_ge(q_fixed, g + 1)
                src = ps[g % 2][:, 0:BG * LQ].rearrange("p (b l) -> p b l", b=BG)[:, :, 0:L]
                dst = [col(t, g, GL).rearrange("p (b l) -> p b l", b=BG) for t in (q_e, qf)]
                fn(dst[0], src, ACT.Relu, bias=q_fix[:, 4:5], scale=-1.0).then_inc(act_n, 1)
                fn(dst[1], src, ACT.Relu, bias=q_fix[:, 3:4]).then_inc(q_ev, 1)
                act.wait_ge(act_n, 2 * g + 1)
                fn(dst[0], dst[0], ACT.Exp, scale=-1.0).then_inc(q_exp, 1)

            def k_parts(g):
                act.wait_ge(kvp_s, 2 * g + 2)
                k_g, e_g = grp(kvt, g)[:, :, 0:D], grp(k_e, g)
                fn(e_g, k_g, ACT.Relu, scale=-1.0).then_inc(act_n, 1)
                act.wait_ge(act_n, 2 * g + 2)
                fn(k_g, k_g, ACT.Relu)
                fn(e_g, e_g, ACT.Exp, scale=-1.0).then_inc(k_exp, 1)

            scale_y(0)
            h_rows(0)
            scale_y(1)
            act.wait_ge(taps_s, 1)
            fn(w_hi[:, 0:9 * D], w_taps, ACT.Copy).then_inc(taps_hi, 1)
            h_rows(1)
            z_high(0)
            scale_y(2)
            h_rows(2)
            z_high(1)
            scale_y(3)
            q_parts(0)
            h_rows(3)
            k_parts(0)
            z_high(2)
            q_parts(1)
            k_parts(1)
            z_high(3)
            for g in (2, 3):
                q_parts(g)
                k_parts(g)
            for g in range(G):
                act.wait_ge(att_tr, g + 1)
                fn(col(attT, g, GL), ps[nd_banks[g][0]][:, 0:GL], ACT.Copy).then_inc(att_ev, 1)

            def x1_features(g):
                act.wait_ge(n1_tr, g + 1)
                fn(x1T[:, GL * g:GL * g + GL], ps[4 + g][:, 0:GL], ACT.Identity, bias=A("ln1_b"), scale=A("ln1_g"))\
                    .then_inc(x1_ev, 1)

            in_turn(lambda g: normalise(1, lambda b: r1[:, b, :], r1, g), x1_features)
            for g in range(G):
                for c in range(2):
                    act.wait_ge(w1_mm, 2 * g + c + 1)
                    fn(gel[:, c, GL * g:GL * g + GL], ps[4 * c + g][:, 0:GL], ACT.Gelu, bias=A("b1")[:, c:c + 1])\
                        .then_inc(gel_ev, 1)
            pb = lambda b: ps[4 + b // BG][0:L, (b % BG) * D:(b % BG + 1) * D]
            for g in range(3):
                normalise(2, pb, r1, g)
            normalise(3, h_row, z, 0)
            normalise(2, pb, r1, 3)
            for g in range(1, G):
                normalise(3, h_row, z, g)
                evacuate(g - 1, zT, z_tr[1], z_ev[1], g - 1)
            evacuate(3, zT, z_tr[1], z_ev[1], 3)
            act.wait_ge(ga_sub, 1)
            fn(sm[:, 1], sm[:, 0], ACT.Exp).then_inc(ga_exp, 1)
            fn(ksc[:, 0:1], A("temp"), ACT.Exp).then_inc(scale_e, 1)
            for n in range(NB // 2):
                act.wait_ge(ga_mm, n + 1)
                fn(ex[:, :, 2 * n:2 * n + 2, :].rearrange("p e b j -> p b e j"),
                   ps[n][:, 0:2 * NE * CAP].rearrange("p (b e j) -> p b e j", b=2, e=NE), ACT.Copy).then_inc(ex_ev, 1)
            for e in range(NE):
                if e >= 2:
                    act.wait_ge(e2_mm, e - 1)
                for c in range(2):
                    act.wait_ge(e1_mm, 2 * e + c + 1)
                    fn(hm[:, e % 2, c, :], ps[2 * (e % 2) + c][:, 0:SL], ACT.Gelu,
                       bias=B("eb1")[:, 2 * e + c:2 * e + c + 1]).then_inc(e1_ev, 1)
            for c in range(2 * NB // 4):
                act.wait_ge(ot_tr, c + 1)
                fn(otok[:, 4 * c:4 * c + 4, :].rearrange("p q d -> p (q d)"), ps[c % 4][0:HC, :], ACT.Copy)\
                    .then_inc(ot_ev, 1)

            def z_high_1(g):
                evacuate(g, z_hi, z_tr[2], z_ev[2], g)

            normalise(4, h_row, z, 0)
            normalise(4, h_row, z, 1)
            z_high_1(0)
            normalise(4, h_row, z, 2)
            z_high_1(1)

            def queries(i, p):
                for q in range(2):
                    bank = qk_banks(i, p)[q]
                    act.wait_ge(qk_mm, (i * 2 + p) * 2 + q + 1)
                    fn(chunks(qT, 2 * p + q), bank[0:DH, 0:2 * P2].rearrange("p (j b t) -> p j b t", j=2, b=2),
                       ACT.Copy).then_inc(q4_ev, 1)

            def values(i):
                for n in range(2):
                    act.wait_ge(vv_mm, i * 2 + n + 1)
                    for q in range(2):
                        fn(vT.rearrange("p (b t j q) -> p j b t q", b=2, j=4, q=2)[:, 2 * n:2 * n + 2, :, :, q],
                           v_banks(i)[n][q * DH:(q + 1) * DH, 0:2 * P2].rearrange("p (j b t) -> p j b t", j=2, b=2),
                           ACT.Copy).then_inc(v4_ev, 1)

            def values_rows():
                for p in range(2):
                    fn(vm[p], ps[4 + p][0:L, :], ACT.Copy).then_inc(vm_ev, 1)

            def exponents(i, p, quads):
                for q in quads:
                    act.wait_ge(max_s, (i * 2 + p) * 2 + q + 1)
                    for a in range(4):
                        hh = 4 * q + a
                        last = fn(col(es[p], hh), ps[2 * p + q][0:L, a * L:(a + 1) * L], ACT.Exp,
                                  bias=mx[:, p, 1, hh:hh + 1], scale=ksc[0:L, 0:1],
                                  accum_out=sums[:, p, 0, hh:hh + 1])
                    last.then_inc(exp_s, 1)

            def weights_across(i):
                act.wait_ge(es_tr, i * 4 + 3)
                fn(esT[1][:, 0:4 * L], ps[6][0:L, 0:4 * L], ACT.Copy).then_inc(es_evA, 1)

            def attention(i, ahead):
                if not (isinstance(i, int) and i == 0):
                    exponents(i, 0, (0, 1))
                exponents(i, 1, (0,))
                if ahead:
                    queries(i + 1, 0)
                exponents(i, 1, (1,))
                if ahead:
                    queries(i + 1, 1)
                weights_across(i)
                if ahead:
                    values(i + 1)
                    act.wait_ge(vt_tr, i * 2 + 4)
                    values_rows()

            queries(0, 0)
            queries(0, 1)
            normalise(4, h_row, z, 3)
            values(0)
            z_high_1(2)
            z_high_1(3)
            act.wait_ge(scale_s, 1)
            exponents(0, 0, (0,))
            act.wait_ge(vt_tr, 2)
            values_rows()
            exponents(0, 0, (1,))
            attention(0, True)
            with act.Fori(1, NB // 2 - 1) as i:
                attention(i, True)
            attention(NB // 2 - 1, False)
            normalise(5, h_row, z, 0)
            normalise(5, h_row, z, 1)
            evacuate(0, zT, z_tr[3], z_ev[3], 0)
            evacuate(1, zT, z_tr[3], z_ev[3], 1)
            for g in (2, 3):
                normalise(5, h_row, z, g)
                evacuate(g, zT, z_tr[3], z_ev[3], g)

            def up(t, q):
                act.wait_ge(x_tr, t + 1)
                fn(xtT[q % 2], ps[q % 2][:, 0:128], ACT.Copy).then_inc(x_ev, 1)
                if not (isinstance(t, int) and t < 4):
                    act.wait_ge(o_s, t - 3)
                fn(h_kept[q], row[q][:, D:], ACT.Copy).then_inc(h_keep, 1)

            def down(t, q):
                act.wait_ge(hb_tr, t + 1)
                fn(hbT[q % 2], ps[4 + q % 2][:, :], ACT.Relu).then_inc(hb_ev, 1)

            def step(t, q):
                if not (isinstance(t, int) and t + 3 >= NT):
                    up(t + 3, (q + 3) % 4)
                if not (isinstance(t, int) and t + 1 >= NT):
                    down(t + 1, (q + 1) % 4)

            for t in range(3):
                up(t, t)
            down(0, 0)
            for t in range(4):
                step(t, t)
            with act.Fori(4, NT_LOOP, BODY) as t:
                for q in range(BODY):
                    step(t + q, q % 4)
            for t in range(NT_LOOP, NT):
                step(t, t % 4)

        @block.gpsimd
        def _(pool):
            count = [0]

            def own(ins):
                count[0] += 1
                ins.then_inc(pool_n, 1)
                pool.wait_ge(pool_n, count[0])

            def rsqrt(n, groups=range(G)):
                for g in groups:
                    pool.wait_ge(stats[n], g + 1)
                    c = slice(BG * g, BG * g + BG)
                    if n > 0:
                        nc.gpsimd.tensor_scalar(shift[:, c], mv[:, c, 0], -1.0, None, ALU.mult)
                    own(nc.gpsimd.tensor_scalar(rv[:, c], mv[:, c, 1], LN_EPS, None, ALU.add))
                    if n == 0:
                        nc.gpsimd.tensor_tensor(rs[:, c], rv[:, c], C("mhalf", L), ALU.pow).then_inc(rstd[n], 1)
                        continue
                    own(nc.gpsimd.tensor_tensor(rs[:, c], rv[:, c], C("mhalf", L), ALU.pow))
                    nc.gpsimd.tensor_tensor(shift[:, c], shift[:, c], rs[:, c], ALU.mult).then_inc(rstd[n], 1)

            for t in z_pad:
                nc.gpsimd.memset(t[:, :, 0:2].bitcast(F32), 0.0)
                last = nc.gpsimd.memset(t[:, :, 2 + L:].bitcast(F32), 0.0)
            last.then_inc(pads, 1)
            pool.wait_ge(cc_in, 16)
            pool.wait_ge(wa_in, 16)
            pool.wait_ge(wc_in, 16)
            nc.gpsimd.tensor_tensor(w_taps.rearrange("p (j c) -> p j c", j=3), A("wqkv")[:, None, :].to_broadcast([128, 3, 3 * D]),
                                    wc[:, 0:9 * D].rearrange("p (j c) -> p j c", j=3), ALU.mult).then_inc(taps_s, 1)

            rsqrt(0, (0,))
            pool.wait_ge(taps_hi, 1)
            nc.gpsimd.tensor_tensor(w_lo[:, 0:9 * D], w_taps, w_hi[:, 0:9 * D].bitcast(F32), ALU.subtract).then_inc(taps_lo, 1)
            rsqrt(0, (1, 2))
            tap = [wc[0:L, j * 3 * D + D:(j + 1) * 3 * D] for j in range(3)]
            own(nc.gpsimd.tensor_scalar(kv_bias, tap[0], C("tap0", L), None, ALU.mult))
            own(nc.gpsimd.tensor_scalar(tap[1], tap[1], C("tap1", L), None, ALU.mult))
            own(nc.gpsimd.tensor_tensor(kv_bias, kv_bias, tap[1], ALU.add))
            own(nc.gpsimd.tensor_tensor(kv_bias, kv_bias, tap[2], ALU.add))
            own(nc.gpsimd.tensor_tensor(kv_bias, kv_bias, wc[0:L, WC["b"][0]:WC["b"][1]], ALU.mult))
            nc.gpsimd.tensor_tensor(kv_bias, kv_bias, wc[0:L, WC["cb"][0]:WC["cb"][1]], ALU.add).then_inc(bias_s, 1)
            rsqrt(0, (3,))
            for g in range(G):
                pool.wait_ge(norm_[0], g + 1)
                nc.gpsimd.tensor_tensor(grp(zb, g), grp(z, g), A("bo")[0:L, None, :].to_broadcast([L, BG, D]),
                                        ALU.add).then_inc(zb_s, 1)
            for g in range(G):
                nc.gpsimd.tensor_tensor(grp(h, g), grp(h, g), A("ln2_b")[0:L, None, :].to_broadcast([L, BG, D]),
                                        ALU.add).then_inc(hpre, 1)
            rsqrt(1)
            rsqrt(2)
            rsqrt(3)
            pool.wait_ge(wqkv_in, 16)
            nc.gpsimd.tensor_copy(w_hi[:], wqkv).then_inc(w_split, 1)
            pool.wait_ge(w_split, 1)
            nc.gpsimd.tensor_tensor(w_lo[:], wqkv, w_hi[:].bitcast(F32), ALU.subtract).then_inc(w_split, 1)
            for g in range(G):
                pool.wait_ge(oneh, g + 1)
                nc.gpsimd.tensor_tensor(grp(gated, g).rearrange("p b e j -> p (b e) j"),
                                        grp(onehot, g).rearrange("p b e j -> p (b e) j"),
                                        grp(gate, g).rearrange("p b e -> p (b e)")[:, :, None]
                                        .to_broadcast([L, BG * NE, CAP]), ALU.mult).then_inc(gat_s, 1)
            rsqrt(4)

            def weights(i):
                for p in range(2):
                    for q in range(2):
                        pool.wait_ge(rec_s, (i * 2 + p) * 2 + q + 1)
                        half = es[p][:, 4 * q * L:4 * (q + 1) * L].rearrange("p (a l) -> p a l", a=4)
                        nc.gpsimd.tensor_tensor(half, half, sums[:, p, 1, 4 * q:4 * q + 4, None].to_broadcast([L, 4, L]),
                                                ALU.mult).then_inc(es_n, 1)

            weights(0)
            with pool.Fori(1, NB // 2 - 1) as i:
                weights(i)
            weights(NB // 2 - 1)
            rsqrt(5)
            pool.wait_ge(rows_st, 64)
            pool.wait_ge(take_s, 1)

            def gather(t):
                if t >= 4:
                    pool.wait_ge(h_keep, t - 3)
                nc.gpsimd.indirect_dma_start(row[t % 4], None, rows_d,
                                             bass.IndirectOffsetOnAxis(ap=take[:, t:t + 1], axis=0))\
                    .then_inc(x_ld[t % 4], 16)

            for t in range(6):
                gather(t)
            pool.wait_ge(give_s, 1)
            for t in range(NT):
                pool.wait_ge(o_s, t + 1)
                nc.gpsimd.indirect_dma_start(out_d, bass.IndirectOffsetOnAxis(ap=give[:, t:t + 1], axis=0),
                                             ot[t % 4], None, bounds_check=T - 1, oob_is_err=False)\
                    .then_inc(y_st[t % 4], 16)
                if t + 6 < NT:
                    gather(t + 6)

        @block.vector
        def _(dve):
            V = nc.vector
            count = [0]

            def own(ins):
                count[0] += 1
                ins.then_inc(dve_n, 1)
                dve.wait_ge(dve_n, count[0])

            def layer_stats(n, src_of, wait, groups=range(G)):
                for g in groups:
                    if wait is not None:
                        dve.wait_ge(wait, g + 1)
                    for i in range(BG):
                        last = V.bn_stats(st[:, BG * g + i, :], src_of(BG * g + i))
                    own(last)
                    for i in range(BG):
                        last = V.bn_aggr(mv[:, BG * g + i, :], st[:, BG * g + i, :])
                    last.then_inc(stats[n], 1)

            def layer_norm(n, src, dst, groups=range(G)):
                for g in groups:
                    dve.wait_ge(stats[n], g + 1)
                    dve.wait_ge(rstd[n], g + 1)
                    for b in range(BG * g, BG * g + BG):
                        last = V.tensor_scalar(dst[:, b, :], src[:, b, :], mv[:, b, 0:1], rs[:, b:b + 1],
                                               ALU.subtract, ALU.mult)
                    last.then_inc(norm_[n], 1)

            dve.wait_ge(wt_in, 16)
            V.tensor_scalar(tk[:, 0, 0:1], W("tok_b"), -0.1, 3.0, ALU.mult, ALU.add).then_inc(tau_e, 1)
            own(V.memset(filt[:, :, 0:1], 0.0))
            dve.wait_ge(tau_e, 2)
            own(V.tensor_scalar(tk[:, 2, :], tk[:, 1, :], 1.0, None, ALU.add))
            own(V.reciprocal(tau, tk[:, 2, :]))
            own(V.tensor_scalar(tk[:, 5, :], tau, 1.0, None, ALU.add))
            own(V.tensor_tensor(tk[:, 4, :], tau, tau, ALU.mult))
            n = 2
            while n < K:
                own(V.scalar_tensor_tensor(tk[:, 5, :], tk[:, 4, :], 1.0, tk[:, 5, :], ALU.add, ALU.mult))
                own(V.tensor_tensor(tk[:, 4, :], tk[:, 4, :], tk[:, 4, :], ALU.mult))
                n *= 2
            assert n == K
            own(V.reciprocal(norm, tk[:, 5, :]))
            own(V.tensor_scalar(npow, tk[:, 4, :], -1.0, None, ALU.mult))
            def window(g):
                dve.wait_ge(x_in[g], 16)
                bs = range(BG * g, BG * g + BG)
                for b in bs:
                    last = V.tensor_tensor_scan(filt[:, b, 1:], tau[:, b:b + 1].to_broadcast([128, LIN]), xT[:, b, :],
                                                0.0, ALU.mult, ALU.add)
                own(last)
                for b in bs:
                    last = V.scalar_tensor_tensor(col(yT, b), filt[:, b, 0:L], npow[:, b:b + 1], filt[:, b, K:K + L],
                                                  ALU.mult, ALU.add)
                last.then_inc(win_s, 1)

            def stats_0(g):
                layer_stats(0, lambda b: h[:, b, :], h_in, (g,))

            def norm_0(g):
                layer_norm(0, h, z, (g,))

            def z_low(g):
                dve.wait_ge(z_ev[0], g + 1)
                dst = grp(z_pad[1], g)[:, :, 2:2 + L]
                V.tensor_tensor(dst, ps[6 + g % 2][:, 0:GL].rearrange("p (b l) -> p b l", b=BG),
                                grp(z_pad[0], g)[:, :, 2:2 + L].bitcast(F32), ALU.subtract).then_inc(zlo_ev, 1)

            def fix_q(g):
                dve.wait_ge(q_mm, g + 1)
                first = ps[g % 2][:, 0:BG * LQ].rearrange("p (b l) -> p b l", b=BG)[:, :, 0:2]
                V.tensor_tensor(first, first, q_fix[:, None, 0:2].to_broadcast([128, BG, 2]), ALU.add).then_inc(q_fixed, 1)

            def bias_kv(g):
                if g == 0:
                    dve.wait_ge(bias_s, 1)
                for n in range(2):
                    dve.wait_ge(kvp_mm, 2 * g + n + 1)
                    b = BG * g + 2 * n
                    V.tensor_tensor(kvt[:, b:b + 2, :], ps[2 + 2 * (g % 2) + n][0:L, :].rearrange("p (b d) -> p b d", b=2),
                                    kv_bias[:, None, :].to_broadcast([L, 2, 2 * D]), ALU.add).then_inc(kvp_s, 1)

            def elu(g):
                dve.wait_ge(k_exp, g + 1)
                k_g = grp(kvt, g)[:, :, 0:D]
                V.tensor_tensor(k_g, grp(k_e, g), k_g, ALU.add).then_inc(k_elu, 1)
                dve.wait_ge(q_exp, g + 1)
                dve.wait_ge(q_ev, g + 1)
                q_g = col(qf, g, GL)
                V.tensor_tensor(q_g, col(q_e, g, GL), q_g, ALU.add).then_inc(q_elu, 1)

            window(0)
            window(1)
            stats_0(0)
            dve.wait_ge(wa_in, 16)
            own(V.tensor_scalar(q_fix[:, 0:3], A("qcw"), A("bq"), None, ALU.mult))
            own(V.scalar_tensor_tensor(q_fix[:, 0:1], q_fix[:, 0:1], -1.0, q_fix[:, 1:2], ALU.mult, ALU.subtract))
            own(V.tensor_tensor(q_fix[:, 3:4], q_fix[:, 2:3], q_fix[:, 0:1], ALU.subtract))
            own(V.tensor_tensor(q_fix[:, 3:4], q_fix[:, 3:4], A("qcb"), ALU.add))
            own(V.tensor_scalar(q_fix[:, 4:5], q_fix[:, 3:4], -1.0, None, ALU.mult))
            own(V.tensor_tensor(q_fix[:, 1:2], q_fix[:, 0:1], q_fix[:, 1:2], ALU.add))
            norm_0(0)
            window(2)
            stats_0(1)
            z_low(0)
            norm_0(1)
            window(3)
            stats_0(2)
            z_low(1)
            norm_0(2)
            fix_q(0)
            bias_kv(0)
            stats_0(3)
            z_low(2)
            norm_0(3)
            fix_q(1)
            elu(0)
            bias_kv(1)
            z_low(3)
            elu(1)
            for g in (2, 3):
                fix_q(g)
                bias_kv(g)
                elu(g)
            for g in range(G):
                dve.wait_ge(kv_mm, g + 1)
                own(V.tensor_scalar(ks[:, BG * g:BG * g + BG], ps[nd_banks[g][1]][:, 0:BG], EPS, None, ALU.add))
                V.tensor_tensor(grp(kv, g)[:, :, 0:D], ps[nd_banks[g][0]][:, :].rearrange("p (b d) -> p b d", b=BG),
                                C("block")[:, None, :].to_broadcast([128, BG, D]), ALU.mult)
                V.tensor_tensor(grp(kv, g)[:, :, D:], C("block8")[:, None, :].to_broadcast([128, BG, H0]),
                                ks[:, BG * g:BG * g + BG, None].to_broadcast([128, BG, H0]), ALU.mult).then_inc(kv_ev, 1)
            for g in range(G):
                dve.wait_ge(nd_mm, g + 1)
                for n in range(2):
                    b = BG * g + 2 * n
                    nd = ps[nd_banks[g][n]][0:L, 0:2 * (D + H0)].rearrange("p (b d) -> p b d", b=2)
                    own(V.reciprocal(rd[:, b:b + 2, :], nd[:, :, D:]))
                    last = V.tensor_tensor(att[:, b:b + 2, :].rearrange("p b (h d) -> p b h d", d=DK),
                                           nd[:, :, 0:D].rearrange("p b (h d) -> p b h d", d=DK),
                                           rd[:, b:b + 2, :, None].to_broadcast([L, 2, H0, DK]), ALU.mult)
                last.then_inc(att_n, 1)
            for g in range(G):
                dve.wait_ge(proj, g + 1)
                dve.wait_ge(zb_s, g + 1)
                V.tensor_tensor(grp(r1, g), ps[g][0:L, :].rearrange("p (b d) -> p b d", b=BG), grp(zb, g), ALU.add)\
                    .then_inc(r1_s, 1)
                layer_stats(1, lambda b: r1[:, b, :], r1_s, (g,))

            def square(g):
                dve.wait_ge(gel_ev, 2 * g + 2)
                g_g = gel[:, :, GL * g:GL * g + GL]
                V.tensor_tensor(hid[:, :, GL * g:GL * g + GL], g_g, g_g, ALU.mult).then_inc(hid_s, 1)

            def add_mlp(g):
                dve.wait_ge(w2_mm, g + 1)
                V.scalar_tensor_tensor(col(y2T, g, GL), ps[g][:, 0:GL], A("b2"), col(x1T, g, GL), ALU.add, ALU.add)\
                    .then_inc(y2_s, 1)

            def residual(g):
                dve.wait_ge(norm_[2], g + 1)
                dve.wait_ge(hpre, g + 1)
                own(V.tensor_tensor(grp(r1, g), grp(r1, g), A("ln2_g")[0:L, None, :].to_broadcast([L, BG, D]), ALU.mult))
                V.tensor_tensor(grp(h, g), grp(h, g), grp(r1, g), ALU.add).then_inc(h_l0, 1)

            pb = lambda b: ps[4 + b // BG][0:L, (b % BG) * D:(b % BG + 1) * D]
            square(0)
            for g in range(G + 4):
                if g + 1 < G:
                    square(g + 1)
                if g < G:
                    add_mlp(g)
                if 1 <= g <= G:
                    layer_stats(2, pb, y2_tr, (g - 1,))
                if 3 <= g < G + 3:
                    residual(g - 3)
                if g >= 4:
                    layer_stats(3, lambda b: h[:, b, :], h_l0, (g - 4,))
            lg = ps[4][0:L, 0:NB * NE].rearrange("p (b e) -> p b e", b=NB)
            wide = lambda r: r[:, :, None].to_broadcast([L, NB, NE])
            dve.wait_ge(lg0_mm, G)
            own(V.tensor_reduce(red[:, 0], lg, AX, ALU.max))
            V.tensor_tensor(sm[:, 0], lg, wide(red[:, 0]), ALU.subtract).then_inc(ga_sub, 1)
            dve.wait_ge(ga_exp, 1)
            own(V.tensor_reduce(red[:, 1], sm[:, 1], AX, ALU.add))
            own(V.reciprocal(red[:, 2], red[:, 1]))
            V.tensor_tensor(gate[:], sm[:, 1], wide(red[:, 2]), ALU.mult).then_inc(gate_s, 1)
            dve.wait_ge(st_tr, 1)
            own(V.tensor_copy(choice[:, 0, :], ps[5][:, 0:L]))
            for n in range(0, CAP, 8):
                own(V.max(top8[:], choice[:, 0, :]))
                if CAP - n < 8:
                    own(V.memset(top8[:, CAP - n:8], -1.0))
                own(V.match_replace(choice[:, 0, :], top8[:], choice[:, 0, :], -1.0))
            own(V.tensor_scalar(choice[:, 1, :], choice[:, 0, :], -1.0, None, ALU.is_equal))
            own(V.tensor_tensor_scan(choice[:, 2, :], C("ones")[:, 0:L], choice[:, 1, :], 0.0, ALU.mult, ALU.add))
            own(V.tensor_tensor(choice[:, 3, :], choice[:, 2, :], choice[:, 1, :], ALU.mult))
            V.tensor_scalar(choice[:, 3, :], choice[:, 3, :], -1.0, None, ALU.add).then_inc(pos_s, 1)
            dve.wait_ge(pos_tr, 1)
            own(V.tensor_copy(posl[:], ps[6][0:L, 0:128]))
            nbe = BG * NE
            for g in range(G):
                V.tensor_tensor(grp(onehot, g).rearrange("p b e j -> p (b e) j"),
                                posl[:, g * nbe:(g + 1) * nbe, None].to_broadcast([L, nbe, CAP]),
                                C("slot", L)[:, None, :].to_broadcast([L, nbe, CAP]), ALU.is_equal).then_inc(oneh, 1)
            for e in range(NE):
                dve.wait_ge(gt_tr, e + 1)
                V.tensor_copy(gatedT[:, 4 * e:4 * e + 4, :].rearrange("p q l -> p (q l)"), ps[6 + e % 2][0:HC, 0:4 * L])\
                    .then_inc(gt_ev, 1)
                dve.wait_ge(e2_mm, e + 1)
                V.tensor_scalar(oT[:, :, e, :], ps[4 + e % 2][:, 0:SL].rearrange("p (b j) -> p b j", b=NB),
                                B("eb2")[:, e:e + 1], None, ALU.add).then_inc(e2_ev, 1)
            for g in range(G):
                dve.wait_ge(sc_mm, BG * g + BG)
                V.tensor_tensor(grp(h, g), ps[4 + g][0:L, :].rearrange("p (b d) -> p b d", b=BG), grp(h, g), ALU.add)\
                    .then_inc(h_l1, 1)
                layer_stats(4, lambda b: h[:, b, :], h_l1, (g,))
            V.tensor_copy(identb[:], C("ident", L)[:, 0:L]).then_inc(bf_s, 1)
            V.tensor_scalar(negd[:], C("ident", L)[:, None, 0:L].to_broadcast([L, 4, L]), BIG, None, ALU.mult)\
                .then_inc(bf_s, 1)
            dve.wait_ge(scale_e, 1)
            V.tensor_scalar(ksc[:, 1:2], ksc[:, 0:1], -1.0, None, ALU.mult).then_inc(scale_s, 1)
            dve.wait_ge(scale_s, 1)
            base = count[0] + 4

            def z_low_1(g):
                dve.wait_ge(z_ev[2], g + 1)
                V.tensor_tensor(col(z_lo, g, GL), ps[g][:, 0:GL], col(z_hi, g, GL).bitcast(F32), ALU.subtract)\
                    .then_inc(z_lo_s, 1)

            def keys(i, p):
                for q in range(2):
                    bank = qk_banks(i, p)[q]
                    dve.wait_ge(qk_mm, (i * 2 + p) * 2 + q + 1)
                    V.tensor_copy(chunks(kT, 2 * p + q),
                                  bank[DH:128, 0:2 * P2].rearrange("p (j b t) -> p j b t", j=2, b=2))\
                        .then_inc(k4_ev, 1)

            def attention(i, ahead, between=lambda place: None):
                done = [0]

                def own2(ins):
                    done[0] += 1
                    ins.then_inc(dve_n, 1)
                    if not ahead:
                        count[0] += 1
                        dve.wait_ge(dve_n, count[0])
                        return
                    dve.wait_ge(dve_n, i * 6 + base + done[0])

                def maxima(i, p, own_=own2, halves=(0, 1)):
                    for q in halves:
                        dve.wait_ge(sc4_mm, (i * 2 + p) * 2 + q + 1)
                        own_(V.tensor_reduce(mx[:, p, 0, 4 * q:4 * q + 4],
                                             ps[2 * p + q][0:L, 0:4 * L].rearrange("p (a l) -> p a l", a=4), AX, ALU.max))
                        V.tensor_scalar(mx[:, p, 1, 4 * q:4 * q + 4], mx[:, p, 0, 4 * q:4 * q + 4], ksc[0:L, 1:2], None,
                                        ALU.mult).then_inc(max_s, 1)

                def output(p):
                    dve.wait_ge(av_mm, i * 2 + p + 1)
                    for q in range(2):
                        for par in range(2):
                            last = V.tensor_copy(oP[p][par * DH:(par + 1) * DH, q * 2 * L:(q + 1) * 2 * L],
                                                 out_banks(p)[q][0:DH, bass.ds(par, 2 * L, step=2)])
                    last.then_inc(o_ev, 1)

                def reciprocals(i, p, q):
                    dve.wait_ge(exp_s, (i * 2 + p) * 2 + q + 1)
                    V.reciprocal(sums[:, p, 1, 4 * q:4 * q + 4], sums[:, p, 0, 4 * q:4 * q + 4]).then_inc(rec_s, 1)

                if i is None:
                    maxima(0, 0, own)
                    z_low_1(2)
                    z_low_1(3)
                    reciprocals(0, 0, 0)
                    maxima(0, 1, own, (0,))
                    reciprocals(0, 0, 1)
                    maxima(0, 1, own, (1,))
                    return
                if ahead:
                    keys(i + 1, 0)
                reciprocals(i, 1, 0)
                for q in range(2):
                    dve.wait_ge(es_tr, i * 4 + q + 1)
                    V.tensor_copy(esT[0][:, 4 * q * L:4 * (q + 1) * L], ps[6 + q][0:L, 0:4 * L]).then_inc(es_evD, 1)
                reciprocals(i, 1, 1)
                if ahead:
                    keys(i + 1, 1)
                between(0)
                dve.wait_ge(es_tr, i * 4 + 4)
                V.tensor_copy(esT[1][:, 4 * L:], ps[7][0:L, 0:4 * L]).then_inc(es_evD, 1)
                output(0)
                between(1)
                output(1)
                if ahead:
                    maxima(i + 1, 0)
                between(2)
                for p in range(2):
                    b = i * 2 + p
                    dve.wait_ge(pr_mm, b + 1)
                    hb_ = h[:, bass.ds(b, 1), :].rearrange("p b d -> p (b d)")
                    own2(V.tensor_tensor(hb_, ps[6 + p][0:L, 0:D], hb_, ALU.add))
                    V.tensor_tensor(hb_, hb_, B("bout")[0:L, :], ALU.add).then_inc(h_l2, 1)
                if ahead:
                    reciprocals(i + 1, 0, 0)
                    maxima(i + 1, 1, halves=(0,))
                    reciprocals(i + 1, 0, 1)
                    maxima(i + 1, 1, halves=(1,))
                assert done[0] == (6 if ahead else 2)

            z_low_1(0)
            z_low_1(1)
            keys(0, 0)
            keys(0, 1)
            attention(None, True)
            attention(0, True)
            with dve.Fori(1, NB // 2 - 1) as i:
                attention(i, True)
            count[0] += 6 * (NB // 2 - 1)

            def next_norm(place):
                if place == 0:
                    dve.wait_ge(h_l2, NB - BG)
                    layer_stats(5, lambda b: h[:, b, :], None, (0,))
                elif place == 1:
                    layer_stats(5, lambda b: h[:, b, :], None, (1,))
                elif place == 2:
                    layer_stats(5, lambda b: h[:, b, :], None, (2,))

            attention(NB // 2 - 1, False, next_norm)
            dve.wait_ge(h_l2, NB)
            layer_stats(5, lambda b: h[:, b, :], None, (3,))
            own(V.tensor_copy(trib[:], C("tri", L)[:, 0:L]))
            own(V.tensor_copy(onesb[:], C("ones", L)))
            over_b = lambda c: c[:, None, :].to_broadcast([L, NB, NE])
            dve.wait_ge(lg1_mm, G)
            own(V.tensor_tensor(sm[:, 0], lg, over_b(B("br")[0:L, :]), ALU.add))
            own(V.tensor_reduce(red[:, 0], sm[:, 0], AX, ALU.max))
            own(V.tensor_tensor(sm[:, 1], sm[:, 0], wide(red[:, 0]), ALU.is_equal))
            own(V.scalar_tensor_tensor(sm[:, 2], sm[:, 1], -float(NE), over_b(C("e8", L)), ALU.mult, ALU.add))
            own(V.tensor_reduce(red[:, 1], sm[:, 2], AX, ALU.min))
            own(V.tensor_tensor(sm[:, 3], over_b(C("e8m", L)), wide(red[:, 1]), ALU.is_equal))
            V.tensor_copy(ohb[:], sm[:, 3]).then_inc(ohb_s, 1)
            dve.wait_ge(rank_mm, 1)
            own(V.tensor_copy(cnt[:, 0, :], ps[6][:, 0:NE]))
            own(V.tensor_tensor(cmp1[:], cnt[:, 0, :, None].to_broadcast([128, NE, NB]),
                                C("thr")[:, None, :].to_broadcast([128, NE, NB]), ALU.is_gt))
            own(V.tensor_reduce(cnt[:, 1, :], cmp1[:], AX, ALU.add))
            own(V.tensor_tensor_scan(cnt[:, 2, :], C("ones")[:, 0:NE], cnt[:, 1, :], 0.0, ALU.mult, ALU.add))
            own(V.tensor_tensor(cnt[:, 3, :], cnt[:, 2, :], cnt[:, 1, :], ALU.subtract))
            own(V.tensor_scalar(cnt[:, 3, :], cnt[:, 3, :], 128.0, None, ALU.mult))
            own(V.tensor_tensor(sm[:, 0], ps[5][0:L, 0:NB * NE].rearrange("p (b e) -> p b e", b=NB),
                                over_b(cnt[0:L, 3, :]), ALU.add))
            own(V.tensor_tensor(sm[:, 1], sm[:, 0], sm[:, 3], ALU.mult))
            own(V.tensor_reduce(red[:, 2], sm[:, 1], AX, ALU.add))
            own(V.tensor_tensor(reach, red[:, 2, :, None].to_broadcast([L, NB, NT + 1]),
                                C("first", L)[:, None, :].to_broadcast([L, NB, NT + 1]), ALU.is_ge))
            own(V.tensor_reduce(red[:, 3], reach, AX, ALU.add))
            own(V.scalar_tensor_tensor(red[:, 1], red[:, 3], -128.0, red[:, 2], ALU.mult, ALU.add))
            own(V.tensor_tensor(in_tile, reach[:, :, 0:NT], reach[:, :, 1:], ALU.subtract))
            V.tensor_scalar(tile_of[:, :, 0:NT], in_tile, C("token", L), None, ALU.mult)
            V.tensor_tensor(tile_of[:, :, NT:], in_tile, C("batch", L)[:, :, None].to_broadcast([L, NB, NT]), ALU.mult)
            for g in range(G):
                V.tensor_tensor(grp(slot_of, g), grp(red[:, 1], g)[:, :, None].to_broadcast([L, BG, 128]),
                                C("r128", L)[:, None, :].to_broadcast([L, BG, 128]), ALU.is_equal).then_inc(slot_s, 1)
            dve.wait_ge(held_mm, 1)
            own(V.tensor_copy(tl[:, 1, :], ps[6][:, 0:NT]))
            own(V.scalar_tensor_tensor(held[:, 0, :], ps[6][:, NT:2 * NT], float(L), tl[:, 1, :], ALU.mult, ALU.add))
            own(V.tensor_scalar(held[:, 1, :], held[:, 0, :], -1.0, None, ALU.add))
            V.tensor_scalar(take[:], held[:, 1, :], 0.0, None, ALU.max).then_inc(take_s, 1)
            own(V.tensor_scalar(held[:, 2, :], held[:, 0, :], 0.0, None, ALU.is_equal))
            own(V.scalar_tensor_tensor(held[:, 3, :], held[:, 2, :], C("none"), held[:, 1, :], ALU.mult, ALU.add))
            V.tensor_copy(give[:], held[:, 3, :]).then_inc(give_s, 1)
            own(V.tensor_tensor(cmp2[:], cnt[:, 2, None, :].to_broadcast([128, NT, NE]),
                                C("tile")[:, :, None].to_broadcast([128, NT, NE]), ALU.is_le))
            own(V.tensor_reduce(tl[:, 0, :], cmp2[:], AX, ALU.add))
            own(V.memset(expert[:, NT:], 0))
            V.tensor_scalar(expert[:, 0:NT], tl[:, 0, :], float(NE - 1), None, ALU.min).then_inc(exp_i, 1)
            dve.wait_ge(exp_i, 1)
            dve.wait_ge(fb_in, 16)

            def up(t, q):
                e = dve.value_load(expert[0:1, bass.ds(t, 1)], min_val=0, max_val=NE - 1)
                dve.wait_ge(h_mm, t + 1)
                V.tensor_tensor(hb[q % 2], ps[2 + q % 2][:, :], fb[:, bass.ds(e * F1, F1)], ALU.add).then_inc(hb_s, 1)

            def out(t, q, first):
                e = dve.value_load(expert[0:1, bass.ds(t, 1)], min_val=0, max_val=NE - 1)
                dve.wait_ge(o_mm, t + 1)
                if not first:
                    dve.wait_ge(y_st[q], (t - q) * 4)
                dve.wait_ge(h_keep, t + 1)
                own3(V.tensor_tensor(ot[q], ps[6 + q % 2][:, 0:D], fb[:, bass.ds(NE * F1 + e * D, D)], ALU.add), t)
                V.tensor_tensor(ot[q], ot[q], h_kept[q], ALU.add).then_inc(o_s, 1)

            def own3(ins, t):
                ins.then_inc(dve_n, 1)
                dve.wait_ge(dve_n, t + 1 + count[0])

            def step(t, q, ahead=True):
                if ahead:
                    up(t + 2, (q + 2) % 4)
                out(t, q, isinstance(t, int) and t < 4)

            up(0, 0)
            up(1, 1)
            for t in range(4):
                step(t, t)
            with dve.Fori(4, NT_LOOP, BODY) as t:
                for q in range(BODY):
                    step(t + q, q % 4)
            for t in range(NT_LOOP, NT):
                step(t, t % 4, ahead=t < NT - 2)


def kernel(**inputs):
    import numpy as _np
    import concourse.bacc as _bacc
    from concourse import mybir as _mybir
    from concourse.bass_utils import run_bass_kernel_spmd as _run

    a = {k: _np.asarray(v) for k, v in inputs.items()}

    def column(v):
        return v.reshape(-1, 1)

    def rows(v):
        return _np.broadcast_to(v.reshape(1, -1), (128, v.size))

    p0 = "L0_attn_"
    part_a = {
        "wqkv": _np.concatenate([a[p0 + "w" + n].T for n in "qkv"], axis=1),
        "wo": a[p0 + "wo"].T, "bq": column(a[p0 + "bq"]),
        "qcw": _np.tile(a[p0 + "qcw"], (H0, 1)), "qcb": _np.tile(column(a[p0 + "qcb"]), (H0, 1)),
        "w1": a[p0 + "w1"].T, "w2": a[p0 + "w2"].T.reshape(2, D, D).transpose(1, 0, 2).reshape(D, 2 * D),
        "b1": a[p0 + "b1"].reshape(2, D).T, "b2": column(a[p0 + "b2"]),
        "ln1_g": column(a[p0 + "ln1_g"]), "ln1_b": column(a[p0 + "ln1_b"]),
        "temp": _np.broadcast_to(a["L1_attn_temperature"].reshape(1, 1), (128, 1)),
        "bo": rows(a[p0 + "bo"]), "ln2_g": rows(a[p0 + "ln2_g"]), "ln2_b": rows(a[p0 + "ln2_b"]),
    }
    taps = _np.stack([_np.tile(a[p0 + n + "cw"], (H0, 1)).T for n in "qkv"], axis=1)
    filters = _np.concatenate([taps.reshape(-1)] + [a[p0 + n] for n in ("bk", "bv")]
                              + [_np.tile(a[p0 + n], H0) for n in ("kcb", "vcb")])
    wqkv = a["L1_attn_w_qkv"]
    part_b = {
        "wg": a["L0_ffn_Wg"], "eb1": a["L0_ffn_b1"].reshape(2 * NE, D).T, "eb2": a["L0_ffn_b2"].T,
        "ew1": a["L0_ffn_W1"].transpose(1, 0, 2).reshape(D, NE * F0),
        "ew2": a["L0_ffn_W2"].reshape(NE * 2, D, D).transpose(1, 0, 2).reshape(D, NE * 2 * D),
        "wout": a["L1_attn_w_out"].reshape(4, D, D).transpose(1, 0, 2).reshape(D, 4 * D),
        "bout": rows(a["L1_attn_b_out"]), "wr": a["L1_ffn_Wr"], "br": rows(a["L1_ffn_br"]),
    }
    arrays = {
        "wt": _np.concatenate([a["L0_tok_W"].T, column(a["L0_tok_b"]), a["x"][:, -1, :].T], axis=1),
        "xT": a["x"].transpose(2, 0, 1),
        "wa": _np.concatenate([part_a[n] for n in WA], axis=1),
        "wc": rows(filters),
        "wb": _np.concatenate([part_b[n] for n in WB], axis=1),
        "fw1": a["L1_ffn_W1"].transpose(1, 0, 2).reshape(D, NE * F1),
        "fw2": a["L1_ffn_W2"].reshape(NE * 4, D, D).transpose(1, 0, 2).reshape(D, NE * 4 * D),
        "fb": rows(_np.concatenate([a["L1_ffn_b1"].reshape(-1), a["L1_ffn_b2"].reshape(-1)])),
        "wqkv": _np.concatenate([wqkv[:, 0:2 * J * DH].reshape(D, 2, J, DH).transpose(0, 2, 1, 3).reshape(D, 2 * J * DH),
                                 wqkv[:, 2 * J * DH:]], axis=1),
        "consts": constants(),
    }
    arrays = {k: _np.ascontiguousarray(v) for k, v in arrays.items()}
    nc = _bacc.Bacc("TRN2", target_bir_lowering=False, num_devices=1)
    args = [nc.dram_tensor(k, v.shape, _mybir.dt.from_np(v.dtype), kind="ExternalInput").ap() for k, v in arrays.items()]
    args.append(nc.dram_tensor("out", (T, D), _mybir.dt.float32, kind="ExternalOutput").ap())
    build(nc, *args)
    r = _run(nc, [arrays], core_ids=[0])
    return r.results[0]["out"].reshape(NB, L, D)
```
